# Optimizing a Trainium2 kernel written in Bass

```python
import numpy as np
import jax
import jax.numpy as jnp

def _softmax(x, axis=-1):
    return jax.nn.softmax(x, axis=axis)

def _gelu(x):
    return jax.nn.gelu(x, approximate=True)

def _silu(x):
    return jax.nn.silu(x)

def _sigmoid(x):
    return jax.nn.sigmoid(x)

def _layernorm(x, axis=-1, eps=1e-05):
    m = jnp.mean(x, axis=axis, keepdims=True)
    v = jnp.var(x, axis=axis, keepdims=True)
    return (x - m) / jnp.sqrt(v + eps)

def _scatter_add(tgt, idx, src, axis=0):
    return tgt.at[idx].add(src)

def _segment_sum(src, seg, n):
    return jax.ops.segment_sum(src, seg, n)
kernel_name = 'mk_sandwich_d2_jaxref_r8_34ea77'

def setup_inputs(seed: int=0):
    np.random.seed(seed)
    _w = jnp.asarray

    def _L0_attn_setup():
        import jax, jax.numpy as jnp
        import numpy as np
        B, L, D, H = (2, 256, 256, 16)
        DH = D // H
        EPS = 1e-05

        def _delta_rule(q, k, v, beta):

            def step(S, inp):
                qt, kt, vt, bt = inp
                v_pred = jnp.einsum('bhk,bhkv->bhv', kt, S)
                delta = (vt - v_pred) * bt[..., None]
                S = S + kt[..., None] * delta[:, :, None, :]
                ot = jnp.einsum('bhk,bhkv->bhv', qt, S)
                return (S, ot)
            xs = (q.transpose(2, 0, 1, 3), k.transpose(2, 0, 1, 3), v.transpose(2, 0, 1, 3), beta.transpose(2, 0, 1))
            S0 = jnp.zeros(q.shape[:2] + (q.shape[-1], v.shape[-1]), q.dtype)
            _, o = jax.lax.scan(step, S0, xs)
            return o.transpose(1, 2, 0, 3)
        key = jax.random.key(seed)
        ks = jax.random.split(key, 6)
        s = 0.02
        return {'hidden_states': jax.random.normal(ks[0], (B, L, D), jnp.float32), 'Wq': jax.random.normal(ks[1], (D, D), jnp.float32) * s, 'Wk': jax.random.normal(ks[2], (D, D), jnp.float32) * s, 'Wv': jax.random.normal(ks[3], (D, D), jnp.float32) * s, 'Wb': jax.random.normal(ks[4], (D, H), jnp.float32) * s, 'o_norm_weight': jnp.ones((DH,), jnp.float32), 'Wo': jax.random.normal(ks[5], (D, D), jnp.float32) * s}
    _L0_attn_in = _L0_attn_setup()

    def _L0_ffn_setup():
        import jax, jax.numpy as jnp
        import numpy as np
        E, K, H, F_EXP = (64, 6, 256, 176)
        B, S = (1, 64)

        def _swiglu(x, g, v, o):
            return jax.nn.silu(x @ g) * (x @ v) @ o
        key = jax.random.key(seed)
        ks = jax.random.split(key, 8)
        s_h = 1.0 / np.sqrt(H)
        s_f = 1.0 / np.sqrt(F_EXP)
        return {'hidden_states': jax.random.normal(ks[0], (B, S, H), jnp.float32), 'w_router': jax.random.normal(ks[1], (E, H), jnp.float32) * s_h, 'wg': jax.random.normal(ks[2], (E, H, F_EXP), jnp.float32) * s_h, 'wv': jax.random.normal(ks[3], (E, H, F_EXP), jnp.float32) * s_h, 'wo': jax.random.normal(ks[4], (E, F_EXP, H), jnp.float32) * s_f, 'swg': jax.random.normal(ks[5], (H, F_EXP), jnp.float32) * s_h, 'swv': jax.random.normal(ks[6], (H, F_EXP), jnp.float32) * s_h, 'swo': jax.random.normal(ks[7], (F_EXP, H), jnp.float32) * s_f}
    _L0_ffn_in = _L0_ffn_setup()

    def _L1_attn_setup():
        import jax, jax.numpy as jnp
        import numpy as np
        B, T, D, H = (2, 256, 256, 16)
        DH = D // H
        ROPE_BASE = 10000.0

        def _rope(x, cos, sin):
            x0 = x[..., 0::2]
            x1 = x[..., 1::2]
            r0 = cos * x0 - sin * x1
            r1 = sin * x0 + cos * x1
            return jnp.stack((r0, r1), axis=-1).reshape(x.shape)
        key = jax.random.key(seed)
        ks = jax.random.split(key, 5)
        s = D ** (-0.5)
        return {'X': jax.random.normal(ks[0], (B, T, D), dtype=jnp.float32), 'Wq': jax.random.normal(ks[1], (D, D), dtype=jnp.float32) * s, 'Wk': jax.random.normal(ks[2], (D, D), dtype=jnp.float32) * s, 'Wv': jax.random.normal(ks[3], (D, D), dtype=jnp.float32) * s, 'Wo': jax.random.normal(ks[4], (D, D), dtype=jnp.float32) * s}
    _L1_attn_in = _L1_attn_setup()

    def _L1_ffn_setup():
        import jax, jax.numpy as jnp
        import numpy as np

        def _sparsify_2to4(h):
            B, S, I = h.shape
            g = h.reshape(B, S, I // 4, 4)
            a = jnp.abs(g)
            _, idx = jax.lax.top_k(a, 2)
            pos = jnp.arange(4)
            mask = (pos == idx[..., 0:1]) | (pos == idx[..., 1:2])
            return (g * mask.astype(g.dtype)).reshape(B, S, I)
        key = jax.random.key(seed)
        k1, k2, k3, k4 = jax.random.split(key, 4)
        B, S, H, I = (4, 256, 256, 1024)
        x = jax.random.normal(k1, (B, S, H), dtype=jnp.float32)
        w_gate = jax.random.normal(k2, (H, I), dtype=jnp.float32) / np.sqrt(H)
        w_up = jax.random.normal(k3, (H, I), dtype=jnp.float32) / np.sqrt(H)
        w_down = jax.random.normal(k4, (I, H), dtype=jnp.float32) / np.sqrt(I)
        return {'x': x, 'w_gate': w_gate, 'w_up': w_up, 'w_down': w_down}
    _L1_ffn_in = _L1_ffn_setup()
    _d = {'L0_attn_hidden_states': _L0_attn_in['hidden_states'], 'L0_attn_Wq': _L0_attn_in['Wq'], 'L0_attn_Wk': _L0_attn_in['Wk'], 'L0_attn_Wv': _L0_attn_in['Wv'], 'L0_attn_Wb': _L0_attn_in['Wb'], 'L0_attn_o_norm_weight': _L0_attn_in['o_norm_weight'], 'L0_attn_Wo': _L0_attn_in['Wo'], 'L0_ffn_w_router': _L0_ffn_in['w_router'], 'L0_ffn_wg': _L0_ffn_in['wg'], 'L0_ffn_wv': _L0_ffn_in['wv'], 'L0_ffn_wo': _L0_ffn_in['wo'], 'L0_ffn_swg': _L0_ffn_in['swg'], 'L0_ffn_swv': _L0_ffn_in['swv'], 'L0_ffn_swo': _L0_ffn_in['swo'], 'L1_attn_Wq': _L1_attn_in['Wq'], 'L1_attn_Wk': _L1_attn_in['Wk'], 'L1_attn_Wv': _L1_attn_in['Wv'], 'L1_attn_Wo': _L1_attn_in['Wo'], 'L1_ffn_w_gate': _L1_ffn_in['w_gate'], 'L1_ffn_w_up': _L1_ffn_in['w_up'], 'L1_ffn_w_down': _L1_ffn_in['w_down']}
    _x0 = _d['L0_attn_hidden_states']
    _d['L0_attn_hidden_states'] = jax.random.normal(jax.random.fold_in(jax.random.key(seed), 1), (4, 512, 256), dtype=_x0.dtype)
    del _x0
    return _d

def reference(L0_attn_hidden_states, L0_attn_Wq, L0_attn_Wk, L0_attn_Wv, L0_attn_Wb, L0_attn_o_norm_weight, L0_attn_Wo, L0_ffn_w_router, L0_ffn_wg, L0_ffn_wv, L0_ffn_wo, L0_ffn_swg, L0_ffn_swv, L0_ffn_swo, L1_attn_Wq, L1_attn_Wk, L1_attn_Wv, L1_attn_Wo, L1_ffn_w_gate, L1_ffn_w_up, L1_ffn_w_down):

    def _L0_attn_ref(hidden_states, Wq, Wk, Wv, Wb, o_norm_weight, Wo):
        import jax, jax.numpy as jnp
        import numpy as np
        B, L, D, H = (2, 256, 256, 16)
        DH = D // H
        EPS = 1e-05

        def _delta_rule(q, k, v, beta):

            def step(S, inp):
                qt, kt, vt, bt = inp
                v_pred = jnp.einsum('bhk,bhkv->bhv', kt, S)
                delta = (vt - v_pred) * bt[..., None]
                S = S + kt[..., None] * delta[:, :, None, :]
                ot = jnp.einsum('bhk,bhkv->bhv', qt, S)
                return (S, ot)
            xs = (q.transpose(2, 0, 1, 3), k.transpose(2, 0, 1, 3), v.transpose(2, 0, 1, 3), beta.transpose(2, 0, 1))
            S0 = jnp.zeros(q.shape[:2] + (q.shape[-1], v.shape[-1]), q.dtype)
            _, o = jax.lax.scan(step, S0, xs)
            return o.transpose(1, 2, 0, 3)
        b, l, d = hidden_states.shape
        h = Wb.shape[1]
        dh = d // h
        q = hidden_states @ Wq
        k = hidden_states @ Wk
        v = jax.nn.silu(hidden_states @ Wv)

        def heads(x):
            return x.reshape(b, l, h, dh).transpose(0, 2, 1, 3)
        q, k, v = (heads(q), heads(k), heads(v))

        def l2n(x):
            n = jnp.sqrt(jnp.sum(x * x, axis=-1, keepdims=True))
            return x / jnp.maximum(n, 1e-12)
        q, k = (l2n(q), l2n(k))
        q = q * dh ** (-0.5)
        beta = jax.nn.sigmoid(hidden_states @ Wb).transpose(0, 2, 1)
        o = _delta_rule(q, k, v, beta)
        o = o.transpose(0, 2, 1, 3)
        o = o * jax.lax.rsqrt(jnp.mean(o * o, axis=-1, keepdims=True) + EPS)
        o = o * o_norm_weight
        return o.reshape(b, l, d) @ Wo

    def _L0_ffn_ref(hidden_states, w_router, wg, wv, wo, swg, swv, swo):
        import jax, jax.numpy as jnp
        import numpy as np
        E, K, H, F_EXP = (64, 6, 256, 176)
        B, S = (1, 64)

        def _swiglu(x, g, v, o):
            return jax.nn.silu(x @ g) * (x @ v) @ o
        b, s, h = hidden_states.shape
        x = hidden_states.reshape(-1, h)
        T = x.shape[0]
        scores = jax.nn.softmax(x @ w_router.T, axis=-1)
        topw, topi = jax.lax.top_k(scores, K)
        combine = jnp.zeros((T, E), x.dtype).at[jnp.arange(T)[:, None], topi].add(topw)

        def body(acc, ws):
            g, v, o, cw = ws
            return (acc + cw[:, None] * _swiglu(x, g, v, o), None)
        routed, _ = jax.lax.scan(body, jnp.zeros_like(x), (wg, wv, wo, combine.T))
        shared = _swiglu(x, swg, swv, swo)
        return (routed + shared).reshape(b, s, h)

    def _L1_attn_ref(X, Wq, Wk, Wv, Wo):
        import jax, jax.numpy as jnp
        import numpy as np
        B, T, D, H = (2, 256, 256, 16)
        DH = D // H
        ROPE_BASE = 10000.0

        def _rope(x, cos, sin):
            x0 = x[..., 0::2]
            x1 = x[..., 1::2]
            r0 = cos * x0 - sin * x1
            r1 = sin * x0 + cos * x1
            return jnp.stack((r0, r1), axis=-1).reshape(x.shape)
        b, t, d = X.shape
        Q = X @ Wq.T
        K = X @ Wk.T
        V = X @ Wv.T
        Qh = Q.reshape(b, t, H, DH).transpose(0, 2, 1, 3)
        Kh = K.reshape(b, t, H, DH).transpose(0, 2, 1, 3)
        Vh = V.reshape(b, t, H, DH).transpose(0, 2, 1, 3)
        theta = ROPE_BASE ** (-2.0 * jnp.arange(DH // 2, dtype=jnp.float32) / DH)
        angles = jnp.arange(t, dtype=jnp.float32)[:, None] * theta[None, :]
        cos = jnp.cos(angles).astype(X.dtype)
        sin = jnp.sin(angles).astype(X.dtype)
        Qr = _rope(Qh, cos, sin)
        Kr = _rope(Kh, cos, sin)
        scores = jnp.einsum('bhqd,bhkd->bhqk', Qr, Kr) * DH ** (-0.5)
        causal = jnp.triu(jnp.ones((t, t), dtype=bool), 1)
        scores = jnp.where(causal, jnp.finfo(scores.dtype).min, scores)
        pattern = jax.nn.softmax(scores, axis=-1)
        heads = jnp.einsum('bhqk,bhkd->bqhd', pattern, Vh).reshape(b, t, d)
        return heads @ Wo.T

    def _L1_ffn_ref(x, w_gate, w_up, w_down):
        import jax, jax.numpy as jnp
        import numpy as np

        def _sparsify_2to4(h):
            B, S, I = h.shape
            g = h.reshape(B, S, I // 4, 4)
            a = jnp.abs(g)
            _, idx = jax.lax.top_k(a, 2)
            pos = jnp.arange(4)
            mask = (pos == idx[..., 0:1]) | (pos == idx[..., 1:2])
            return (g * mask.astype(g.dtype)).reshape(B, S, I)
        h = jax.nn.silu(jnp.einsum('bsh,hi->bsi', x, w_gate)) * jnp.einsum('bsh,hi->bsi', x, w_up)
        h_sparse = _sparsify_2to4(h)
        return jnp.einsum('bsi,ih->bsh', h_sparse, w_down)
    x = L0_attn_hidden_states
    x = x + _layernorm(_L0_attn_ref(_layernorm(x, axis=-1), L0_attn_Wq, L0_attn_Wk, L0_attn_Wv, L0_attn_Wb, L0_attn_o_norm_weight, L0_attn_Wo), axis=-1)
    x = x + _layernorm(_L0_ffn_ref(_layernorm(x, axis=-1), L0_ffn_w_router, L0_ffn_wg, L0_ffn_wv, L0_ffn_wo, L0_ffn_swg, L0_ffn_swv, L0_ffn_swo), axis=-1)
    x = x + _layernorm(_L1_attn_ref(_layernorm(x, axis=-1), L1_attn_Wq, L1_attn_Wk, L1_attn_Wv, L1_attn_Wo), axis=-1)
    x = x + _layernorm(_L1_ffn_ref(_layernorm(x, axis=-1), L1_ffn_w_gate, L1_ffn_w_up, L1_ffn_w_down), axis=-1)
    return x

_drawn_inputs = setup_inputs


def setup_inputs(seed=0):
    import zlib

    import numpy as np

    out = dict(_drawn_inputs(seed))
    spreads = {'L0_attn_o_norm_weight': (1.0, 0.2)}
    factors = {}
    for name, (base, spread) in spreads.items():
        noise = np.random.default_rng([zlib.crc32(name.encode()), seed]).standard_normal(out[name].shape)
        drawn = base * np.exp(spread * noise) if base else spread * noise
        out[name] = jnp.asarray(drawn.astype(out[name].dtype))
    for name, factor in factors.items():
        out[name] = (out[name] * factor).astype(out[name].dtype)
    return out
```

```python
from contextlib import ExitStack

import concourse.bass as bass
import numpy as np
from concourse import mybir

F32 = mybir.dt.float32
BF16 = mybir.dt.bfloat16
I32 = mybir.dt.int32
U32 = mybir.dt.uint32
ALU = mybir.AluOpType
ACT = mybir.ActivationFunctionType
AX = mybir.AxisListType
ds = bass.ds

B, L, D = 4, 512, 256
T = B * L
P = 128
NT = T // P
TB = L // P
KD = D // P
H, DH = 16, 16
HG = H * DH // P
HP = P // DH
G = B * HG
C = 16
NC_ = L // C
CT = P // C
EPS = 1e-5
NE, TOPK, FE = 64, 6, 176
FH = FE // 2
XT = 160
ST = NT
MT = XT + ST
FF = 1024
Q = 32
KVW = 2 * DH + 2

_C = {}
_off = 0
for _name, _w in (("ident", P), ("pair", 2), ("eye16", DH), ("mask_a", C), ("mask_m", C), ("mean_blk", P),
                  ("even", 1), ("odd", 1), ("causal", P), ("tri", P), ("ones", P), ("iota_e", NE), ("iota_p", 2),
                  ("k128", 16), ("cos", TB * DH // 2), ("sin", TB * DH // 2)):
    _C[_name] = (_off, _off + _w)
    _off += _w
CW = _off


def constants():
    c = np.zeros((P, CW), np.float32)
    p = np.arange(P)

    def put(name, v):
        c[:, _C[name][0]:_C[name][1]] = v

    put("ident", np.eye(P))
    put("pair", p[:, None] // DH % 2 == np.arange(2)[None])
    put("eye16", p[:, None] % DH == np.arange(DH)[None])
    put("mask_a", -1.0 * (np.arange(C)[None] < p[:, None] % C))
    put("mask_m", np.arange(C)[None] >= p[:, None] % C)
    put("mean_blk", (p[:, None] // DH == p[None] // DH) / DH)
    put("even", ((p[:, None] // DH) % 2 == 0) * DH ** -0.5)
    put("odd", ((p[:, None] // DH) % 2 == 1) * DH ** -0.5)
    put("causal", np.where(p[None] > p[:, None], -1e30, 0.0))
    put("tri", p[:, None] < p[None])
    put("ones", 1.0)
    put("iota_e", np.arange(NE)[None])
    put("iota_p", p[:, None] + P * np.arange(2)[None])
    put("k128", P * np.arange(16)[None])
    theta = np.float32(10000.0) ** (-2.0 * np.arange(DH // 2, dtype=np.float32) / DH)
    ang = (p[:, None, None] + P * np.arange(TB)[None, :, None]).astype(np.float32) * theta.astype(np.float32)
    put("cos", np.cos(ang).reshape(P, -1))
    put("sin", np.sin(ang).reshape(P, -1))
    return c


class State:

    def __init__(self, nc, ctx):
        self.nc = nc
        self.n = 0
        self.x = ctx.enter_context(nc.sbuf_tensor("x_res", [P, NT, D], F32))
        self.cst = ctx.enter_context(nc.sbuf_tensor("cst", [P, CW], F32))
        self.cb = ctx.enter_context(nc.sbuf_tensor("cst_bf16", [P, 4, P], BF16))
        self.mv = ctx.enter_context(nc.sbuf_tensor("mean_var", [P, NT, 2], F32))
        self.rstd = ctx.enter_context(nc.sbuf_tensor("rstd", [P, NT], F32))

    def c(self, name):
        return self.cst[:, _C[name][0]:_C[name][1]]


def opener(nc, ctx, phase):
    sems = []

    def give_back():
        nc.clear_and_free_semaphores(sems)
        nc.all_engine_barrier()

    ctx.callback(give_back)

    def sb(name, shape, dt=F32):
        return ctx.enter_context(nc.sbuf_tensor(f"{phase}_{name}", shape, dt))

    def ps(name, shape, dt=F32):
        return ctx.enter_context(nc.psum_tensor(f"{phase}_{name}", shape, dt))

    def sem(name):
        sems.append(nc.alloc_semaphore(f"{phase}_{name}"))
        return sems[-1]

    return sb, ps, sem


def phase_load(nc, st, x_in, cst_in):
    with ExitStack() as ctx:
        sb, ps, sem = opener(nc, ctx, "ld")
        x_in_sem, cst_sem, cast, stat, agg = sem("x"), sem("c"), sem("cast"), sem("stat"), sem("agg")
        stats = sb("stats", [P, NT, 6])
        block = ctx.enter_context(nc.Block())

        @block.sync
        def _(sp):
            for b in range(B):
                sp.dma_start(st.x[:, b * TB:(b + 1) * TB, :],
                             x_in[b].rearrange("(t p) d -> p t d", p=P)).then_inc(x_in_sem, 16)
            sp.wait_ge(x_in_sem, 16 * B)

        @block.scalar
        def _(act):
            act.dma_start(st.cst[:, :], cst_in).then_inc(cst_sem, 16)
            act.wait_ge(cst_sem, 16)
            for k, name in enumerate(("ident", "causal", "tri", "ones")):
                act.activation(st.cb[:, k, :], st.c(name), ACT.Copy).then_inc(cast, 1)

        @block.vector
        def _(dve):
            dve.wait_ge(x_in_sem, 16 * B)
            for t in range(NT):
                dve.bn_stats(stats[:, t, :], st.x[:, t, :]).then_inc(stat, 1)
            for t in range(NT):
                dve.wait_ge(stat, t + 1)
                dve.bn_aggr(st.mv[:, t, :], stats[:, t, :]).then_inc(agg, 1)


def finish_stats(nc, st, act, dve, eps_sem, root_sem, rstd_sem):
    if dve is not None:
        dve.tensor_scalar(st.rstd[:, :], st.mv[:, :, 1], EPS, None, ALU.add).then_inc(eps_sem, 1)
        dve.wait_ge(root_sem, 1)
        dve.reciprocal(st.rstd[:, :], st.rstd[:, :]).then_inc(rstd_sem, 1)
        dve.wait_ge(rstd_sem, 1)
    if act is not None:
        act.wait_ge(eps_sem, 1)
        act.activation(st.rstd[:, :], st.rstd[:, :], ACT.Sqrt).then_inc(root_sem, 1)


def phase_update(nc, st, y, tag):
    with ExitStack() as ctx:
        sb, ps, sem = opener(nc, ctx, tag)
        eps, root, rstd = sem("eps"), sem("root"), sem("rstd")
        yn, xs, stat, agg = sem("yn"), sem("x"), sem("stat"), sem("agg")
        stats = sb("stats", [P, NT, 6])
        mean = sb("mean", [P, NT, 1])
        block = ctx.enter_context(nc.Block())

        @block.scalar
        def _(act):
            finish_stats(nc, st, act, None, eps, root, rstd)

        @block.gpsimd
        def _(pool):
            pool.wait_ge(rstd, 2)
            for t in range(NT):
                pool.tensor_scalar(y[:, t, :], y[:, t, :], mean[:, t, :], st.rstd[:, t:t + 1],
                                   ALU.subtract, ALU.mult).then_inc(yn, 1)

        @block.vector
        def _(dve):
            finish_stats(nc, st, None, dve, eps, root, rstd)
            dve.tensor_copy(mean[:, :, 0], st.mv[:, :, 0]).then_inc(rstd, 1)
            dve.wait_ge(rstd, 2)
            for t in range(NT):
                dve.wait_ge(yn, t + 1)
                dve.tensor_tensor(st.x[:, t, :], st.x[:, t, :], y[:, t, :], ALU.add).then_inc(xs, 1)
                dve.wait_ge(xs, t + 1)
                dve.bn_stats(stats[:, t, :], st.x[:, t, :]).then_inc(stat, 1)
                dve.wait_ge(stat, t + 1)
                dve.bn_aggr(st.mv[:, t, :], stats[:, t, :]).then_inc(agg, 1)
            dve.wait_ge(agg, NT)


def phase_delta_project(nc, st, w_in, qr, kvb, norms, wall, zeros):
    W = 3 * D + H
    VB = D + H
    with ExitStack() as ctx:
        sb, ps, sem = opener(nc, ctx, "dp")
        w_ld, eps, root, rstd = sem("w_ld"), sem("eps"), sem("root"), sem("rstd")
        xn_ok, xt_ps, xt_ok, proj = sem("xn"), sem("xt_ps"), sem("xt"), sem("proj")
        sq_ok, tanh_ok, q_out, k_out, v_out, b_out, ss_ok, pad_ok = (
            sem(n) for n in ("sq", "tanh", "q_out", "k_out", "v_out", "b_out", "ss", "pad"))
        xn = sb("xn", [P, 2, D])
        xt = sb("xt", [P, 2, KD, P])
        sq = sb("sq", [P, 2, 2 * D])
        th = sb("th", [P, 2, H])
        p_t = [ps(f"p_t{i}", [P, 4, P]) for i in range(2)]
        p_qk = [ps(f"p_qk{i}", [P, 2 * D]) for i in range(2)]
        p_vb = [ps(f"p_vb{i}", [P, 512]) for i in range(2)]
        block = ctx.enter_context(nc.Block())

        @block.sync
        def _(sp):
            sp.dma_start(wall[:, :, :], w_in).then_inc(w_ld, 16)
            sp.wait_ge(w_ld, 16)

        @block.vector
        def _(dve):
            dve.memset(kvb[:, :, :, KVW - 1:KVW], 0.0).then_inc(pad_ok, 1)
            dve.memset(zeros[:, :], 0.0).then_inc(pad_ok, 1)
            finish_stats(nc, st, None, dve, eps, root, rstd)
            with dve.Fori(0, TB) as tb:
                for b in range(B):
                    n, u, t = tb * B + b, b % 2, tb + b * TB
                    dve.wait_ge(xt_ps, n + 1)
                    dve.tensor_scalar(xn[:, u, :], st.x[:, ds(t, 1), :], st.mv[:, ds(t, 1), 0], st.rstd[:, ds(t, 1)],
                                      ALU.subtract, ALU.mult).then_inc(xn_ok, 1)
                for b in range(B):
                    n, u, t = tb * B + b, b % 2, tb + b * TB
                    dve.wait_ge(sq_ok, n + 1)
                    dve.tensor_reduce(norms[:, ds(t, 1), :], sq[:, u, :].rearrange("p (h d) -> p h d", d=DH),
                                      AX.X, ALU.add).then_inc(ss_ok, 1)
                    dve.wait_ge(tanh_ok, n + 3)
                    dve.tensor_scalar(kvb[:, ds(t, 1), :, 2 * DH], th[:, u, :], 0.5, 0.5,
                                      ALU.mult, ALU.add).then_inc(b_out, 1)

        @block.tensor
        def _(pe):
            pe.sem_inc(xt_ps, 2)
            pe.wait_ge(w_ld, 16)

            def transposes(tb, b):
                n, u = tb * B + b, b % 2
                pe.wait_ge(xn_ok, n + 1)
                pe.wait_ge(xt_ok, n + 1)
                for k in range(KD):
                    last = pe.transpose(p_t[u][:, k, :], xn[:, u, k * P:(k + 1) * P], st.c("ident"))
                last.then_inc(xt_ps, 1)

            def project(tb, b):
                n, u = tb * B + b, b % 2
                pe.wait_ge(xt_ok, n + 3)
                pe.wait_ge(k_out, n + 1)
                pe.wait_ge(tanh_ok, n + 1)
                for k in range(KD):
                    pe.matmul(p_qk[u][:, :], xt[:, u, k, :], wall[:, k, 0:2 * D], start=k == 0, stop=k == KD - 1)
                for k in range(KD):
                    last = pe.matmul(p_vb[u][:, 0:VB], xt[:, u, k, :], wall[:, k, 2 * D:W], start=k == 0, stop=k == KD - 1)
                last.then_inc(proj, 1)

            with pe.Fori(0, TB) as tb:
                transposes(tb, 0)
                for b in range(B):
                    if b + 1 < B:
                        transposes(tb, b + 1)
                    project(tb, b)

        @block.scalar
        def _(act):
            finish_stats(nc, st, act, None, eps, root, rstd)
            for s in (xt_ok, k_out):
                act.sem_inc(s, 2)
            act.sem_inc(ss_ok, 2)
            act.sem_inc(b_out, 2)
            act.sem_inc(tanh_ok, 2)
            act.sem_inc(proj, 2)

            def take_xt(tb, b):
                n, u = tb * B + b, b % 2
                act.wait_ge(xt_ps, n + 3)
                act.wait_ge(proj, n + 1)
                act.activation(xt[:, u], p_t[u][:, 0:KD, :], ACT.Copy).then_inc(xt_ok, 1)

            with act.Fori(0, TB) as tb:
                take_xt(tb, 0)
                for b in range(B):
                    n, u, t = tb * B + b, b % 2, tb + b * TB
                    if b + 1 < B:
                        take_xt(tb, b + 1)
                    act.wait_ge(proj, n + 3)
                    act.activation(kvb[:, ds(t, 1), :, DH:2 * DH],
                                   p_vb[u][:, 0:D].rearrange("p (h d) -> p h d", d=DH), ACT.Silu).then_inc(v_out, 1)
                    act.wait_ge(b_out, n + 1)
                    act.activation(th[:, u, :], p_vb[u][:, D:VB], ACT.Tanh, scale=0.5).then_inc(tanh_ok, 1)
                    act.wait_ge(ss_ok, n + 1)
                    act.activation(sq[:, u, :], p_qk[u][:, :], ACT.Square).then_inc(sq_ok, 1)
                    act.activation(qr[:, ds(t, 1), :], p_qk[u][:, 0:D], ACT.Copy).then_inc(q_out, 1)
                    act.activation(kvb[:, ds(t, 1), :, 0:DH],
                                   p_qk[u][:, D:2 * D].rearrange("p (h d) -> p h d", d=DH), ACT.Copy).then_inc(k_out, 1)


def phase_delta_layout(nc, st, qr, kvb, norms, kqt, kvb_dram):
    with ExitStack() as ctx:
        sb, ps, sem = opener(nc, ctx, "dl")
        lim, root, rec, scal = sem("lim"), sem("root"), sem("rec"), sem("scal")
        n_ok, t_ps, k_back, st_d = (sem(n) for n in ("n", "t_ps", "k_back", "st"))
        taken = [sem("taken_act"), sem("taken_dve")]
        kq = sb("kq", [P, 2, 2, D])
        p_t = [[ps(f"p_t{i}{hg}", [P, 4, P]) for hg in range(HG)] for i in range(2)]
        flat = norms[:, :, :].rearrange("p t h -> p (t h)")
        block = ctx.enter_context(nc.Block())

        def take(eng, tb, b, hg):
            n, u = tb * B + b, b % 2
            eng.wait_ge(t_ps, n + 3)
            dst = kqt[:, ds(tb * CT, CT), b * HG + hg, :, :].rearrange("p c s i -> p s c i")
            src = p_t[u][hg][:, 0:2, :].rearrange("p s (c i) -> p s c i", i=C)
            for s in range(2):
                if hg == 0:
                    i = eng.activation(dst[:, s], src[:, s], ACT.Copy)
                else:
                    i = eng.tensor_copy(dst[:, s], src[:, s])
                i.then_inc(taken[hg], 1)

        @block.vector
        def _(dve):
            dve.tensor_scalar(flat, flat, 1e-24, None, ALU.max).then_inc(lim, 1)
            dve.wait_ge(root, 1)
            dve.reciprocal(flat, flat).then_inc(rec, 1)
            dve.wait_ge(rec, 1)
            dve.tensor_scalar(norms[:, :, 0:H], norms[:, :, 0:H], DH ** -0.5, None, ALU.mult).then_inc(scal, 1)
            dve.wait_ge(scal, 1)
            with dve.Fori(0, TB) as tb:
                for b in range(B):
                    n, u, t = tb * B + b, b % 2, tb + b * TB
                    dve.wait_ge(t_ps, n + 1)
                    dve.wait_ge(k_back, n + 1)
                    dve.tensor_tensor(kq[:, u, 0, :].rearrange("p (h d) -> p h d", d=DH),
                                      kvb[:, ds(t, 1), :, 0:DH],
                                      norms[:, ds(t, 1), H:2 * H].rearrange("p o h -> p (o h)").unsqueeze(2)
                                      .to_broadcast([P, H, DH]), ALU.mult).then_inc(n_ok, 1)
                    dve.tensor_tensor(kq[:, u, 1, :].rearrange("p (h d) -> p h d", d=DH),
                                      qr[:, ds(t, 1), :].rearrange("p o (h d) -> p (o h) d", d=DH),
                                      norms[:, ds(t, 1), 0:H].rearrange("p o h -> p (o h)").unsqueeze(2)
                                      .to_broadcast([P, H, DH]), ALU.mult).then_inc(n_ok, 1)
                    if b % 2:
                        for m in (b - 1, b):
                            take(dve, tb, m, 1)

        @block.tensor
        def _(pe):
            pe.sem_inc(t_ps, 2)
            with pe.Fori(0, TB) as tb:
                for b in range(B):
                    n, u = tb * B + b, b % 2
                    pe.wait_ge(n_ok, 2 * n + 2)
                    for s in taken:
                        pe.wait_ge(s, 2 * n + 1)
                    for s in range(2):
                        for hg in range(HG):
                            last = pe.transpose(p_t[u][hg][:, s, :], kq[:, u, s, hg * P:(hg + 1) * P], st.c("ident"))
                    last.then_inc(t_ps, 1)

        @block.scalar
        def _(act):
            act.sem_inc(taken[0], 3)
            act.sem_inc(taken[1], 3)
            act.wait_ge(lim, 1)
            act.activation(flat, flat, ACT.Sqrt).then_inc(root, 1)
            with act.Fori(0, TB) as tb:
                for b in range(B):
                    take(act, tb, b, 0)

        @block.gpsimd
        def _(pool):
            pool.sem_inc(k_back, 2)
            with pool.Fori(0, TB) as tb:
                for b in range(B):
                    n, u, t = tb * B + b, b % 2, tb + b * TB
                    pool.wait_ge(n_ok, 2 * n + 1)
                    pool.tensor_copy(kvb[:, ds(t, 1), :, 0:DH],
                                     kq[:, u, 0, :].rearrange("p (h d) -> p h d", d=DH)).then_inc(k_back, 1)

        @block.sync
        def _(sp):
            for tb in range(TB):
                sp.wait_ge(k_back, tb * B + B + 2)
                sp.dma_start(kvb_dram.rearrange("(b t p) h w -> p b t (h w)", b=B, p=P)[:, :, tb, :],
                             kvb[:, :, :, :].rearrange("p (b t) h w -> p b t (h w)", b=B)[:, :, tb, :]
                             ).then_inc(st_d, 16)
            sp.wait_ge(st_d, 16 * TB)


def tiles():
    for s in range(G):
        for q in range(P // Q):
            yield (2 * q + s) % G, slice(q * Q, (q + 1) * Q)


def expand(st, eng, dst, src, done):
    shape = [P, src.shape[1], 2, C]
    eng.tensor_tensor(dst, src.unsqueeze(2).to_broadcast(shape),
                      st.c("pair").unsqueeze(1).unsqueeze(3).to_broadcast(shape), ALU.mult).then_inc(done, 1)


def phase_delta_scores(nc, st, kqt, kvb_dram, mkv, att):
    with ExitStack() as ctx:
        sb, ps, sem = opener(nc, ctx, "ds")
        begun, ld_d, kbd_ok, kq_ok, s_ps, a_out, m_out, scaled = (
            sem(n) for n in ("begun", "ld", "kbd", "kq", "s_ps", "a_out", "m_out", "scaled"))
        kq = sb("kq", [P, 2, G, 2, C])
        kbd = sb("kbd", [P, 2, G, 2, C])
        p_s = [ps(f"p_s{i}", [P, G, 256]) for i in range(2)]
        att_c = att[:, :, :].rearrange("p j (c g) -> p g j c", g=G)
        block = ctx.enter_context(nc.Block())

        @block.sync
        def _(sp):
            rows = kvb_dram.rearrange("(b c j) (g h) w -> h j c b g w", b=B, j=C, g=HG)
            for h in range(HP):
                for b in range(B):
                    for hg in range(HG):
                        sp.dma_start(mkv[h * C:(h + 1) * C, :, b * HG + hg, C:C + KVW],
                                     rows[h, :, :, b, hg, :]).then_inc(ld_d, 16)
            sp.wait_ge(ld_d, 16 * HP * G)

        @block.scalar
        def _(act):
            with act.Fori(0, NC_ // 2) as cc:
                for u in range(2):
                    act.wait_ge(s_ps, 2 * cc + u + 1)
                    act.activation(kq[:, u], kqt[:, ds(2 * cc + u, 1), :, :, :].rearrange("p o g s i -> p (o g) s i"),
                                   ACT.Copy).then_inc(kq_ok, 1)

        @block.vector
        def _(dve):
            def take(n, u):
                dve.wait_ge(s_ps, n + 3)
                dve.tensor_tensor(att_c[:, :, :, ds(n, 1)].rearrange("p g j o -> p g (j o)"), p_s[u][:, :, 0:C],
                                  st.c("mask_a").unsqueeze(1).to_broadcast([P, G, C]), ALU.mult).then_inc(a_out, 1)
                dve.tensor_tensor(mkv[:, ds(n, 1), :, 0:C].rearrange("p o g i -> p (o g) i"), p_s[u][:, :, C:2 * C],
                                  st.c("mask_m").unsqueeze(1).to_broadcast([P, G, C]), ALU.mult).then_inc(m_out, 1)

            with dve.Fori(0, NC_ // 2) as cc:
                for u in range(2):
                    dve.wait_ge(s_ps, 2 * cc + u + 1)
                    expand(st, dve, kbd[:, u], kqt[:, ds(2 * cc + u, 1), :, 0, :].rearrange("p o g d -> p (o g) d"),
                           kbd_ok)
                for u in range(2):
                    take(2 * cc + u, u)
            dve.wait_ge(a_out, NC_)
            dve.wait_ge(ld_d, 16 * HP * G)
            dve.tensor_tensor(att[:, :, :].rearrange("p j (c g) -> p j c g", g=G),
                              att[:, :, :].rearrange("p j (c g) -> p j c g", g=G),
                              mkv[:, :, :, C + 2 * DH].unsqueeze(1).to_broadcast([P, C, NC_, G]),
                              ALU.mult).then_inc(scaled, 1)

        @block.tensor
        def _(pe):
            pe.sem_inc(s_ps, 2)
            pe.sem_inc(m_out, 2)
            with pe.Fori(0, NC_ // 2) as cc:
                for u in range(2):
                    n = 2 * cc + u
                    pe.wait_ge(kbd_ok, n + 1)
                    pe.wait_ge(kq_ok, n + 1)
                    pe.wait_ge(m_out, n + 1)
                    pe.sem_inc(begun, 1)
                    for g, q in tiles():
                        last = pe.matmul(p_s[u][q, g, 0:2 * C], kbd[q, u, g, :, :], kq[q, u, g, :, :],
                                         start=True, stop=True)
                    last.then_inc(s_ps, 1)


def phase_delta_invert(nc, st, mkv, att, zeros, xs_dram, zero_sem, n_zero):
    JB = 4
    NB = C // JB
    HC = 2 * HP
    with ExitStack() as ctx:
        sb, ps, sem = opener(nc, ctx, "di")
        t_ps, out_a, out_v, one, back, b_out = (sem(n) for n in ("t_ps", "out_a", "out_v", "one", "back", "b_out"))
        products, rows, zero = sem("products"), sem("rows"), sem("zero")
        au = sb("au", [P, HC, C, C])
        tt = sb("tt", [P, C, HC, C])
        prod = sb("prod", [P, HC, C - 1, C - 1])
        bank = [ps(f"bank{i}", [P, JB, P]) for i in range(2 * NB)]
        block = ctx.enter_context(nc.Block())

        @block.sync
        def _(sp):
            slots = xs_dram[0:XT * P, :].rearrange("(p r) d -> p (r d)", p=P)
            w = zeros.shape[1]
            for i in range(n_zero):
                sp.dma_start(slots[:, i * w:(i + 1) * w], zeros[:, :]).then_inc(zero_sem, 16)

        @block.tensor
        def _(pe):
            for half in range(2):
                for jb in range(NB):
                    for j in range(JB):
                        last = pe.transpose(bank[half * NB + jb][:, j, :],
                                            att[:, jb * JB + j, half * P:(half + 1) * P], st.c("ident"))
                    last.then_inc(t_ps, 1)
            pe.wait_ge(rows, C - 1)
            pe.wait_ge(one, C)
            for half in range(2):
                pe.wait_ge(out_a, (half + 1) * NB // 2)
                pe.wait_ge(out_v, (half + 1) * NB // 2)
                for ib in range(NB):
                    for i in range(JB):
                        last = pe.transpose(bank[half * NB + ib][:, i, :],
                                            tt[:, ib * JB + i, half * HP:(half + 1) * HP, :], st.c("ident"))
                    last.then_inc(back, 1)

        def spread(eng, n, done):
            half, jb = n // NB, n % NB
            eng.wait_ge(t_ps, n + 1)
            dst = au[:, half * HP:(half + 1) * HP, :, jb * JB:(jb + 1) * JB].rearrange("p h i j -> p j (h i)")
            i = eng.activation(dst, bank[n][:, :, :], ACT.Copy) if done is out_a else eng.tensor_copy(
                dst, bank[n][:, :, :])
            i.then_inc(done, 1)

        @block.scalar
        def _(act):
            for n in range(0, 2 * NB, 2):
                spread(act, n, out_a)

        @block.gpsimd
        def _(pool):
            pool.memset(tt[:, :, :, :], 0.0).then_inc(zero, 1)
            pool.wait_ge(zero, 1)
            for i in range(C):
                pool.memset(tt[:, i, :, i], 1.0).then_inc(one, 1)

        @block.vector
        def _(dve):
            for n in range(1, 2 * NB, 2):
                spread(dve, n, out_v)
            dve.wait_ge(out_a, NB)
            dve.wait_ge(out_v, NB)
            dve.wait_ge(one, C)
            for i in range(1, C):
                terms = prod[:, :, 0:i, 0:i]
                if i > 1:
                    dve.wait_ge(rows, i - 1)
                dve.tensor_tensor(terms, au[:, :, i, 0:i].unsqueeze(2).to_broadcast([P, HC, i, i]),
                                  tt[:, 0:i, :, 0:i].rearrange("p m h j -> p h j m"), ALU.mult).then_inc(products, 1)
                dve.wait_ge(products, i)
                dve.tensor_reduce(tt[:, i, :, 0:i], terms, AX.X, ALU.add).then_inc(rows, 1)
            for n in range(2 * NB):
                half, ib = n // NB, n % NB
                dve.wait_ge(back, n + 1)
                beta = mkv[:, :, :, C + 2 * DH].rearrange("p c g -> p (c g)")[:, half * P:(half + 1) * P]
                dve.tensor_tensor(att[:, ib * JB:(ib + 1) * JB, half * P:(half + 1) * P], bank[n][:, :, :],
                                  beta.unsqueeze(1).to_broadcast([P, JB, P]), ALU.mult).then_inc(b_out, 1)


def phase_delta_wy(nc, st, kqt, mkv, att, xt):
    U = 4
    with ExitStack() as ctx:
        sb, ps, sem = opener(nc, ctx, "dw")
        begun, tb_ok, mk_ok, w_ps, w_out, wv_out, wk_ok, x_ps, q_out, i_out = (
            sem(n) for n in ("begun", "tb", "mk", "w_ps", "w_out", "wv_out", "wk", "x_ps", "q_out", "i_out"))
        mk = sb("mk", [P, 2, G, C + 2 * DH])
        tbd = sb("tbd", [P, 2, G, 2, C])
        wkd = sb("wkd", [P, 2, G, 2, C])
        wc = sb("wc", [P, 2, G, DH])
        p_w, p_x = (ps(n, [P, G, 256]) for n in ("p_w", "p_x"))
        att_c = att[:, :, :].rearrange("p j (c g) -> p g j c", g=G)

        block = ctx.enter_context(nc.Block())

        @block.gpsimd
        def _(pool):
            with pool.Fori(0, NC_ // U) as cc:
                for k in range(U):
                    n, u = U * cc + k, k % 2
                    pool.wait_ge(w_ps, n + 1)
                    expand(st, pool, tbd[:, u], att_c[:, :, :, ds(n, 1)].rearrange("p g j o -> p g (j o)"), tb_ok)

        @block.scalar
        def _(act):
            act.sem_inc(wk_ok, 2)
            act.sem_inc(wv_out, 1)

            def copy_mk(cc, k):
                n, u = U * cc + k, k % 2
                act.wait_ge(x_ps, n + 1)
                act.activation(mk[:, u], mkv[:, ds(n, 1), :, 0:C + 2 * DH].rearrange("p o g w -> p (o g) w"),
                               ACT.Copy).then_inc(mk_ok, 1)

            with act.Fori(0, NC_ // U) as cc:
                copy_mk(cc, 0)
                for k in range(U):
                    if k + 1 < U:
                        copy_mk(cc, k + 1)
                    n, u = U * cc + k, k % 2
                    act.wait_ge(w_ps, n + 3)
                    act.wait_ge(wk_ok, n + 1)
                    act.activation(wc[:, u], p_w[:, :, 0:DH], ACT.Copy).then_inc(w_out, 1)
                    act.activation(mkv[:, ds(n, 1), :, C + DH:C + 2 * DH].rearrange("p o g v -> p (o g) v"),
                                   p_w[:, :, DH:2 * DH], ACT.Copy).then_inc(wv_out, 1)

        @block.vector
        def _(dve):
            dve.sem_inc(x_ps, 2)

            def x_part(cc, k):
                n = U * cc + k
                dve.wait_ge(x_ps, n + 3)
                dst = xt[:, ds(n, 1), :, :, :].rearrange("p o g s i -> p (o g) s i")
                dve.tensor_tensor(dst[:, :, 0, :], kqt[:, ds(n, 1), :, 1, :].rearrange("p o g i -> p (o g) i"),
                                  p_x[:, :, 0:C], ALU.subtract).then_inc(q_out, 1)
                dve.tensor_tensor(dst[:, :, 1, :], st.c("eye16").unsqueeze(1).to_broadcast([P, G, DH]),
                                  p_x[:, :, C:2 * C], ALU.subtract).then_inc(i_out, 1)

            with dve.Fori(0, NC_ // U) as cc:
                for k in range(U):
                    n, u = U * cc + k, k % 2
                    dve.wait_ge(w_out, n + 1)
                    dve.wait_ge(x_ps, n + 1)
                    expand(st, dve, wkd[:, u], wc[:, u], wk_ok)
                    if k > 0:
                        x_part(cc, k - 1)
                x_part(cc, U - 1)

        @block.tensor
        def _(pe):
            pe.sem_inc(w_ps, 2)
            pe.sem_inc(i_out, 1)

            def w_part(cc, k):
                n, u = U * cc + k, k % 2
                pe.wait_ge(tb_ok, n + 1)
                pe.wait_ge(mk_ok, n + 1)
                pe.wait_ge(wv_out, n + 1)
                pe.sem_inc(begun, 1)
                for g, q in tiles():
                    last = pe.matmul(p_w[q, g, 0:2 * DH], tbd[q, u, g, :, :], mk[q, u, g, C:C + 2 * DH],
                                     start=True, stop=True)
                last.then_inc(w_ps, 1)

            def x_part(cc, k):
                n, u = U * cc + k, k % 2
                pe.wait_ge(wk_ok, n + 3)
                pe.wait_ge(i_out, n + 1)
                pe.sem_inc(begun, 1)
                for g, q in tiles():
                    last = pe.matmul(p_x[q, g, 0:C + DH], wkd[q, u, g, :, :], mk[q, u, g, 0:C + DH],
                                     start=True, stop=True)
                last.then_inc(x_ps, 1)

            with pe.Fori(0, NC_ // U) as cc:
                w_part(cc, 0)
                for k in range(U):
                    if k + 1 < U:
                        w_part(cc, k + 1)
                    x_part(cc, k)


def phase_delta_chain(nc, st, mkv, xt, ot):
    N = 2 * DH + C
    with ExitStack() as ctx:
        sb, ps, sem = opener(nc, ctx, "dc")
        km_ok, xx_ok, wv_ok, s_ok, r_ps, o_out = (sem(n) for n in ("km", "xx", "wv", "s", "r_ps", "o_out"))
        km_k, xx_p, begun = sem("km_k"), sem("xx_p"), sem("begun")
        km = sb("km", [P, 2, G, N])
        xx = sb("xx", [P, 2, G, N])
        wvd = sb("wvd", [P, 2, G, 2, DH])
        s = sb("s", [P, 2, G, 2 * DH])
        p_r = [ps(f"p_r{i}", [P, G, 256]) for i in range(2)]

        def pair(t):
            return t[:, :, 0:2 * DH].rearrange("p g (s i) -> p g s i", s=2)

        def part(t, n, lo):
            return t[:, ds(n, 1), :, lo:lo + C].rearrange("p o g i -> p (o g) i")

        def xt_part(n, k):
            return xt[:, ds(n, 1), :, k, :].rearrange("p o g i -> p (o g) i")

        block = ctx.enter_context(nc.Block())

        @block.gpsimd
        def _(pool):
            with pool.Fori(0, NC_ // 2) as cc:
                for u in range(2):
                    n = 2 * cc + u
                    pool.wait_ge(r_ps, n + 1)
                    expand(st, pool, pair(km[:, u]), part(mkv, n, C), km_k)
                    expand(st, pool, wvd[:, u], part(mkv, n, C + DH), wv_ok)

        def ahead(eng, prepare, finish):
            prepare(0, 0)
            with eng.Fori(0, NC_ // 2 - 1) as cc:
                for u in range(2):
                    prepare(2 * cc + u + 1, 1 - u)
                    finish(2 * cc + u, u)
            prepare(NC_ - 1, 1)
            finish(NC_ - 2, 0)
            finish(NC_ - 1, 1)

        @block.vector
        def _(dve):
            def prepare(n, u):
                dve.wait_ge(r_ps, n + 1)
                expand(st, dve, pair(xx[:, u]), xt_part(n, 1), xx_p)

            def turn(n, u):
                dve.wait_ge(r_ps, n + 3)
                dve.transpose(s[:, 1 - u], p_r[u][:, :, 0:2 * DH]).then_inc(s_ok, 1)

            dve.memset(s[:, 0], 0.0).then_inc(s_ok, 1)
            ahead(dve, prepare, turn)

        @block.scalar
        def _(act):
            def prepare(n, u):
                act.wait_ge(r_ps, n + 1)
                act.activation(km[:, u, :, 2 * DH:N], part(mkv, n, 0), ACT.Copy).then_inc(km_ok, 1)
                act.activation(xx[:, u, :, 2 * DH:N], xt_part(n, 0), ACT.Copy).then_inc(xx_ok, 1)

            def take(n, u):
                act.wait_ge(s_ok, n + 2)
                act.activation(ot[:, :, :, ds(n * C, C)].rearrange("p g b i -> p b g i"),
                               p_r[u][:, :, 2 * DH:N].rearrange("p (b g) i -> p b g i", g=HG),
                               ACT.Copy).then_inc(o_out, 1)

            ahead(act, prepare, take)

        @block.tensor
        def _(pe):
            pe.sem_inc(r_ps, 2)
            pe.sem_inc(o_out, 2)

            with pe.Fori(0, NC_ // 2) as cc:
                for u in range(2):
                    n = 2 * cc + u
                    for done in (km_k, wv_ok, km_ok):
                        pe.wait_ge(done, n + 1)
                    pe.wait_ge(o_out, n + 1)
                    pe.sem_inc(begun, 1)
                    for g, q in tiles():
                        pe.matmul(p_r[u][q, g, 0:N], wvd[q, u, g, :, :], km[q, u, g, :], start=g % 2 == 0, stop=False)
                    pe.wait_ge(xx_p, n + 1)
                    pe.wait_ge(xx_ok, n + 1)
                    pe.wait_ge(s_ok, n + 1)
                    pe.sem_inc(begun, 1)
                    for g, q in tiles():
                        last = pe.matmul(p_r[u][q, g, 0:N], s[q, u, g, :], xx[q, u, g, :], start=False, stop=g % 2 == 1)
                    last.then_inc(r_ps, 1)


def phase_delta_out(nc, st, ot, wo_in, onw_in, y):
    with ExitStack() as ctx:
        sb, ps, sem = opener(nc, ctx, "do")
        w_ld, sq_ok, ms_ps, eps_ok, root, rec, on_ok, y_ps, y_ok, stat, agg = (
            sem(n) for n in ("w_ld", "sq", "ms_ps", "eps", "root", "rec", "on", "y_ps", "y", "stat", "agg"))
        wo = sb("wo", [P, HG, D])
        onw = sb("onw", [P, 1])
        sq = sb("sq", [P, 2, L])
        r = sb("r", [P, 2, L])
        on = sb("on", [P, HG, L])
        stats = sb("stats", [P, NT, 6])
        p_ms = [ps(f"p_ms{i}", [P, L]) for i in range(2)]
        p_y = [ps(f"p_y{i}", [P, 512]) for i in range(2)]
        block = ctx.enter_context(nc.Block())

        @block.sync
        def _(sp):
            sp.dma_start(wo[:, :, :], wo_in).then_inc(w_ld, 16)
            sp.dma_start(onw[:, :], onw_in).then_inc(w_ld, 16)
            sp.wait_ge(w_ld, 32)

        @block.scalar
        def _(act):
            act.sem_inc(y_ok, 1)
            act.sem_inc(ms_ps, 2)
            with act.Fori(0, B) as b:
                for g in range(HG):
                    act.wait_ge(ms_ps, 2 * b + g + 1)
                    act.activation(sq[:, g, :], ot[:, g, ds(b, 1), :].rearrange("p o l -> p (o l)"),
                                   ACT.Square).then_inc(sq_ok, 1)
                for g in range(HG):
                    act.wait_ge(eps_ok, 2 * b + g + 1)
                    act.activation(r[:, g, :], r[:, g, :], ACT.Sqrt).then_inc(root, 1)
                for t in range(TB):
                    n = TB * b + t
                    act.wait_ge(y_ps, n + 2)
                    act.activation(y[:, ds(n, 1), :].rearrange("p o d -> p (o d)"), p_y[t % 2][:, 0:D],
                                   ACT.Copy).then_inc(y_ok, 1)

        @block.vector
        def _(dve):
            dve.sem_inc(on_ok, 1)
            dve.wait_ge(w_ld, 32)
            with dve.Fori(0, B) as b:
                for g in range(HG):
                    dve.wait_ge(ms_ps, 2 * b + g + 3)
                    dve.tensor_scalar(r[:, g, :], p_ms[g][:, :], EPS, None, ALU.add).then_inc(eps_ok, 1)
                for g in range(HG):
                    n = 2 * b + g
                    dve.wait_ge(root, n + 1)
                    dve.reciprocal(r[:, g, :], r[:, g, :]).then_inc(rec, 1)
                    dve.wait_ge(rec, n + 1)
                    dve.wait_ge(y_ps, TB * b + 1)
                    dve.scalar_tensor_tensor(on[:, g, :], ot[:, g, ds(b, 1), :].rearrange("p o l -> p (o l)"),
                                             onw[:, 0:1], r[:, g, :], ALU.mult, ALU.mult).then_inc(on_ok, 1)
                for t in range(TB):
                    n = TB * b + t
                    dve.wait_ge(y_ok, n + 2)
                    dve.bn_stats(stats[:, ds(n, 1), :].rearrange("p o s -> p (o s)"),
                                 y[:, ds(n, 1), :].rearrange("p o d -> p (o d)")).then_inc(stat, 1)
            dve.wait_ge(stat, NT)
            for n in range(NT):
                dve.bn_aggr(st.mv[:, n, :], stats[:, n, :]).then_inc(agg, 1)

        @block.tensor
        def _(pe):
            pe.sem_inc(y_ps, 1)
            with pe.Fori(0, B) as b:
                for g in range(HG):
                    n = 2 * b + g
                    pe.wait_ge(sq_ok, n + 1)
                    pe.wait_ge(on_ok, 2 * b + 1)
                    pe.matmul(p_ms[g][:, :], st.c("mean_blk"), sq[:, g, :], start=True, stop=True).then_inc(ms_ps, 1)
                pe.wait_ge(on_ok, 2 * b + 3)
                pe.wait_ge(w_ld, 32)
                for t in range(TB):
                    n = TB * b + t
                    if t >= 2:
                        pe.wait_ge(y_ok, n)
                    else:
                        pe.wait_ge(y_ok, TB * b + 1)
                    for g in range(HG):
                        last = pe.matmul(p_y[t % 2][:, 0:D], on[:, g, t * P:(t + 1) * P], wo[:, g, :],
                                         start=g == 0, stop=g == HG - 1)
                    last.then_inc(y_ps, 1)


class Routing:

    def __init__(self, nc, ctx):
        def sb(name, shape, dt=F32):
            return ctx.enter_context(nc.sbuf_tensor(f"rt_{name}", shape, dt))

        self.top = sb("top", [P, NT, 8])
        self.hot = sb("hot", [P, NT, TOPK, NE], BF16)
        self.sel = sb("sel", [P, NT, NE], BF16)
        self.cum = sb("cum", [P, NT + 1, NE], BF16)
        self.pos = sb("pos", [P, NT, 8], U32)
        self.erow = sb("erow", [1, MT], I32)


def phase_route(nc, st, rt, wr_in, xna):
    with ExitStack() as ctx:
        sb, ps, sem = opener(nc, ctx, "ro")
        w_ld, eps, root, rstd = sem("w_ld"), sem("eps"), sem("root"), sem("rstd")
        xn_ok, xs_ok, xt_ps, xt_ok, l_ps, mx_ok, e_ok, rec, sc_ok, begun, top_ok, kept, idx_ok, idf_ok, hot_ok, sel_ok, cum_ok = (
            sem(n) for n in ("xn", "xs", "xt_ps", "xt", "l_ps", "mx", "e", "rec", "sc", "begun", "top", "kept", "idx", "idf", "hot",
                             "sel", "cum"))
        wr = sb("wr", [P, KD, NE])
        xn = sb("xn", [P, 2, D])
        xt = sb("xt", [P, 2, KD, P])
        nm = sb("nm", [P, 2, 1])
        e = sb("e", [P, 2, NE])
        se = sb("se", [P, 2, 1])
        sc = sb("sc", [P, 2, NE])
        top = sb("top", [P, 2, 8])
        idx = sb("idx", [P, 2, 8], U32)
        idf = sb("idf", [P, 2, 8])
        p_t = [ps(f"p_t{i}", [P, 4, P]) for i in range(2)]
        p_l = [ps(f"p_l{i}", [P, 512]) for i in range(2)]
        block = ctx.enter_context(nc.Block())

        def tile(t, ap):
            return ap[:, ds(t, 1)]

        @block.sync
        def _(sp):
            sp.dma_start(wr[:, :, :], wr_in).then_inc(w_ld, 16)
            sp.wait_ge(w_ld, 16)

        @block.vector
        def _(dve):
            dve.sem_inc(mx_ok, 2)
            dve.sem_inc(sc_ok, 2)
            dve.sem_inc(xt_ps, 2)
            finish_stats(nc, st, None, dve, eps, root, rstd)
            dve.memset(rt.cum[:, 0, :], 0.0).then_inc(cum_ok, 1)
            with dve.Fori(0, NT // 4) as q:
                for k in range(4):
                    n, u = 4 * q + k, k % 2
                    dve.wait_ge(xt_ps, n + 1)
                    dve.wait_ge(xs_ok, n + 1)
                    dve.tensor_scalar(xn[:, u, :], tile(n, st.x), st.mv[:, ds(n, 1), 0], st.rstd[:, ds(n, 1)],
                                      ALU.subtract, ALU.mult).then_inc(xn_ok, 1)
                for k in range(4):
                    n, u = 4 * q + k, k % 2
                    dve.wait_ge(l_ps, n + 1)
                    dve.wait_ge(e_ok, n + 1)
                    dve.tensor_reduce(nm[:, u, :], p_l[u][:, 0:NE], AX.X, ALU.max, negate=True).then_inc(mx_ok, 1)
                    dve.wait_ge(e_ok, n + 3)
                    dve.reciprocal(se[:, u, :], se[:, u, :]).then_inc(rec, 1)
                    dve.wait_ge(rec, n + 1)
                    dve.tensor_scalar(sc[:, u, :], e[:, u, :], se[:, u, :], None, ALU.mult).then_inc(sc_ok, 1)
                    dve.wait_ge(sc_ok, n + 3)
                    dve.sem_inc(begun, 1)
                    dve.max(top[:, u, :], sc[:, u, :]).then_inc(top_ok, 1)
                    dve.wait_ge(top_ok, n + 1)
                    dve.tensor_scalar(tile(n, rt.top).rearrange("p o k -> p (o k)"), top[:, u, :], 1.0, None,
                                      ALU.mult).then_inc(kept, 1)
                    dve.max_index(idx[:, u, :], top[:, u, :], sc[:, u, :]).then_inc(idx_ok, 1)
                    dve.wait_ge(idx_ok, n + 1)
                    dve.tensor_copy(idf[:, u, :], idx[:, u, :]).then_inc(idf_ok, 1)
                    dve.wait_ge(idf_ok, n + 1)
                    hot = tile(n, rt.hot).rearrange("p o k e -> p (o k) e")
                    dve.tensor_tensor(hot, idf[:, u, 0:TOPK].unsqueeze(2).to_broadcast([P, TOPK, NE]),
                                      st.c("iota_e").unsqueeze(1).to_broadcast([P, TOPK, NE]),
                                      ALU.is_equal).then_inc(hot_ok, 1)
                    dve.wait_ge(hot_ok, n + 1)
                    with nc.allow_low_precision("zeros and ones"):
                        dve.tensor_reduce(tile(n, rt.sel).rearrange("p o e -> p (o e)"),
                                          hot.rearrange("p k e -> p e k"), AX.X, ALU.add).then_inc(sel_ok, 1)
                    dve.wait_ge(sel_ok, n + 1)
                    dve.wait_ge(cum_ok, n + 1)
                    dve.tensor_tensor(tile(n + 1, rt.cum), tile(n, rt.cum), tile(n, rt.sel),
                                      ALU.add).then_inc(cum_ok, 1)

        @block.gpsimd
        def _(pool):
            pool.sem_inc(xs_ok, 2)
            with pool.Fori(0, NT // 4) as q:
                for k in range(4):
                    n, u = 4 * q + k, k % 2
                    pool.wait_ge(xn_ok, n + 1)
                    pool.tensor_copy(xna[:, ds(n, 1), :].rearrange("p o d -> p (o d)"), xn[:, u, :]).then_inc(xs_ok, 1)

        @block.tensor
        def _(pe):
            pe.wait_ge(w_ld, 16)
            with pe.Fori(0, NT // 4) as q:
                def transposes(k):
                    n, u = 4 * q + k, k % 2
                    pe.wait_ge(xn_ok, n + 1)
                    pe.wait_ge(xt_ok, n + 1)
                    for c in range(KD):
                        last = pe.transpose(p_t[u][:, c, :], xn[:, u, c * P:(c + 1) * P], st.c("ident"))
                    last.then_inc(xt_ps, 1)

                transposes(0)
                for k in range(4):
                    n, u = 4 * q + k, k % 2
                    if k < 3:
                        transposes(k + 1)
                    pe.wait_ge(xt_ok, n + 3)
                    pe.wait_ge(mx_ok, n + 1)
                    pe.wait_ge(e_ok, n + 1)
                    for c in range(KD):
                        last = pe.matmul(p_l[u][:, 0:NE], xt[:, u, c, :], wr[:, c, :], start=c == 0, stop=c == KD - 1)
                    last.then_inc(l_ps, 1)

        @block.scalar
        def _(act):
            finish_stats(nc, st, act, None, eps, root, rstd)
            act.sem_inc(xt_ok, 2)
            act.sem_inc(e_ok, 2)
            with act.Fori(0, NT // 4) as q:
                def take_xt(k):
                    n, u = 4 * q + k, k % 2
                    act.wait_ge(xt_ps, n + 3)
                    act.wait_ge(mx_ok, n + 1)
                    act.activation(xt[:, u], p_t[u][:, 0:KD, :], ACT.Copy).then_inc(xt_ok, 1)

                take_xt(0)
                for k in range(4):
                    n, u = 4 * q + k, k % 2
                    if k < 3:
                        take_xt(k + 1)
                    act.wait_ge(mx_ok, n + 3)
                    act.wait_ge(sc_ok, n + 1)
                    act.activation(e[:, u, :], p_l[u][:, 0:NE], ACT.Exp, bias=nm[:, u, :],
                                   accum_out=se[:, u, :]).then_inc(e_ok, 1)


def phase_dispatch(nc, st, rt, xna, xs_dram, zero_sem, n_zero):
    with ExitStack() as ctx:
        sb, ps, sem = opener(nc, ctx, "dp2")
        cnt_ps, gt_ok, til_ok, scan_ok, base_ok, cmp_ok, ecol_ok, erow_ps, erf_ok, er_ok = (
            sem(n) for n in ("cnt", "gt", "til", "scan", "base", "cmp", "ecol", "erow_ps", "erf", "er"))
        begun, r_ps, posf_ok, prod_ok, pos_ok, posu_ok, stg_ok, sent, sh_d = (
            sem(n) for n in ("begun", "r_ps", "posf", "prod", "pos", "posu", "stg", "sent", "sh"))
        scat = [sem(f"scat{i}") for i in range(2)]
        gt = sb("gt", [P, NE, 16])
        til = sb("til", [P, NE])
        scan = sb("scan", [P, NE])
        base = sb("base", [P, NE])
        cmp_ = sb("cmp", [P, 2, NE])
        ecol = sb("ecol", [P, 2])
        erf = sb("erf", [1, MT])
        posf = sb("posf", [P, 2, NE])
        prod = sb("prod", [P, 2, TOPK, NE])
        pos = sb("pos", [P, 2, 8])
        posu = [sb(f"posu{i}", [P, 8], U32) for i in range(2)]
        stg = [sb(f"stg{i}", [P, D]) for i in range(2)]
        p_c = ps("p_c", [P, 512])
        p_e = ps("p_e", [P, 512])
        p_r = [ps(f"p_r{i}", [P, 512]) for i in range(2)]
        block = ctx.enter_context(nc.Block())

        @block.sync
        def _(sp):
            sp.dma_start(xs_dram[XT * P:MT * P, :].rearrange("(t p) d -> p t d", p=P), xna[:, :, :]).then_inc(sh_d, 16)
            sp.wait_ge(sh_d, 16)

        @block.tensor
        def _(pe):
            pe.sem_inc(posf_ok, 2)
            pe.sem_inc(sent, 2)
            pe.matmul(p_c[:, 0:NE], st.cb[:, 3, :], rt.cum[:, NT, :], start=True, stop=True).then_inc(cnt_ps, 1)
            pe.wait_ge(ecol_ok, 2)
            for i in range(2):
                last = pe.matmul(p_e[0:1, i * P:(i + 1) * P], ecol[:, i:i + 1], st.c("ident"), start=True, stop=True)
            last.then_inc(erow_ps, 1)
            with pe.Fori(0, NT // 2) as q:
                for u in range(2):
                    n = 2 * q + u
                    pe.wait_ge(posf_ok, n + 1)
                    pe.matmul(p_r[u][:, 0:NE], st.cb[:, 3, :], rt.cum[:, ds(n, 1), :].rearrange("p o e -> p (o e)"),
                              start=True, stop=False)
                    pe.matmul(p_r[u][:, 0:NE], st.cb[:, 2, :], rt.sel[:, ds(n, 1), :].rearrange("p o e -> p (o e)"),
                              start=False, stop=True).then_inc(r_ps, 1)

        @block.vector
        def _(dve):
            dve.wait_ge(cnt_ps, 1)
            dve.tensor_tensor(gt[:, :, :], p_c[:, 0:NE].unsqueeze(2).to_broadcast([P, NE, 16]),
                              st.c("k128").unsqueeze(1).to_broadcast([P, NE, 16]), ALU.is_gt).then_inc(gt_ok, 1)
            dve.wait_ge(gt_ok, 1)
            dve.tensor_reduce(til[:, :], gt[:, :, :], AX.X, ALU.add).then_inc(til_ok, 1)
            dve.wait_ge(til_ok, 1)
            dve.tensor_tensor_scan(scan[:, :], st.c("ones")[:, 0:NE], til[:, :], 0.0, ALU.mult,
                                   ALU.add).then_inc(scan_ok, 1)
            dve.wait_ge(scan_ok, 1)
            dve.tensor_tensor(base[:, :], scan[:, :], til[:, :], ALU.subtract).then_inc(base_ok, 1)
            dve.wait_ge(base_ok, 1)
            dve.tensor_scalar(base[:, :], base[:, :], float(P), None, ALU.mult).then_inc(base_ok, 1)
            for i in range(2):
                dve.tensor_scalar(cmp_[:, i, :], scan[:, :], st.c("iota_p")[:, i:i + 1], None,
                                  ALU.is_le).then_inc(cmp_ok, 1)
                dve.wait_ge(cmp_ok, i + 1)
                dve.tensor_reduce(ecol[:, i:i + 1], cmp_[:, i, :], AX.X, ALU.add).then_inc(ecol_ok, 1)
            dve.memset(erf[:, XT:MT], float(NE)).then_inc(erf_ok, 1)
            dve.wait_ge(erow_ps, 1)
            dve.tensor_scalar(erf[:, 0:XT], p_e[0:1, 0:XT], float(NE - 1), None, ALU.min).then_inc(erf_ok, 1)
            dve.wait_ge(erf_ok, 2)
            dve.tensor_copy(rt.erow[:, :], erf[:, :]).then_inc(er_ok, 1)
            dve.wait_ge(base_ok, 2)
            with dve.Fori(0, NT // 2) as q:
                for u in range(2):
                    n = 2 * q + u
                    dve.wait_ge(r_ps, n + 1)
                    dve.tensor_tensor(posf[:, u, :], p_r[u][:, 0:NE], base[:, :], ALU.add).then_inc(posf_ok, 1)
                    dve.wait_ge(posf_ok, n + 3)
                    dve.tensor_tensor(prod[:, u], rt.hot[:, ds(n, 1)].rearrange("p o k e -> p (o k) e"),
                                      posf[:, u, :].unsqueeze(1).to_broadcast([P, TOPK, NE]),
                                      ALU.mult).then_inc(prod_ok, 1)
                    dve.wait_ge(prod_ok, n + 1)
                    dve.tensor_reduce(pos[:, u, 0:TOPK], prod[:, u], AX.X, ALU.add).then_inc(pos_ok, 1)
                    dve.wait_ge(pos_ok, n + 1)
                    dve.wait_ge(sent, n + 1)
                    dve.tensor_copy(posu[u][:, 0:TOPK], pos[:, u, 0:TOPK]).then_inc(posu_ok, 1)
                    dve.tensor_copy(rt.pos[:, ds(n, 1), 0:TOPK].rearrange("p o k -> p (o k)"),
                                    pos[:, u, 0:TOPK]).then_inc(posu_ok, 1)

        @block.scalar
        def _(act):
            with act.Fori(0, NT // 2) as q:
                for u in range(2):
                    n = 2 * q + u
                    act.wait_ge(sent, n + 1)
                    act.activation(stg[u][:, :], xna[:, ds(n, 1), :].rearrange("p o d -> p (o d)"),
                                   ACT.Copy).then_inc(stg_ok, 1)

        @block.gpsimd
        def _(pool):
            pool.wait_ge(zero_sem, 16 * n_zero)
            with pool.Fori(0, NT // 2) as q:
                for u in range(2):
                    n = 2 * q + u
                    pool.wait_ge(posu_ok, 2 * n + 1)
                    pool.wait_ge(stg_ok, n + 1)
                    pool.sem_inc(begun, 1)
                    for k in range(TOPK):
                        pool.indirect_dma_start(xs_dram[0:XT * P, :],
                                                bass.IndirectOffsetOnAxis(posu[u][:, k:k + 1], 0),
                                                stg[u][:, :], None).then_inc(scat[u], 16)
                for u in range(2):
                    pool.wait_ge(scat[u], 16 * TOPK * (q + 1))
                    pool.sem_inc(sent, 1)


def phase_experts(nc, st, rt, xs_dram, ys_dram, wgv_in, we_in):
    U, NB = 8, 4
    with ExitStack() as ctx:
        sb, ps, sem = opener(nc, ctx, "ex")
        ld_w = [sem(f"ld_w{i}") for i in range(NB)]
        ld_x = [sem(f"ld_x{i}") for i in range(NB)]
        stored = [sem(f"stored{i}") for i in range(2)]
        xt_ps, xt_ok, gv_ps, sg_ok, h_ok, ht_ps, ht_ok, y_ps, y_ok, y_free = (
            sem(n) for n in ("xt_ps", "xt", "gv_ps", "sg", "h", "ht_ps", "ht", "y_ps", "y", "y_free"))
        xs = sb("xs", [P, NB, D])
        wgv = sb("wgv", [P, NB, KD, 2 * FE])
        we = sb("we", [FH, NB, 2, D])
        xt = sb("xt", [P, 2, KD, P])
        sg = sb("sg", [P, 2, FE])
        h = sb("h", [P, 2, FE])
        ht = sb("ht", [FH, 2, 2, P])
        y = sb("y", [P, NB, D])
        p_x, p_gv, p_h, p_y = ([ps(f"p_{m}{i}", [P, 512]) for i in range(2)] for m in ("x", "gv", "h", "y"))
        block = ctx.enter_context(nc.Block())

        @block.sync
        def _(sp):
            sp.sem_inc(y_ps, NB)
            sp.sem_inc(xt_ps, NB)
            with sp.Fori(0, MT // U) as q:
                for k in range(U):
                    n, s = U * q + k, k % NB
                    e = sp.value_load(rt.erow[0:1, ds(n, 1)], min_val=0, max_val=NE)
                    sp.wait_ge(xt_ps, n + 1)
                    sp.dma_start(xs[:, s, :],
                                 xs_dram[ds(n * P, P), :]).then_inc(ld_x[s], 16)
                    sp.wait_ge(y_ps, n + 1)
                    sp.dma_start(wgv[:, s, :, :], wgv_in[ds(e, 1)].rearrange("o p k f -> p (o k) f")
                                 ).then_inc(ld_w[s], 16)
                    sp.dma_start(we[:, s, :, :], we_in[ds(e, 1)].rearrange("o p k f -> p (o k) f")
                                 ).then_inc(ld_w[s], 16)

        @block.tensor
        def _(pe):
            with pe.Fori(0, MT // U) as q:
                m = q * (U // NB)

                def x_part(k):
                    n, s, u = U * q + k, k % NB, k % 2
                    pe.wait_ge(ld_x[s], 16 * m + 16 * (k // NB) + 16)
                    pe.wait_ge(xt_ok, n + 1)
                    for c in range(KD):
                        last = pe.transpose(p_x[u][:, c * P:(c + 1) * P], xs[:, s, c * P:(c + 1) * P], st.c("ident"))
                    last.then_inc(xt_ps, 1)

                def gv_part(k):
                    n, s, u = U * q + k, k % NB, k % 2
                    pe.wait_ge(ld_w[s], 32 * m + 32 * (k // NB) + 32)
                    pe.wait_ge(xt_ok, n + 3)
                    pe.wait_ge(h_ok, n + 1)
                    for c in range(KD):
                        last = pe.matmul(p_gv[u][:, 0:2 * FE], xt[:, u, c, :], wgv[:, s, c, :],
                                         start=c == 0, stop=c == KD - 1)
                    last.then_inc(gv_ps, 1)

                def h_part(k):
                    n, u = U * q + k, k % 2
                    pe.wait_ge(h_ok, n + 3)
                    pe.wait_ge(ht_ok, n + 1)
                    for c in range(2):
                        last = pe.transpose(p_h[u][0:FH, c * P:(c + 1) * P], h[:, u, c * FH:(c + 1) * FH],
                                            st.c("ident"))
                    last.then_inc(ht_ps, 1)

                def y_part(k):
                    n, s, u = U * q + k, k % NB, k % 2
                    pe.wait_ge(ht_ok, n + 3)
                    pe.wait_ge(y_ok, n + 1)
                    for c in range(2):
                        last = pe.matmul(p_y[u][:, 0:D], ht[:, u, c, :], we[:, s, c, :], start=c == 0, stop=c == 1)
                    last.then_inc(y_ps, 1)

                for k in range(U + 3):
                    if k < U:
                        x_part(k)
                    if 1 <= k < U + 1:
                        gv_part(k - 1)
                    if 2 <= k < U + 2:
                        h_part(k - 2)
                    if 3 <= k:
                        y_part(k - 3)

        @block.scalar
        def _(act):
            act.sem_inc(xt_ok, 2)
            act.sem_inc(ht_ok, 2)
            act.sem_inc(gv_ps, 2)
            act.sem_inc(ht_ps, 2)
            with act.Fori(0, MT // U) as q:
                def take_x(k):
                    n, u = U * q + k, k % 2
                    act.wait_ge(xt_ps, n + NB + 1)
                    act.wait_ge(gv_ps, n + 1)
                    act.activation(xt[:, u], p_x[u][:, 0:D].rearrange("p (c t) -> p c t", c=KD),
                                   ACT.Copy).then_inc(xt_ok, 1)

                def gate(k):
                    n, u = U * q + k, k % 2
                    act.wait_ge(gv_ps, n + 3)
                    act.wait_ge(h_ok, n + 1)
                    act.activation(sg[:, u, :], p_gv[u][:, 0:FE], ACT.Silu).then_inc(sg_ok, 1)

                def take_h(k):
                    n, u = U * q + k, k % 2
                    act.wait_ge(ht_ps, n + 3)
                    act.wait_ge(y_ps, n + NB - 1)
                    act.activation(ht[:, u], p_h[u][0:FH, 0:2 * P].rearrange("p (c t) -> p c t", c=2),
                                   ACT.Copy).then_inc(ht_ok, 1)

                for k in range(U + 2):
                    if k < U:
                        take_x(k)
                    if 1 <= k < U + 1:
                        gate(k - 1)
                    if 2 <= k:
                        take_h(k - 2)

        @block.vector
        def _(dve):
            dve.sem_inc(h_ok, 2)
            dve.sem_inc(y_ok, 2)
            dve.sem_inc(y_free, NB)
            with dve.Fori(0, MT // U) as q:
                def gate(k):
                    n, u = U * q + k, k % 2
                    dve.wait_ge(sg_ok, n + 1)
                    dve.wait_ge(ht_ps, n + 1)
                    dve.tensor_tensor(h[:, u, :], sg[:, u, :], p_gv[u][:, FE:2 * FE], ALU.mult).then_inc(h_ok, 1)

                def take_y(k):
                    n, u = U * q + k, k % 2
                    dve.wait_ge(y_ps, n + NB + 1)
                    dve.wait_ge(y_free, n + 1)
                    dve.tensor_copy(y[:, k % NB, :], p_y[u][:, 0:D]).then_inc(y_ok, 1)

                for k in range(U + 2):
                    if k < U:
                        gate(k)
                    if 2 <= k:
                        take_y(k - 2)

        @block.gpsimd
        def _(pool):
            with pool.Fori(0, MT // U) as q:
                for k in range(U):
                    n, u = U * q + k, k % 2
                    pool.wait_ge(y_ok, n + 3)
                    pool.dma_start(ys_dram[ds(n * P, P), :], y[:, k % NB, :]).then_inc(stored[u], 16)
                    if u == 1:
                        for done in stored:
                            pool.wait_ge(done, 16 * (U // 2) * q + 16 * ((k + 1) // 2))
                            pool.sem_inc(y_free, 1)


def phase_combine(nc, st, rt, ys_dram, yout):
    with ExitStack() as ctx:
        sb, ps, sem = opener(nc, ctx, "cb")
        begun, pos_ok, w_ok, sh_d, y_ok, stat, agg = (
            sem(n) for n in ("begun", "pos", "w", "sh", "y", "stat", "agg"))
        g_d = [sem(f"g{i}") for i in range(2)]
        posu = [sb(f"posu{i}", [P, 8], U32) for i in range(2)]
        w = sb("w", [P, 2, 8])
        g = [[sb(f"g{i}_{k}", [P, D]) for k in range(TOPK)] for i in range(2)]
        acc = sb("acc", [P, 2, 2, D])
        stats = sb("stats", [P, NT, 6])
        block = ctx.enter_context(nc.Block())
        S = TOPK

        @block.sync
        def _(sp):
            sp.dma_start(yout[:, :, :], ys_dram[XT * P:MT * P, :].rearrange("(t p) d -> p t d", p=P)).then_inc(sh_d, 16)
            sp.wait_ge(sh_d, 16)

        @block.vector
        def _(dve):
            dve.sem_inc(y_ok, S + 1)
            dve.wait_ge(sh_d, 16)
            with dve.Fori(0, NT // 2) as q:
                for u in range(2):
                    n = 2 * q + u
                    dve.tensor_copy(w[:, u, :], rt.top[:, ds(n, 1), :].rearrange("p o k -> p (o k)")).then_inc(w_ok, 1)
                    dve.wait_ge(w_ok, n + 1)
                    dve.wait_ge(g_d[u], 16 * TOPK * q + 16 * TOPK)
                    for k in range(TOPK):
                        dve.wait_ge(y_ok, S * n + S + k + 1)
                        src = yout[:, ds(n, 1), :].rearrange("p o d -> p (o d)") if k == 0 else acc[:, u, k % 2, :]
                        dst = yout[:, ds(n, 1), :].rearrange("p o d -> p (o d)") if k == TOPK - 1 \
                            else acc[:, u, (k + 1) % 2, :]
                        dve.scalar_tensor_tensor(dst, g[u][k][:, :], w[:, u, k:k + 1], src,
                                                 ALU.mult, ALU.add).then_inc(y_ok, 1)
                    dve.wait_ge(y_ok, S * n + 2 * S + 1)
                    dve.bn_stats(stats[:, ds(n, 1), :].rearrange("p o d -> p (o d)"),
                                 yout[:, ds(n, 1), :].rearrange("p o d -> p (o d)")).then_inc(stat, 1)
            dve.wait_ge(stat, NT)
            for n in range(NT):
                dve.bn_aggr(st.mv[:, n, :], stats[:, n, :]).then_inc(agg, 1)

        @block.scalar
        def _(act):
            for u in range(2):
                act.activation(posu[u][:, 0:TOPK], rt.pos[:, u, 0:TOPK], ACT.Copy).then_inc(pos_ok, 1)
            with act.Fori(0, NT // 2 - 1) as q:
                for u in range(2):
                    n = 2 * q + u
                    act.wait_ge(g_d[u], 16 * TOPK * q + 16 * TOPK)
                    act.activation(posu[u][:, 0:TOPK], rt.pos[:, ds(n + 2, 1), 0:TOPK].rearrange("p o k -> p (o k)"),
                                   ACT.Copy).then_inc(pos_ok, 1)

        @block.gpsimd
        def _(pool):
            with pool.Fori(0, NT // 2) as q:
                for u in range(2):
                    n = 2 * q + u
                    pool.wait_ge(pos_ok, n + 1)
                    pool.wait_ge(y_ok, S * n + 1)
                    pool.sem_inc(begun, 1)
                    for k in range(TOPK):
                        pool.indirect_dma_start(g[u][k][:, :], None, ys_dram[0:XT * P, :],
                                                bass.IndirectOffsetOnAxis(posu[u][:, k:k + 1], 0)).then_inc(g_d[u], 16)


def phase_attention(nc, st, w_in, wo_in, y):
    UN = TB * H
    SB, PB = 3, 4
    with ExitStack() as ctx:
        sb, ps, sem = opener(nc, ctx, "at")
        w_ld, eps, root, rstd, pad_ok = (sem(n) for n in ("w_ld", "eps", "root", "rstd", "pad"))
        xn_ok, xt_ps, xt_ok, qk_ps, rot_in, rot_ok, qkt_ps, v_out, qkt_out = (
            sem(n) for n in ("xn", "xt_ps", "xt", "qk_ps", "rot_in", "rot", "qkt_ps", "v_out", "qkt_out"))
        s_ps, max_ok, exp_ok, rec_ok, norm_ok, pt_ps, pt_a, pt_v, o_ps, on_ok, y_ps, y_ok = (
            sem(n) for n in ("s_ps", "max", "exp", "rec", "norm", "pt_ps", "pt_a", "pt_v", "o_ps", "on", "y_ps", "y"))
        stat, agg, begun = sem("stat"), sem("agg"), sem("begun")
        w = sb("w", [P, KD, 3 * D])
        wo = sb("wo", [P, HG, D])
        xn = sb("xn", [P, 2, D])
        xt = sb("xt", [P, 2, KD, P])
        rc = sb("rc", [P, 2, 2 * D])
        rs = sb("rs", [P, 2, 2 * D])
        qk = sb("qk", [P, 2, 2 * D])
        kt = sb("kt", [P, HG, L])
        qm = [sb(f"qm{i}", [P, HG, L]) for i in range(2)]
        vp = sb("vp", [P, TB, H, 2 * DH])
        nm = sb("nm", [P, PB, 1])
        se = sb("se", [P, PB, 1])
        pr = sb("pr", [P, PB, L])
        pt = sb("pt", [P, 2, L])
        on = sb("on", [P, 2, HG, P])
        stats = sb("stats", [P, NT, 6])
        p_s = [ps(f"p_s{i}", [P, L]) for i in range(SB)]
        p_t = [ps(f"p_t{i}", [P, L]) for i in range(2)]
        p_o = [ps(f"p_o{i}", [P, 4, P]) for i in range(2)]
        p_y = ps("p_y", [P, L])
        block = ctx.enter_context(nc.Block())

        def by_act(i):
            return i % 4 == 3

        n_act = sum(by_act(i) for i in range(UN))

        def taken(i):
            a = sum(by_act(k) for k in range(i + 1))
            return a, i + 1 - a

        @block.sync
        def _(sp):
            sp.dma_start(w[:, :, :], w_in).then_inc(w_ld, 16)
            sp.dma_start(wo[:, :, :], wo_in).then_inc(w_ld, 16)
            sp.wait_ge(w_ld, 32)

        @block.vector
        def _(dve):
            finish_stats(nc, st, None, dve, eps, root, rstd)
            with dve.Fori(0, B) as b:
                for t in range(TB):
                    n = TB * b + t
                    if t < 2:
                        dve.wait_ge(xt_ps, TB * b + 1)
                    else:
                        dve.wait_ge(xt_ps, n)
                    dve.tensor_scalar(xn[:, t % 2, :], st.x[:, ds(n, 1), :], st.mv[:, ds(n, 1), 0],
                                      st.rstd[:, ds(n, 1)], ALU.subtract, ALU.mult).then_inc(xn_ok, 1)
                for t in range(TB):
                    n = TB * b + t
                    dve.wait_ge(qk_ps, n + 1)
                    if t < 2:
                        dve.wait_ge(rot_ok, 2 * TB * b + 1)
                    else:
                        dve.wait_ge(rot_ok, 2 * n - 1)
                    src = p_s[t % 2][:, :].rearrange("p (h j s) -> p h (j s)", h=2 * H, s=2) \
                        .rearrange("p h (j s) -> p h j s", s=2)
                    for dst, name in ((rc, "cos"), (rs, "sin")):
                        table = st.c(name)[:, t * DH // 2:(t + 1) * DH // 2]
                        for s in range(2):
                            dve.tensor_tensor(dst[:, t % 2, :].rearrange("p (h j s) -> p h j s", h=2 * H, s=2)[..., s],
                                              src[..., s], table.unsqueeze(1).to_broadcast([P, 2 * H, DH // 2]),
                                              ALU.mult).then_inc(rot_in, 1)

                for i in range(UN + 3):
                    if i < UN:
                        n = UN * b + i
                        dve.wait_ge(s_ps, n + 1)
                        if i >= PB:
                            dve.wait_ge(exp_ok, n - PB + 1)
                        nk = i // H + 1
                        dve.tensor_reduce(nm[:, i % PB, :], p_s[i % SB][:, 0:nk * P], AX.X, ALU.max,
                                          negate=True).then_inc(max_ok, 1)
                    if 1 <= i <= UN:
                        dve.wait_ge(exp_ok, UN * b + i)
                        dve.reciprocal(se[:, (i - 1) % PB, :], se[:, (i - 1) % PB, :]).then_inc(rec_ok, 1)
                    if i >= 3:
                        k = i - 3
                        if not by_act(k):
                            nk = k // H + 1
                            dve.wait_ge(pt_ps, UN * b + k + 1)
                            if k >= 2:
                                dve.wait_ge(o_ps, UN * b + k - 1)
                            dve.tensor_copy(pt[:, k % 2, 0:nk * P], p_t[k % 2][:, 0:nk * P]).then_inc(pt_v, 1)
                for t in range(TB):
                    n = TB * b + t
                    dve.wait_ge(y_ok, n + 2)
                    dve.bn_stats(stats[:, ds(n, 1), :].rearrange("p o s -> p (o s)"),
                                 y[:, ds(n, 1), :].rearrange("p o d -> p (o d)")).then_inc(stat, 1)
            dve.wait_ge(stat, NT)
            for n in range(NT):
                dve.bn_aggr(st.mv[:, n, :], stats[:, n, :]).then_inc(agg, 1)

        @block.gpsimd
        def _(pool):
            pool.sem_inc(rot_ok, 1)
            pool.memset(vp[:, :, :, :], 0.0).then_inc(pad_ok, 1)
            with pool.Fori(0, B) as b:
                for t in range(TB):
                    n = TB * b + t
                    pool.wait_ge(rot_in, 4 * n + 4)
                    if t < 2:
                        pool.wait_ge(qkt_ps, TB * b + 1)
                    else:
                        pool.wait_ge(qkt_ps, n)
                    c, s, o = (a[:, t % 2, :].rearrange("p (m e) -> p m e", e=2) for a in (rc, rs, qk))
                    pool.tensor_tensor(o[:, :, 0], c[:, :, 0], s[:, :, 1], ALU.subtract).then_inc(rot_ok, 1)
                    pool.tensor_tensor(o[:, :, 1], s[:, :, 0], c[:, :, 1], ALU.add).then_inc(rot_ok, 1)
                for i in range(UN):
                    nk = i // H + 1
                    pool.wait_ge(rec_ok, UN * b + i + 1)
                    pool.sem_inc(begun, 1)
                    pool.tensor_scalar(pr[:, i % PB, 0:nk * P], pr[:, i % PB, 0:nk * P], se[:, i % PB, :], None,
                                       ALU.mult).then_inc(norm_ok, 1)

        @block.scalar
        def _(act):
            act.sem_inc(y_ok, 1)
            finish_stats(nc, st, act, None, eps, root, rstd)
            act.wait_ge(pad_ok, 1)
            with act.Fori(0, B) as b:
                def take_xt(t):
                    n = TB * b + t
                    act.wait_ge(xt_ps, n + 2)
                    if t >= 2:
                        act.wait_ge(qk_ps, n - 1)
                    act.activation(xt[:, t % 2], p_t[t % 2][:, 0:D].rearrange("p (c t) -> p c t", c=KD),
                                   ACT.Copy).then_inc(xt_ok, 1)

                def take_v(t):
                    n = TB * b + t
                    act.wait_ge(qk_ps, n + 1)
                    for s in range(2):
                        act.activation(vp[:, t, s:H:2, s * DH:(s + 1) * DH],
                                       p_o[t % 2][:, 0:2, :].rearrange("p a (h s d) -> p (a h) s d", s=2, d=DH)[:, :, s],
                                       ACT.Copy).then_inc(v_out, 1)

                def take_qkt(t):
                    n = TB * b + t
                    act.wait_ge(qkt_ps, n + 2)
                    src = p_y[:, :].rearrange("p (m t) -> p m t", m=4)
                    cols = slice(t * P, (t + 1) * P)
                    act.activation(kt[:, :, cols], src[:, 2:4], ACT.Copy).then_inc(qkt_out, 1)
                    for s, name in enumerate(("even", "odd")):
                        act.activation(qm[s][:, :, cols], src[:, 0:2], ACT.Copy, scale=st.c(name)).then_inc(qkt_out, 1)

                take_xt(0)
                for t in range(TB + 1):
                    if t + 1 < TB:
                        take_xt(t + 1)
                    if t < TB:
                        take_v(t)
                    if t >= 1:
                        take_qkt(t - 1)

                for i in range(UN + 3):
                    if i < UN:
                        nk = i // H + 1
                        act.wait_ge(max_ok, UN * b + i + 1)
                        if i >= PB:
                            act.wait_ge(pt_ps, UN * b + i - PB + 1)
                        act.activation(pr[:, i % PB, 0:nk * P], p_s[i % SB][:, 0:nk * P], ACT.Exp,
                                       bias=nm[:, i % PB, :], accum_out=se[:, i % PB, :]).then_inc(exp_ok, 1)
                    if i >= 3 and by_act(i - 3):
                        k = i - 3
                        nk = k // H + 1
                        act.wait_ge(pt_ps, UN * b + k + 1)
                        if k >= 2:
                            act.wait_ge(o_ps, UN * b + k - 1)
                        act.activation(pt[:, k % 2, 0:nk * P], p_t[k % 2][:, 0:nk * P], ACT.Copy).then_inc(pt_a, 1)
                    for t in range(TB):
                        if i == min(H * (t + 1) + 5, UN + 2):
                            n = TB * b + t
                            act.wait_ge(o_ps, UN * b + H * (t + 1))
                            if t >= 2:
                                act.wait_ge(y_ps, n - 1)
                            act.activation(on[:, t % 2], p_o[t % 2][:, 0:HG, :], ACT.Copy).then_inc(on_ok, 1)
                            act.wait_ge(y_ps, n + 1)
                            act.activation(y[:, ds(n, 1), :].rearrange("p o d -> p (o d)"), p_y[:, 0:D],
                                           ACT.Copy).then_inc(y_ok, 1)

        @block.tensor
        def _(pe):
            pe.sem_inc(xt_ps, 1)
            pe.sem_inc(qkt_ps, 1)
            pe.wait_ge(w_ld, 32)
            with pe.Fori(0, B) as b:
                pe.wait_ge(y_ok, TB * b + 1)

                def x_part(t):
                    n = TB * b + t
                    pe.wait_ge(xn_ok, n + 1)
                    if t >= 2:
                        pe.wait_ge(xt_ok, n - 1)
                    for c in range(KD):
                        last = pe.transpose(p_t[t % 2][:, c * P:(c + 1) * P], xn[:, t % 2, c * P:(c + 1) * P],
                                            st.c("ident"))
                    last.then_inc(xt_ps, 1)

                def qkv_part(t):
                    n = TB * b + t
                    pe.wait_ge(xt_ok, n + 1)
                    if t >= 2:
                        pe.wait_ge(rot_in, 4 * n - 4)
                        pe.wait_ge(v_out, 2 * n - 2)
                    for c in range(KD):
                        pe.matmul(p_s[t % 2][:, :], xt[:, t % 2, c, :], w[:, c, 0:2 * D], start=c == 0, stop=c == KD - 1)
                    for c in range(KD):
                        last = pe.matmul(p_o[t % 2][:, 0:2, :], xt[:, t % 2, c, :], w[:, c, 2 * D:3 * D],
                                         start=c == 0, stop=c == KD - 1)
                    last.then_inc(qk_ps, 1)

                def qkt_part(t):
                    n = TB * b + t
                    pe.wait_ge(rot_ok, 2 * n + 3)
                    if t >= 1:
                        pe.wait_ge(qkt_out, 3 * n)
                    for m in range(4):
                        last = pe.transpose(p_y[:, m * P:(m + 1) * P], qk[:, t % 2, m * P:(m + 1) * P], st.c("ident"))
                    last.then_inc(qkt_ps, 1)

                x_part(0)
                for t in range(TB + 1):
                    if t + 1 < TB:
                        x_part(t + 1)
                    if t < TB:
                        qkv_part(t)
                    if t >= 1:
                        qkt_part(t - 1)

                def scores(i):
                    t, h = i // H, i % H
                    nk, hg, r = t + 1, h // HP, (h % HP) // 2 * 2 * DH
                    if i == 0:
                        pe.wait_ge(qkt_out, 3 * TB * (b + 1))
                        pe.wait_ge(rot_in, 4 * TB * (b + 1))
                    if i >= SB:
                        pe.wait_ge(exp_ok, UN * b + i - SB + 1)
                    rows = slice(r, r + 2 * DH)
                    pe.matmul(p_s[i % SB][:, 0:nk * P], qm[h % 2][rows, hg, t * P:(t + 1) * P], kt[rows, hg, 0:nk * P],
                              start=True, stop=False)
                    pe.matmul(p_s[i % SB][:, t * P:nk * P], st.cb[:, 0, :], st.cb[:, 1, :],
                              start=False, stop=True).then_inc(s_ps, 1)

                def transposes(i):
                    nk = i // H + 1
                    pe.wait_ge(norm_ok, UN * b + i + 1)
                    if i >= 2:
                        if by_act(i - 2):
                            pe.wait_ge(pt_a, n_act * b + taken(i - 2)[0])
                        else:
                            pe.wait_ge(pt_v, (UN - n_act) * b + taken(i - 2)[1])
                    for c in range(nk):
                        last = pe.transpose(p_t[i % 2][:, c * P:(c + 1) * P], pr[:, i % PB, c * P:(c + 1) * P],
                                            st.c("ident"))
                    last.then_inc(pt_ps, 1)

                def values(i):
                    t, h = i // H, i % H
                    nk, hg, r = t + 1, h // HP, (h % HP) // 2 * 2 * DH
                    if i == 0:
                        pe.wait_ge(v_out, 2 * TB * (b + 1))
                    if h == 0 and t >= 2:
                        pe.wait_ge(on_ok, TB * b + t - 1)
                    if by_act(i):
                        pe.wait_ge(pt_a, n_act * b + taken(i)[0])
                    else:
                        pe.wait_ge(pt_v, (UN - n_act) * b + taken(i)[1])
                    for c in range(nk):
                        last = pe.matmul(p_o[t % 2][r:r + 2 * DH, hg, :], vp[:, c, h, :], pt[:, i % 2, c * P:(c + 1) * P],
                                         start=c == 0 and h % 2 == 0, stop=c == nk - 1 and h % 2 == 1)
                    last.then_inc(o_ps, 1)

                def project(t):
                    n = TB * b + t
                    pe.wait_ge(on_ok, n + 1)
                    if t >= 1:
                        pe.wait_ge(y_ok, n + 1)
                    for g in range(HG):
                        last = pe.matmul(p_y[:, 0:D], on[:, t % 2, g, :], wo[:, g, :], start=g == 0, stop=g == HG - 1)
                    last.then_inc(y_ps, 1)

                for i in range(UN + 4):
                    if i < UN:
                        scores(i)
                    if 3 <= i < UN + 3:
                        transposes(i - 3)
                    if 4 <= i:
                        values(i - 4)
                    for t in range(TB):
                        if i == min(H * (t + 1) + 5, UN + 3):
                            project(t)


def phase_ffn(nc, st, wgu_in, wd_in, y):
    U = 4
    FQ = FF // 4
    with ExitStack() as ctx:
        sb, ps, sem = opener(nc, ctx, "ff")
        w_ld, wd_ld, eps, root, rstd, stat, agg = (sem(n) for n in ("w_ld", "wd_ld", "eps", "root", "rstd", "stat", "agg"))
        xn_ok, xt_ps, xt_ok, g_ps, u_ps, sg_ok, h_ok, abs_ok, c_ok, ef_ok, s_ok, k_ok, ht_ps, ht_ok, y_ps, y_ok = (
            sem(n) for n in ("xn", "xt_ps", "xt", "g_ps", "u_ps", "sg", "h", "abs", "c", "ef", "s", "k",
                             "ht_ps", "ht", "y_ps", "y"))
        wgu = sb("wgu", [P, KD, 2, FF])
        wd = sb("wd", [P, FF // P, D])
        xn = sb("xn", [P, 2, D])
        xt = sb("xt", [P, 2, KD, P])
        sg = sb("sg", [P, 2, 512])
        h = sb("h", [P, 2, FF])
        a = sb("a", [P, 2, FF])
        cm = sb("cm", [P, 2, 3, 2, FQ], BF16)
        ef = sb("ef", [P, 2, 2, 2, FQ], BF16)
        sm = sb("sm", [P, 2, 4, FQ], BF16)
        hk = sb("hk", [P, 2, FF])
        ht = sb("ht", [P, 2, FF // P, P])
        stats = sb("stats", [P, NT, 6])
        p_t = ps("p_t", [P, 512])
        p_g = [ps(f"p_g{i}", [P, 512]) for i in range(2)]
        p_u = [ps(f"p_u{i}", [P, 512]) for i in range(2)]
        p_h = [ps(f"p_h{i}", [P, 512]) for i in range(2)]
        p_y = ps("p_y", [P, 512])
        block = ctx.enter_context(nc.Block())

        def quads(ap):
            return ap.rearrange("p (m s) -> p s m", s=4)

        def self_stats(dve, n):
            dve.bn_stats(stats[:, ds(n, 1), :].rearrange("p o s -> p (o s)"),
                         y[:, ds(n, 1), :].rearrange("p o d -> p (o d)")).then_inc(stat, 1)

        @block.sync
        def _(sp):
            sp.dma_start(wgu[:, :, :, :], wgu_in).then_inc(w_ld, 16)
            sp.dma_start(wd[:, :, :], wd_in).then_inc(wd_ld, 16)
            sp.wait_ge(w_ld, 16)
            sp.wait_ge(wd_ld, 16)

        @block.vector
        def _(dve):
            dve.sem_inc(xt_ps, 2)
            dve.sem_inc(abs_ok, 2)
            dve.sem_inc(ef_ok, 4)
            dve.sem_inc(s_ok, 5)
            dve.sem_inc(ht_ps, 3)
            finish_stats(nc, st, None, dve, eps, root, rstd)

            def normalise(n, u):
                dve.wait_ge(xt_ps, n + 1)
                dve.tensor_scalar(xn[:, u, :], st.x[:, ds(n, 1), :], st.mv[:, ds(n, 1), 0], st.rstd[:, ds(n, 1)],
                                  ALU.subtract, ALU.mult).then_inc(xn_ok, 1)

            with dve.Fori(0, NT // U) as q:
                normalise(U * q, 0)
                for k in range(U):
                    n, u = U * q + k, k % 2
                    if k + 1 < U:
                        normalise(n + 1, 1 - u)
                    for j in range(2):
                        dve.wait_ge(sg_ok, 2 * n + j + 1)
                        dve.wait_ge(u_ps, 2 * n + j + 4)
                        dve.tensor_tensor(h[:, u, j * 512:(j + 1) * 512], sg[:, j, :], p_u[j][:, :],
                                          ALU.mult).then_inc(h_ok, 1)
                    dve.wait_ge(abs_ok, 2 * n + 4)
                    dve.wait_ge(s_ok, 4 * n + 1)
                    v = quads(a[:, u, :])
                    dve.tensor_tensor(cm[:, u, 0], v[:, 0:4:2], v[:, 1:4:2], ALU.is_ge).then_inc(c_ok, 1)
                    dve.tensor_tensor(cm[:, u, 1], v[:, 0:2], v[:, 2:4], ALU.is_ge).then_inc(c_ok, 1)
                    for s in range(2):
                        dve.tensor_tensor(cm[:, u, 2, s], v[:, s], v[:, 3 - s], ALU.is_ge).then_inc(c_ok, 1)
                    hv, kv = quads(h[:, u, :]), quads(hk[:, u, :])
                    dve.wait_ge(ht_ps, 2 * n + 1)
                    for s, (least, op) in enumerate(((2.0, ALU.is_ge), (1.0, ALU.is_ge), (0.0, ALU.is_ge),
                                                     (1.0, ALU.is_le))):
                        dve.wait_ge(s_ok, 4 * n + s + 6)
                        dve.scalar_tensor_tensor(kv[:, s], sm[:, u, s], least, hv[:, s], op, ALU.mult).then_inc(k_ok, 1)
                    dve.wait_ge(y_ok, n + 1)
                    if k > 0:
                        self_stats(dve, n - 1)
                dve.wait_ge(y_ok, U * q + U + 1)
                self_stats(dve, U * q + U - 1)
            dve.wait_ge(stat, NT)
            for n in range(NT):
                dve.bn_aggr(st.mv[:, n, :], stats[:, n, :]).then_inc(agg, 1)

        @block.gpsimd
        def _(pool):
            pool.sem_inc(k_ok, 5)
            with pool.Fori(0, NT // U) as q:
                for k in range(U):
                    n, u = U * q + k, k % 2
                    c, e = cm[:, u], ef[:, u]
                    pool.wait_ge(c_ok, 4 * n + 9)
                    pool.tensor_tensor(e[:, 0], c[:, 1], c[:, 2], ALU.add).then_inc(ef_ok, 1)
                    for s in range(2):
                        pool.tensor_tensor(e[:, 1, s], c[:, 1, s], c[:, 2, 1 - s], ALU.add).then_inc(ef_ok, 1)
                    pool.wait_ge(ef_ok, 3 * n + 7)
                    pool.wait_ge(k_ok, 4 * n + 1)
                    pool.tensor_tensor(sm[:, u, 0], c[:, 0, 0], e[:, 0, 0], ALU.add).then_inc(s_ok, 1)
                    pool.tensor_tensor(sm[:, u, 1], e[:, 0, 1], c[:, 0, 0], ALU.subtract).then_inc(s_ok, 1)
                    pool.tensor_tensor(sm[:, u, 2], c[:, 0, 1], e[:, 1, 0], ALU.subtract).then_inc(s_ok, 1)
                    pool.tensor_tensor(sm[:, u, 3], c[:, 0, 1], e[:, 1, 1], ALU.add).then_inc(s_ok, 1)

        @block.scalar
        def _(act):
            act.sem_inc(y_ok, 1)
            finish_stats(nc, st, act, None, eps, root, rstd)
            act.sem_inc(xt_ok, 1)
            act.sem_inc(h_ok, 2)
            act.sem_inc(c_ok, 5)
            act.sem_inc(u_ps, 3)
            act.sem_inc(ht_ok, 2)
            act.sem_inc(y_ps, 2)

            with act.Fori(0, NT // U) as q:
                def take_x(n, u):
                    act.wait_ge(xt_ps, n + 3)
                    act.wait_ge(u_ps, 2 * n + 1)
                    act.activation(xt[:, u], p_t[:, 0:D].rearrange("p (c t) -> p c t", c=KD), ACT.Copy).then_inc(xt_ok, 1)

                def take_h(n, u):
                    for j in range(2):
                        act.wait_ge(ht_ps, 2 * n + j + 4)
                        act.wait_ge(y_ps, n + 1)
                        act.activation(ht[:, u, 4 * j:4 * j + 4, :], p_h[j][:, :].rearrange("p (c t) -> p c t", t=P),
                                       ACT.Copy).then_inc(ht_ok, 1)

                def take_y(n):
                    act.wait_ge(y_ps, n + 3)
                    act.activation(y[:, ds(n, 1), :].rearrange("p o d -> p (o d)"), p_y[:, 0:D], ACT.Copy).then_inc(y_ok, 1)

                take_x(U * q, 0)
                for k in range(U):
                    n, u = U * q + k, k % 2
                    if k + 1 < U:
                        take_x(n + 1, 1 - u)
                    for j in range(2):
                        act.wait_ge(g_ps, 2 * n + j + 1)
                        act.wait_ge(h_ok, 2 * n + j + 1)
                        act.activation(sg[:, j, :], p_g[j][:, :], ACT.Silu).then_inc(sg_ok, 1)
                    for j in range(2):
                        act.wait_ge(h_ok, 2 * n + j + 3)
                        act.wait_ge(c_ok, 4 * n + 1)
                        act.activation(a[:, u, j * 512:(j + 1) * 512], h[:, u, j * 512:(j + 1) * 512],
                                       ACT.Abs).then_inc(abs_ok, 1)
                    if k > 0:
                        take_h(n - 1, 1 - u)
                        take_y(n - 1)
                take_h(U * q + U - 1, (U - 1) % 2)
                take_y(U * q + U - 1)

        @block.tensor
        def _(pe):
            pe.wait_ge(w_ld, 16)
            pe.wait_ge(wd_ld, 16)
            with pe.Fori(0, NT // U) as q:
                def x_part(n, u):
                    pe.wait_ge(xn_ok, n + 1)
                    pe.wait_ge(xt_ok, n + 1)
                    for c in range(KD):
                        last = pe.transpose(p_t[:, c * P:(c + 1) * P], xn[:, u, c * P:(c + 1) * P], st.c("ident"))
                    last.then_inc(xt_ps, 1)

                def gu_part(n, u):
                    pe.wait_ge(xt_ok, n + 2)
                    for j in range(2):
                        pe.wait_ge(h_ok, 2 * n + j + 1)
                        for m, (bank, done) in enumerate(((p_g[j], g_ps), (p_u[j], u_ps))):
                            for c in range(KD):
                                last = pe.matmul(bank[:, :], xt[:, u, c, :], wgu[:, c, m, j * 512:(j + 1) * 512],
                                                 start=c == 0, stop=c == KD - 1)
                            last.then_inc(done, 1)

                def h_part(n, u):
                    pe.wait_ge(k_ok, 4 * n + 9)
                    for j in range(2):
                        pe.wait_ge(ht_ok, 2 * n + j + 1)
                        for c in range(4):
                            last = pe.transpose(p_h[j][:, c * P:(c + 1) * P],
                                                hk[:, u, (4 * j + c) * P:(4 * j + c + 1) * P], st.c("ident"))
                        last.then_inc(ht_ps, 1)

                def y_part(n, u):
                    pe.wait_ge(ht_ok, 2 * n + 4)
                    pe.wait_ge(y_ok, n + 1)
                    for c in range(FF // P):
                        last = pe.matmul(p_y[:, 0:D], ht[:, u, c, :], wd[:, c, :], start=c == 0, stop=c == FF // P - 1)
                    last.then_inc(y_ps, 1)

                x_part(U * q, 0)
                for k in range(U):
                    n, u = U * q + k, k % 2
                    if k + 1 < U:
                        x_part(n + 1, 1 - u)
                    gu_part(n, u)
                    if k > 0:
                        h_part(n - 1, 1 - u)
                        y_part(n - 1, 1 - u)
                h_part(U * q + U - 1, (U - 1) % 2)
                y_part(U * q + U - 1, (U - 1) % 2)


def phase_last(nc, st, y, out):
    with ExitStack() as ctx:
        sb, ps, sem = opener(nc, ctx, "la")
        eps, root, rstd, yn, xs, o_d, cp = (sem(n) for n in ("eps", "root", "rstd", "yn", "x", "out", "copied"))
        block = ctx.enter_context(nc.Block())

        @block.scalar
        def _(act):
            finish_stats(nc, st, act, None, eps, root, rstd)

        @block.vector
        def _(dve):
            finish_stats(nc, st, None, dve, eps, root, rstd)
            for t in range(NT):
                dve.tensor_scalar(y[:, t, :], y[:, t, :], st.mv[:, t, 0:1], st.rstd[:, t:t + 1],
                                  ALU.subtract, ALU.mult).then_inc(yn, 1)
                dve.wait_ge(yn, t + 1)
                dve.tensor_tensor(st.x[:, t, :], st.x[:, t, :], y[:, t, :], ALU.add).then_inc(xs, 1)

        @block.sync
        def _(sp):
            for b in range(B):
                sp.wait_ge(xs, TB * (b + 1))
                sp.dma_start(out[b].rearrange("(t p) d -> p t d", p=P),
                             st.x[:, b * TB:(b + 1) * TB, :]).then_inc(o_d, 16)
            sp.wait_ge(o_d, 16 * B)


def build(nc, x, cst, w_dp, wo_d, onw, w_r, w_gv, w_e, w_at, wo_a, w_gu, w_down, out):
    kvb_dram = nc.dram_tensor("kvb_dram", (T, H, KVW), F32, kind="Internal").ap()
    xs_dram = nc.dram_tensor("xs_dram", (MT * P, D), F32, kind="Internal").ap()
    ys_dram = nc.dram_tensor("ys_dram", (MT * P, D), F32, kind="Internal").ap()
    with ExitStack() as ctx:
        def sb(c, name, shape, dt=F32):
            return c.enter_context(nc.sbuf_tensor(name, shape, dt))

        st = State(nc, ctx)
        phase_load(nc, st, x, cst)
        with ExitStack() as until_dispatch:
            zeros = sb(until_dispatch, "zeros", [P, 1024])
            zero_sem = until_dispatch.enter_context(nc.semaphore("slots_zeroed"))
            n_zero = XT * D // 1024
            att = sb(until_dispatch, "att", [P, C, NC_ * G])
            with ExitStack() as delta:
                mkv = sb(delta, "mkv", [P, NC_, G, C + KVW])
                kqt = sb(delta, "kqt", [P, NC_, G, 2, C])
                with ExitStack() as raw:
                    qr = sb(raw, "q_raw", [P, NT, D])
                    kvb = sb(raw, "kvb", [P, NT, H, KVW])
                    norms = sb(raw, "norms", [P, NT, 2 * H])
                    wall = sb(raw, "w_qkvb", [P, KD, 3 * D + H])
                    phase_delta_project(nc, st, w_dp, qr, kvb, norms, wall, zeros)
                    phase_delta_layout(nc, st, qr, kvb, norms, kqt, kvb_dram)
                phase_delta_scores(nc, st, kqt, kvb_dram, mkv, att)
                phase_delta_invert(nc, st, mkv, att, zeros, xs_dram, zero_sem, n_zero)
                xt = sb(delta, "xt", [P, NC_, G, 2, C])
                phase_delta_wy(nc, st, kqt, mkv, att, xt)
                ot = att[:, :, :].rearrange("p a b -> p (a b)").rearrange("p (g b l) -> p g b l", g=HG, b=B)
                phase_delta_chain(nc, st, mkv, xt, ot)
            y = sb(until_dispatch, "y_first", [P, NT, D])
            phase_delta_out(nc, st, ot, wo_d, onw, y)
            phase_update(nc, st, y, "up1")
            rt = Routing(nc, until_dispatch)
            phase_route(nc, st, rt, w_r, y)
            phase_dispatch(nc, st, rt, y, xs_dram, zero_sem, n_zero)
            phase_experts(nc, st, rt, xs_dram, ys_dram, w_gv, w_e)
            phase_combine(nc, st, rt, ys_dram, y)
            phase_update(nc, st, y, "up2")
        y = sb(ctx, "y", [P, NT, D])
        phase_attention(nc, st, w_at, wo_a, y)
        phase_update(nc, st, y, "up3")
        phase_ffn(nc, st, w_gu, w_down, y)
        phase_last(nc, st, y, out)


def rows(w, k):
    return np.ascontiguousarray(np.moveaxis(w.reshape(w.shape[:-2] + (k, w.shape[-2] // k, w.shape[-1])), -3, -2))


def kernel(**inputs):
    import concourse.bacc as _bacc
    from concourse.bass_utils import run_bass_kernel_spmd as _run

    a = {k: np.asarray(v) for k, v in inputs.items()}
    l0, lf, l1, lg = "L0_attn_", "L0_ffn_", "L1_attn_", "L1_ffn_"

    def with_shared(name):
        return np.concatenate([a[lf + name], a[lf + "s" + name][None]])

    arrays = {
        "x": a[l0 + "hidden_states"],
        "cst": constants(),
        "w_dp": rows(np.concatenate([a[l0 + n] for n in ("Wq", "Wk", "Wv", "Wb")], 1), KD),
        "wo_d": rows(a[l0 + "Wo"], HG),
        "onw": np.ascontiguousarray(np.tile(a[l0 + "o_norm_weight"], HP)[:, None]),
        "w_r": rows(a[lf + "w_router"].T, KD),
        "w_gv": rows(np.concatenate([with_shared("wg"), with_shared("wv")], 2), KD),
        "w_e": rows(with_shared("wo"), 2),
        "w_at": rows(np.concatenate([a[l1 + n].T for n in ("Wq", "Wk", "Wv")], 1), KD),
        "wo_a": rows(a[l1 + "Wo"].T, HG),
        "w_gu": np.ascontiguousarray(np.stack([rows(a[lg + "w_gate"], KD), rows(a[lg + "w_up"], KD)], 2)),
        "w_down": rows(a[lg + "w_down"], FF // P),
    }
    nc = _bacc.Bacc("TRN2", target_bir_lowering=False, num_devices=1)
    args = [nc.dram_tensor(f"in_{k}", v.shape, mybir.dt.from_np(v.dtype), kind="ExternalInput").ap()
            for k, v in arrays.items()]
    out = nc.dram_tensor("out", (B, L, D), F32, kind="ExternalOutput").ap()
    build(nc, *args, out)
    r = _run(nc, [{f"in_{k}": v for k, v in arrays.items()}], core_ids=[0])
    return r.results[0]["out"]
```

```python
from contextlib import ExitStack

import concourse.bass as bass
import numpy as np
from concourse import mybir

F32 = mybir.dt.float32
BF16 = mybir.dt.bfloat16
I32 = mybir.dt.int32
U32 = mybir.dt.uint32
ALU = mybir.AluOpType
ACT = mybir.ActivationFunctionType
AX = mybir.AxisListType
ds = bass.ds

B, L, D = 4, 512, 256
T = B * L
P = 128
NT = T // P
TB = L // P
KD = D // P
H, DH = 16, 16
HG = H * DH // P
HP = P // DH
G = B * HG
C = 16
NC_ = L // C
CT = P // C
EPS = 1e-5
NE, TOPK, FE = 64, 6, 176
KF = -(-FE // P)
WX = KD * 2 * FE + KF * D
XT = 160
NW = 8
ST = NT
MT = XT + ST
FF = 1024
Q = 32
KVW = 2 * DH + 2

_C = {}
_off = 0
for _name, _w in (("ident", P), ("pair", 2), ("eye16", DH), ("mask_a", C), ("mask_m", C), ("mean_blk", P),
                  ("heads", HP), ("causal", P), ("tri", P), ("ones", P), ("iota_e", NE), ("iota_p", 2),
                  ("k128", 16), ("cos", TB * DH // 2), ("sin", TB * DH // 2)):
    _C[_name] = (_off, _off + _w)
    _off += _w
CW = _off


def constants():
    c = np.zeros((P, CW), np.float32)
    p = np.arange(P)

    def put(name, v):
        c[:, _C[name][0]:_C[name][1]] = v

    put("ident", np.eye(P))
    put("pair", p[:, None] // DH % 2 == np.arange(2)[None])
    put("eye16", p[:, None] % DH == np.arange(DH)[None])
    put("mask_a", -1.0 * (np.arange(C)[None] < p[:, None] % C))
    put("mask_m", np.arange(C)[None] >= p[:, None] % C)
    put("mean_blk", (p[:, None] // DH == p[None] // DH) / DH)
    put("heads", (p[:, None] // DH == np.arange(HP)[None]) * DH ** -0.5)
    put("causal", np.where(p[None] > p[:, None], -1e30, 0.0))
    put("tri", p[:, None] < p[None])
    put("ones", 1.0)
    put("iota_e", np.arange(NE)[None])
    put("iota_p", p[:, None] + P * np.arange(2)[None])
    put("k128", P * np.arange(16)[None])
    theta = np.float32(10000.0) ** (-2.0 * np.arange(DH // 2, dtype=np.float32) / DH)
    ang = (p[:, None, None] + P * np.arange(TB)[None, :, None]).astype(np.float32) * theta.astype(np.float32)
    put("cos", np.cos(ang).reshape(P, -1))
    put("sin", np.sin(ang).reshape(P, -1))
    return c


class State:

    def __init__(self, nc, ctx):
        self.nc = nc
        self.n = 0
        self.x = ctx.enter_context(nc.sbuf_tensor("x_res", [P, NT, D], F32))
        self.cst = ctx.enter_context(nc.sbuf_tensor("cst", [P, CW], F32))
        self.cb = ctx.enter_context(nc.sbuf_tensor("cst_bf16", [P, 4, P], BF16))
        self.mv = ctx.enter_context(nc.sbuf_tensor("mean_var", [P, NT, 2], F32))
        self.rstd = ctx.enter_context(nc.sbuf_tensor("rstd", [P, NT], F32))

    def c(self, name):
        return self.cst[:, _C[name][0]:_C[name][1]]


def opener(nc, ctx, phase):
    sems = []

    def give_back():
        nc.clear_and_free_semaphores(sems)
        nc.all_engine_barrier()

    ctx.callback(give_back)

    def sb(name, shape, dt=F32):
        return ctx.enter_context(nc.sbuf_tensor(f"{phase}_{name}", shape, dt))

    def ps(name, shape, dt=F32):
        return ctx.enter_context(nc.psum_tensor(f"{phase}_{name}", shape, dt))

    def sem(name):
        sems.append(nc.alloc_semaphore(f"{phase}_{name}"))
        return sems[-1]

    return sb, ps, sem


def pipeline(eng, count, unroll, *stages):
    behind = max(lag for lag, _ in stages)
    first = -(-behind // unroll) * unroll
    passes = (count - first) // unroll

    def step(k, base):
        for lag, stage in stages:
            if 0 <= k - lag < count:
                stage(base + (k - lag), (k - lag) % unroll)

    for k in range(first):
        step(k, 0)
    with eng.Fori(0, passes) as c:
        for k in range(first, first + unroll):
            step(k, unroll * c)
    for k in range(first + unroll * passes, count + behind):
        step(k, 0)


def phase_load(nc, st, x_in, cst_in):
    with ExitStack() as ctx:
        sb, ps, sem = opener(nc, ctx, "ld")
        x_in_sem, cst_sem, cast, stat, agg = sem("x"), sem("c"), sem("cast"), sem("stat"), sem("agg")
        stats = sb("stats", [P, NT, 6])
        block = ctx.enter_context(nc.Block())

        @block.sync
        def _(sp):
            for b in range(B):
                sp.dma_start(st.x[:, b * TB:(b + 1) * TB, :],
                             x_in[b].rearrange("(t p) d -> p t d", p=P)).then_inc(x_in_sem, 16)
            sp.wait_ge(x_in_sem, 16 * B)

        @block.scalar
        def _(act):
            act.dma_start(st.cst[:, :], cst_in).then_inc(cst_sem, 16)
            act.wait_ge(cst_sem, 16)
            for k, name in enumerate(("ident", "causal", "tri", "ones")):
                act.activation(st.cb[:, k, :], st.c(name), ACT.Copy).then_inc(cast, 1)

        @block.vector
        def _(dve):
            dve.wait_ge(x_in_sem, 16 * B)
            for t in range(NT):
                dve.bn_stats(stats[:, t, :], st.x[:, t, :]).then_inc(stat, 1)
            for t in range(NT):
                dve.wait_ge(stat, t + 1)
                dve.bn_aggr(st.mv[:, t, :], stats[:, t, :]).then_inc(agg, 1)


def finish_stats(nc, st, act, dve, eps_sem, root_sem, rstd_sem):
    if dve is not None:
        dve.tensor_scalar(st.rstd[:, :], st.mv[:, :, 1], EPS, None, ALU.add).then_inc(eps_sem, 1)
        dve.wait_ge(root_sem, 1)
        dve.reciprocal(st.rstd[:, :], st.rstd[:, :]).then_inc(rstd_sem, 1)
        dve.wait_ge(rstd_sem, 1)
    if act is not None:
        act.wait_ge(eps_sem, 1)
        act.activation(st.rstd[:, :], st.rstd[:, :], ACT.Sqrt).then_inc(root_sem, 1)


def phase_update(nc, st, y, tag):
    with ExitStack() as ctx:
        sb, ps, sem = opener(nc, ctx, tag)
        eps, root, rstd = sem("eps"), sem("root"), sem("rstd")
        yn, xs, stat, agg = sem("yn"), sem("x"), sem("stat"), sem("agg")
        stats = sb("stats", [P, NT, 6])
        mean = sb("mean", [P, NT, 1])
        block = ctx.enter_context(nc.Block())

        @block.scalar
        def _(act):
            finish_stats(nc, st, act, None, eps, root, rstd)

        @block.gpsimd
        def _(pool):
            for t in range(NT):
                pool.wait_ge(yn, t + 1)
                pool.tensor_tensor(st.x[:, t, :], st.x[:, t, :], y[:, t, :], ALU.add).then_inc(xs, 1)

        @block.vector
        def _(dve):
            finish_stats(nc, st, None, dve, eps, root, rstd)
            dve.tensor_copy(mean[:, :, 0], st.mv[:, :, 0]).then_inc(rstd, 1)
            dve.wait_ge(rstd, 2)
            for t in range(NT + 2):
                if t < NT:
                    dve.tensor_scalar(y[:, t, :], y[:, t, :], mean[:, t, :], st.rstd[:, t:t + 1],
                                      ALU.subtract, ALU.mult).then_inc(yn, 1)
                if t >= 2:
                    dve.wait_ge(xs, t - 1)
                    dve.bn_stats(stats[:, t - 2, :], st.x[:, t - 2, :]).then_inc(stat, 1)
            for t in range(NT):
                dve.wait_ge(stat, t + 1)
                dve.bn_aggr(st.mv[:, t, :], stats[:, t, :]).then_inc(agg, 1)
            dve.wait_ge(agg, NT)


def phase_delta_project(nc, st, w_in, qr, kvb, norms, wall, zeros):
    W = 3 * D + H
    VB = D + H
    with ExitStack() as ctx:
        sb, ps, sem = opener(nc, ctx, "dp")
        w_ld, eps, root, rstd = sem("w_ld"), sem("eps"), sem("root"), sem("rstd")
        xn_ok, xt_ps, xt_ok, proj = sem("xn"), sem("xt_ps"), sem("xt"), sem("proj")
        sq_ok, tanh_ok, q_out, k_out, v_out, b_out, ss_ok, pad_ok = (
            sem(n) for n in ("sq", "tanh", "q_out", "k_out", "v_out", "b_out", "ss", "pad"))
        xn = sb("xn", [P, 2, D])
        xt = sb("xt", [P, 2, KD, P])
        sq = sb("sq", [P, 2, 2 * D])
        th = sb("th", [P, 2, H])
        p_t = [ps(f"p_t{i}", [P, 4, P]) for i in range(2)]
        p_qk = [ps(f"p_qk{i}", [P, 2 * D]) for i in range(2)]
        p_vb = [ps(f"p_vb{i}", [P, 512]) for i in range(2)]
        block = ctx.enter_context(nc.Block())

        @block.sync
        def _(sp):
            sp.dma_start(wall[:, :, :], w_in).then_inc(w_ld, 16)
            sp.wait_ge(w_ld, 16)

        @block.vector
        def _(dve):
            dve.memset(kvb[:, :, :, KVW - 1:KVW], 0.0).then_inc(pad_ok, 1)
            dve.memset(zeros[:, :], 0.0).then_inc(pad_ok, 1)
            finish_stats(nc, st, None, dve, eps, root, rstd)

            def normalise(n, k):
                dve.wait_ge(xt_ps, n + 1)
                dve.tensor_scalar(xn[:, k % 2, :], st.x[:, ds(n, 1), :], st.mv[:, ds(n, 1), 0],
                                  st.rstd[:, ds(n, 1)], ALU.subtract, ALU.mult).then_inc(xn_ok, 1)

            def finish(n, k):
                dve.wait_ge(sq_ok, n + 1)
                dve.tensor_reduce(norms[:, ds(n, 1), :], sq[:, k % 2, :].rearrange("p (h d) -> p h d", d=DH),
                                  AX.X, ALU.add).then_inc(ss_ok, 1)
                dve.wait_ge(tanh_ok, n + 3)
                dve.tensor_scalar(kvb[:, ds(n, 1), :, 2 * DH], th[:, k % 2, :], 0.5, 0.5,
                                  ALU.mult, ALU.add).then_inc(b_out, 1)

            pipeline(dve, NT, 2, (0, normalise), (2, finish))

        @block.tensor
        def _(pe):
            pe.sem_inc(xt_ps, 2)
            pe.wait_ge(w_ld, 16)

            def transposes(n, k):
                pe.wait_ge(xn_ok, n + 1)
                pe.wait_ge(xt_ok, n + 1)
                for c in range(KD):
                    last = pe.transpose(p_t[k % 2][:, c, :], xn[:, k % 2, c * P:(c + 1) * P], st.c("ident"))
                last.then_inc(xt_ps, 1)

            def project(n, k):
                pe.wait_ge(xt_ok, n + 3)
                pe.wait_ge(k_out, n + 1)
                pe.wait_ge(tanh_ok, n + 1)
                for c in range(KD):
                    pe.matmul(p_qk[k % 2][:, :], xt[:, k % 2, c, :], wall[:, c, 0:2 * D], start=c == 0, stop=c == KD - 1)
                for c in range(KD):
                    last = pe.matmul(p_vb[k % 2][:, 0:VB], xt[:, k % 2, c, :], wall[:, c, 2 * D:W],
                                     start=c == 0, stop=c == KD - 1)
                last.then_inc(proj, 1)

            pipeline(pe, NT, 2, (0, transposes), (1, project))

        @block.scalar
        def _(act):
            finish_stats(nc, st, act, None, eps, root, rstd)
            for s in (xt_ok, k_out, ss_ok, b_out, tanh_ok, proj):
                act.sem_inc(s, 2)

            def take_xt(n, k):
                act.wait_ge(xt_ps, n + 3)
                act.wait_ge(proj, n + 1)
                act.activation(xt[:, k % 2], p_t[k % 2][:, 0:KD, :], ACT.Copy).then_inc(xt_ok, 1)

            def take(n, k):
                act.wait_ge(proj, n + 3)
                act.activation(kvb[:, ds(n, 1), :, DH:2 * DH],
                               p_vb[k % 2][:, 0:D].rearrange("p (h d) -> p h d", d=DH), ACT.Silu).then_inc(v_out, 1)
                act.wait_ge(b_out, n + 1)
                act.activation(th[:, k % 2, :], p_vb[k % 2][:, D:VB], ACT.Tanh, scale=0.5).then_inc(tanh_ok, 1)
                act.wait_ge(ss_ok, n + 1)
                act.activation(sq[:, k % 2, :], p_qk[k % 2][:, :], ACT.Square).then_inc(sq_ok, 1)
                act.activation(qr[:, ds(n, 1), :], p_qk[k % 2][:, 0:D], ACT.Copy).then_inc(q_out, 1)
                act.activation(kvb[:, ds(n, 1), :, 0:DH],
                               p_qk[k % 2][:, D:2 * D].rearrange("p (h d) -> p h d", d=DH), ACT.Copy).then_inc(k_out, 1)

            pipeline(act, NT, 2, (0, take_xt), (1, take))


def phase_delta_layout(nc, st, qr, kvb, norms, kqt, kvb_dram):
    with ExitStack() as ctx:
        sb, ps, sem = opener(nc, ctx, "dl")
        lim, root, rec, scal = sem("lim"), sem("root"), sem("rec"), sem("scal")
        n_ok, t_ps, k_back, st_d = (sem(n) for n in ("n", "t_ps", "k_back", "st"))
        taken = [sem("taken_act"), sem("taken_dve")]
        kq = sb("kq", [P, 2, 2, D])
        p_t = [[ps(f"p_t{i}{hg}", [P, 4, P]) for hg in range(HG)] for i in range(2)]
        flat = norms[:, :, :].rearrange("p t h -> p (t h)")
        block = ctx.enter_context(nc.Block())

        def take(eng, tb, b, hg):
            n, u = tb * B + b, b % 2
            eng.wait_ge(t_ps, n + 3)
            dst = kqt[:, ds(tb * CT, CT), b * HG + hg, :, :].rearrange("p c s i -> p s c i")
            src = p_t[u][hg][:, 0:2, :].rearrange("p s (c i) -> p s c i", i=C)
            for s in range(2):
                if hg == 0:
                    i = eng.activation(dst[:, s], src[:, s], ACT.Copy)
                else:
                    i = eng.tensor_copy(dst[:, s], src[:, s])
                i.then_inc(taken[hg], 1)

        @block.vector
        def _(dve):
            dve.tensor_scalar(flat, flat, 1e-24, None, ALU.max).then_inc(lim, 1)
            dve.wait_ge(root, 1)
            dve.reciprocal(flat, flat).then_inc(rec, 1)
            dve.wait_ge(rec, 1)
            dve.tensor_scalar(norms[:, :, 0:H], norms[:, :, 0:H], DH ** -0.5, None, ALU.mult).then_inc(scal, 1)
            dve.wait_ge(scal, 1)
            with dve.Fori(0, TB) as tb:
                for b in range(B):
                    n, u, t = tb * B + b, b % 2, tb + b * TB
                    dve.wait_ge(t_ps, n + 1)
                    dve.wait_ge(k_back, n + 1)
                    dve.tensor_tensor(kq[:, u, 0, :].rearrange("p (h d) -> p h d", d=DH),
                                      kvb[:, ds(t, 1), :, 0:DH],
                                      norms[:, ds(t, 1), H:2 * H].rearrange("p o h -> p (o h)").unsqueeze(2)
                                      .to_broadcast([P, H, DH]), ALU.mult).then_inc(n_ok, 1)
                    dve.tensor_tensor(kq[:, u, 1, :].rearrange("p (h d) -> p h d", d=DH),
                                      qr[:, ds(t, 1), :].rearrange("p o (h d) -> p (o h) d", d=DH),
                                      norms[:, ds(t, 1), 0:H].rearrange("p o h -> p (o h)").unsqueeze(2)
                                      .to_broadcast([P, H, DH]), ALU.mult).then_inc(n_ok, 1)
                    if b % 2:
                        for m in (b - 1, b):
                            take(dve, tb, m, 1)

        @block.tensor
        def _(pe):
            pe.sem_inc(t_ps, 2)
            with pe.Fori(0, TB) as tb:
                for b in range(B):
                    n, u = tb * B + b, b % 2
                    pe.wait_ge(n_ok, 2 * n + 2)
                    for s in taken:
                        pe.wait_ge(s, 2 * n + 1)
                    for s in range(2):
                        for hg in range(HG):
                            last = pe.transpose(p_t[u][hg][:, s, :], kq[:, u, s, hg * P:(hg + 1) * P], st.c("ident"))
                    last.then_inc(t_ps, 1)

        @block.scalar
        def _(act):
            act.sem_inc(taken[0], 3)
            act.sem_inc(taken[1], 3)
            act.wait_ge(lim, 1)
            act.activation(flat, flat, ACT.Sqrt).then_inc(root, 1)
            with act.Fori(0, TB) as tb:
                for b in range(B):
                    take(act, tb, b, 0)

        @block.gpsimd
        def _(pool):
            pool.sem_inc(k_back, 2)
            with pool.Fori(0, TB) as tb:
                for b in range(B):
                    n, u, t = tb * B + b, b % 2, tb + b * TB
                    pool.wait_ge(n_ok, 2 * n + 1)
                    pool.tensor_copy(kvb[:, ds(t, 1), :, 0:DH],
                                     kq[:, u, 0, :].rearrange("p (h d) -> p h d", d=DH)).then_inc(k_back, 1)

        @block.sync
        def _(sp):
            for tb in range(TB):
                sp.wait_ge(k_back, tb * B + B + 2)
                sp.dma_start(kvb_dram.rearrange("(b t p) h w -> p b t (h w)", b=B, p=P)[:, :, tb, :],
                             kvb[:, :, :, :].rearrange("p (b t) h w -> p b t (h w)", b=B)[:, :, tb, :]
                             ).then_inc(st_d, 16)
            sp.wait_ge(st_d, 16 * TB)


def tiles():
    for s in range(G):
        for q in range(P // Q):
            yield (2 * q + s) % G, slice(q * Q, (q + 1) * Q)


def expand(st, eng, dst, src, done):
    shape = [P, src.shape[1], 2, C]
    eng.tensor_tensor(dst, src.unsqueeze(2).to_broadcast(shape),
                      st.c("pair").unsqueeze(1).unsqueeze(3).to_broadcast(shape), ALU.mult).then_inc(done, 1)


def phase_delta_scores(nc, st, kqt, kvb_dram, mkv, att):
    with ExitStack() as ctx:
        sb, ps, sem = opener(nc, ctx, "ds")
        begun, ld_d, kbd_ok, kq_ok, s_ps, a_out, m_out, scaled = (
            sem(n) for n in ("begun", "ld", "kbd", "kq", "s_ps", "a_out", "m_out", "scaled"))
        kq = sb("kq", [P, 2, G, 2, C])
        kbd = sb("kbd", [P, 2, G, 2, C])
        p_s = [ps(f"p_s{i}", [P, G, 256]) for i in range(2)]
        att_c = att[:, :, :].rearrange("p j (c g) -> p g j c", g=G)
        block = ctx.enter_context(nc.Block())

        @block.sync
        def _(sp):
            rows = kvb_dram.rearrange("(b c j) (g h) w -> h j c b g w", b=B, j=C, g=HG)
            for h in range(HP):
                for b in range(B):
                    for hg in range(HG):
                        sp.dma_start(mkv[h * C:(h + 1) * C, :, b * HG + hg, C:C + KVW],
                                     rows[h, :, :, b, hg, :]).then_inc(ld_d, 16)
            sp.wait_ge(ld_d, 16 * HP * G)

        @block.scalar
        def _(act):
            def copy_kq(n, u):
                act.wait_ge(s_ps, n + 1)
                act.activation(kq[:, u], kqt[:, ds(n, 1), :, :, :].rearrange("p o g s i -> p (o g) s i"),
                               ACT.Copy).then_inc(kq_ok, 1)

            pipeline(act, NC_, 2, (0, copy_kq))

        @block.vector
        def _(dve):
            def expand_k(n, u):
                dve.wait_ge(s_ps, n + 1)
                expand(st, dve, kbd[:, u], kqt[:, ds(n, 1), :, 0, :].rearrange("p o g d -> p (o g) d"), kbd_ok)

            def take(n, u):
                dve.wait_ge(s_ps, n + 3)
                dve.tensor_tensor(att_c[:, :, :, ds(n, 1)].rearrange("p g j o -> p g (j o)"), p_s[u][:, :, 0:C],
                                  st.c("mask_a").unsqueeze(1).to_broadcast([P, G, C]), ALU.mult).then_inc(a_out, 1)
                dve.tensor_tensor(mkv[:, ds(n, 1), :, 0:C].rearrange("p o g i -> p (o g) i"), p_s[u][:, :, C:2 * C],
                                  st.c("mask_m").unsqueeze(1).to_broadcast([P, G, C]), ALU.mult).then_inc(m_out, 1)

            pipeline(dve, NC_, 2, (0, expand_k), (1, take))
            dve.wait_ge(a_out, NC_)
            dve.wait_ge(ld_d, 16 * HP * G)
            dve.tensor_tensor(att[:, :, :].rearrange("p j (c g) -> p j c g", g=G),
                              att[:, :, :].rearrange("p j (c g) -> p j c g", g=G),
                              mkv[:, :, :, C + 2 * DH].unsqueeze(1).to_broadcast([P, C, NC_, G]),
                              ALU.mult).then_inc(scaled, 1)

        @block.tensor
        def _(pe):
            pe.sem_inc(s_ps, 2)
            pe.sem_inc(m_out, 2)

            def scores(n, u):
                pe.wait_ge(kbd_ok, n + 1)
                pe.wait_ge(kq_ok, n + 1)
                pe.wait_ge(m_out, n + 1)
                pe.sem_inc(begun, 1)
                for g, q in tiles():
                    last = pe.matmul(p_s[u][q, g, 0:2 * C], kbd[q, u, g, :, :], kq[q, u, g, :, :],
                                     start=True, stop=True)
                last.then_inc(s_ps, 1)

            pipeline(pe, NC_, 2, (0, scores))


def phase_delta_invert(nc, st, mkv, att, zeros, xs_dram, zero_sem, n_zero):
    JB = 4
    NB = C // JB
    HC = 2 * HP
    with ExitStack() as ctx:
        sb, ps, sem = opener(nc, ctx, "di")
        t_ps, out_a, out_v, one, back, b_out = (sem(n) for n in ("t_ps", "out_a", "out_v", "one", "back", "b_out"))
        products, rows, zero = sem("products"), sem("rows"), sem("zero")
        au = sb("au", [P, HC, C, C])
        tt = sb("tt", [P, C, HC, C])
        prod = sb("prod", [P, HC, C - 1, C - 1])
        bank = [ps(f"bank{i}", [P, JB, P]) for i in range(2 * NB)]
        block = ctx.enter_context(nc.Block())

        @block.sync
        def _(sp):
            slots = xs_dram[0:XT * P, :].rearrange("(p r) d -> p (r d)", p=P)
            w = zeros.shape[1]
            for i in range(n_zero):
                sp.dma_start(slots[:, i * w:(i + 1) * w], zeros[:, :]).then_inc(zero_sem, 16)

        @block.tensor
        def _(pe):
            for half in range(2):
                for jb in range(NB):
                    for j in range(JB):
                        last = pe.transpose(bank[half * NB + jb][:, j, :],
                                            att[:, jb * JB + j, half * P:(half + 1) * P], st.c("ident"))
                    last.then_inc(t_ps, 1)
            pe.wait_ge(rows, C - 1)
            pe.wait_ge(one, C)
            for half in range(2):
                pe.wait_ge(out_a, (half + 1) * NB // 2)
                pe.wait_ge(out_v, (half + 1) * NB // 2)
                for ib in range(NB):
                    for i in range(JB):
                        last = pe.transpose(bank[half * NB + ib][:, i, :],
                                            tt[:, ib * JB + i, half * HP:(half + 1) * HP, :], st.c("ident"))
                    last.then_inc(back, 1)

        def spread(eng, n, done):
            half, jb = n // NB, n % NB
            eng.wait_ge(t_ps, n + 1)
            dst = au[:, half * HP:(half + 1) * HP, :, jb * JB:(jb + 1) * JB].rearrange("p h i j -> p j (h i)")
            i = eng.activation(dst, bank[n][:, :, :], ACT.Copy) if done is out_a else eng.tensor_copy(
                dst, bank[n][:, :, :])
            i.then_inc(done, 1)

        @block.scalar
        def _(act):
            for n in range(0, 2 * NB, 2):
                spread(act, n, out_a)

        @block.gpsimd
        def _(pool):
            pool.memset(tt[:, :, :, :], 0.0).then_inc(zero, 1)
            pool.wait_ge(zero, 1)
            for i in range(C):
                pool.memset(tt[:, i, :, i], 1.0).then_inc(one, 1)

        @block.vector
        def _(dve):
            for n in range(1, 2 * NB, 2):
                spread(dve, n, out_v)
            dve.wait_ge(out_a, NB)
            dve.wait_ge(out_v, NB)
            dve.wait_ge(one, C)
            for i in range(1, C):
                terms = prod[:, :, 0:i, 0:i]
                if i > 1:
                    dve.wait_ge(rows, i - 1)
                dve.tensor_tensor(terms, au[:, :, i, 0:i].unsqueeze(2).to_broadcast([P, HC, i, i]),
                                  tt[:, 0:i, :, 0:i].rearrange("p m h j -> p h j m"), ALU.mult).then_inc(products, 1)
                dve.wait_ge(products, i)
                dve.tensor_reduce(tt[:, i, :, 0:i], terms, AX.X, ALU.add).then_inc(rows, 1)
            for n in range(2 * NB):
                half, ib = n // NB, n % NB
                dve.wait_ge(back, n + 1)
                beta = mkv[:, :, :, C + 2 * DH].rearrange("p c g -> p (c g)")[:, half * P:(half + 1) * P]
                dve.tensor_tensor(att[:, ib * JB:(ib + 1) * JB, half * P:(half + 1) * P], bank[n][:, :, :],
                                  beta.unsqueeze(1).to_broadcast([P, JB, P]), ALU.mult).then_inc(b_out, 1)


def phase_delta_wy(nc, st, kqt, mkv, att, xt):
    with ExitStack() as ctx:
        sb, ps, sem = opener(nc, ctx, "dw")
        begun, tb_ok, mk_ok, w_ps, w_out, wv_out, wk_ok, x_ps, q_out, i_out = (
            sem(n) for n in ("begun", "tb", "mk", "w_ps", "w_out", "wv_out", "wk", "x_ps", "q_out", "i_out"))
        mk = sb("mk", [P, 4, G, C + 2 * DH])
        tbd = sb("tbd", [P, 2, G, 2, C])
        wkd = sb("wkd", [P, 2, G, 2, C])
        wc = sb("wc", [P, 2, G, DH])
        p_w, p_x = (ps(n, [P, G, 256]) for n in ("p_w", "p_x"))
        att_c = att[:, :, :].rearrange("p j (c g) -> p g j c", g=G)

        block = ctx.enter_context(nc.Block())

        @block.gpsimd
        def _(pool):
            def expand_t(n, u):
                pool.wait_ge(w_ps, n + 1)
                expand(st, pool, tbd[:, u], att_c[:, :, :, ds(n, 1)].rearrange("p g j o -> p g (j o)"), tb_ok)

            pipeline(pool, NC_, 2, (0, expand_t))

        @block.scalar
        def _(act):
            act.sem_inc(wk_ok, 2)
            act.sem_inc(wv_out, 1)

            def copy_mk(n, u):
                act.wait_ge(x_ps, n + 1)
                act.activation(mk[:, u], mkv[:, ds(n, 1), :, 0:C + 2 * DH].rearrange("p o g w -> p (o g) w"),
                               ACT.Copy).then_inc(mk_ok, 1)

            def take_w(n, u):
                act.wait_ge(w_ps, n + 3)
                act.wait_ge(wk_ok, n + 1)
                act.activation(wc[:, u % 2], p_w[:, :, 0:DH], ACT.Copy).then_inc(w_out, 1)
                act.activation(mkv[:, ds(n, 1), :, C + DH:C + 2 * DH].rearrange("p o g v -> p (o g) v"),
                               p_w[:, :, DH:2 * DH], ACT.Copy).then_inc(wv_out, 1)

            pipeline(act, NC_, 4, (0, copy_mk), (1, take_w))

        @block.vector
        def _(dve):
            dve.sem_inc(x_ps, 4)

            def expand_w(n, u):
                dve.wait_ge(w_out, n + 1)
                dve.wait_ge(x_ps, n + 3)
                expand(st, dve, wkd[:, u % 2], wc[:, u % 2], wk_ok)

            def take_x(n, u):
                dve.wait_ge(x_ps, n + 5)
                dst = xt[:, ds(n, 1), :, :, :].rearrange("p o g s i -> p (o g) s i")
                dve.tensor_tensor(dst[:, :, 0, :], kqt[:, ds(n, 1), :, 1, :].rearrange("p o g i -> p (o g) i"),
                                  p_x[:, :, 0:C], ALU.subtract).then_inc(q_out, 1)
                dve.tensor_tensor(dst[:, :, 1, :], st.c("eye16").unsqueeze(1).to_broadcast([P, G, DH]),
                                  p_x[:, :, C:2 * C], ALU.subtract).then_inc(i_out, 1)

            pipeline(dve, NC_, 4, (1, expand_w), (2, take_x))

        @block.tensor
        def _(pe):
            pe.sem_inc(w_ps, 2)
            pe.sem_inc(i_out, 1)

            def w_part(n, u):
                pe.wait_ge(tb_ok, n + 1)
                pe.wait_ge(mk_ok, n + 1)
                pe.wait_ge(wv_out, n + 1)
                pe.sem_inc(begun, 1)
                for g, q in tiles():
                    last = pe.matmul(p_w[q, g, 0:2 * DH], tbd[q, u % 2, g, :, :], mk[q, u, g, C:C + 2 * DH],
                                     start=True, stop=True)
                last.then_inc(w_ps, 1)

            def x_part(n, u):
                pe.wait_ge(wk_ok, n + 3)
                pe.wait_ge(i_out, n + 1)
                pe.sem_inc(begun, 1)
                for g, q in tiles():
                    last = pe.matmul(p_x[q, g, 0:C + DH], wkd[q, u % 2, g, :, :], mk[q, u, g, 0:C + DH],
                                     start=True, stop=True)
                last.then_inc(x_ps, 1)

            pipeline(pe, NC_, 4, (0, w_part), (1, x_part))


def phase_delta_chain(nc, st, mkv, xt, ot):
    N = 2 * DH + C
    with ExitStack() as ctx:
        sb, ps, sem = opener(nc, ctx, "dc")
        km_ok, xx_ok, wv_ok, s_ok, r_ps, o_out = (sem(n) for n in ("km", "xx", "wv", "s", "r_ps", "o_out"))
        km_k, xx_p, begun = sem("km_k"), sem("xx_p"), sem("begun")
        km = sb("km", [P, 2, G, N])
        xx = sb("xx", [P, 2, G, N])
        wvd = sb("wvd", [P, 2, G, 2, DH])
        s = sb("s", [P, 2, G, 2 * DH])
        p_r = [ps(f"p_r{i}", [P, G, 256]) for i in range(2)]

        def pair(t):
            return t[:, :, 0:2 * DH].rearrange("p g (s i) -> p g s i", s=2)

        def part(t, n, lo):
            return t[:, ds(n, 1), :, lo:lo + C].rearrange("p o g i -> p (o g) i")

        def xt_part(n, k):
            return xt[:, ds(n, 1), :, k, :].rearrange("p o g i -> p (o g) i")

        block = ctx.enter_context(nc.Block())

        @block.gpsimd
        def _(pool):
            with pool.Fori(0, NC_ // 2) as cc:
                for u in range(2):
                    n = 2 * cc + u
                    pool.wait_ge(r_ps, n + 1)
                    expand(st, pool, pair(km[:, u]), part(mkv, n, C), km_k)
                    expand(st, pool, wvd[:, u], part(mkv, n, C + DH), wv_ok)

        def ahead(eng, prepare, finish):
            prepare(0, 0)
            with eng.Fori(0, NC_ // 2 - 1) as cc:
                for u in range(2):
                    prepare(2 * cc + u + 1, 1 - u)
                    finish(2 * cc + u, u)
            prepare(NC_ - 1, 1)
            finish(NC_ - 2, 0)
            finish(NC_ - 1, 1)

        @block.vector
        def _(dve):
            def prepare(n, u):
                dve.wait_ge(r_ps, n + 1)
                expand(st, dve, pair(xx[:, u]), xt_part(n, 1), xx_p)

            def turn(n, u):
                dve.wait_ge(r_ps, n + 3)
                dve.transpose(s[:, 1 - u], p_r[u][:, :, 0:2 * DH]).then_inc(s_ok, 1)

            dve.memset(s[:, 0], 0.0).then_inc(s_ok, 1)
            ahead(dve, prepare, turn)

        @block.scalar
        def _(act):
            def prepare(n, u):
                act.wait_ge(r_ps, n + 1)
                act.activation(km[:, u, :, 2 * DH:N], part(mkv, n, 0), ACT.Copy).then_inc(km_ok, 1)
                act.activation(xx[:, u, :, 2 * DH:N], xt_part(n, 0), ACT.Copy).then_inc(xx_ok, 1)

            def take(n, u):
                act.wait_ge(s_ok, n + 2)
                act.activation(ot[:, :, :, ds(n * C, C)].rearrange("p g b i -> p b g i"),
                               p_r[u][:, :, 2 * DH:N].rearrange("p (b g) i -> p b g i", g=HG),
                               ACT.Copy).then_inc(o_out, 1)

            ahead(act, prepare, take)

        @block.tensor
        def _(pe):
            pe.sem_inc(r_ps, 2)
            pe.sem_inc(o_out, 2)

            with pe.Fori(0, NC_ // 2) as cc:
                for u in range(2):
                    n = 2 * cc + u
                    for done in (km_k, wv_ok, km_ok):
                        pe.wait_ge(done, n + 1)
                    pe.wait_ge(o_out, n + 1)
                    pe.sem_inc(begun, 1)
                    for g, q in tiles():
                        pe.matmul(p_r[u][q, g, 0:N], wvd[q, u, g, :, :], km[q, u, g, :], start=g % 2 == 0, stop=False)
                    pe.wait_ge(xx_p, n + 1)
                    pe.wait_ge(xx_ok, n + 1)
                    pe.wait_ge(s_ok, n + 1)
                    pe.sem_inc(begun, 1)
                    for g, q in tiles():
                        last = pe.matmul(p_r[u][q, g, 0:N], s[q, u, g, :], xx[q, u, g, :], start=False, stop=g % 2 == 1)
                    last.then_inc(r_ps, 1)


def phase_delta_out(nc, st, ot, wo_in, onw_in, y):
    with ExitStack() as ctx:
        sb, ps, sem = opener(nc, ctx, "do")
        w_ld, sq_ok, ms_ps, eps_ok, root, rec, on_ok, y_ps, y_ok, stat, agg = (
            sem(n) for n in ("w_ld", "sq", "ms_ps", "eps", "root", "rec", "on", "y_ps", "y", "stat", "agg"))
        wo = sb("wo", [P, HG, D])
        onw = sb("onw", [P, 1])
        eps = sb("eps", [P, 1])
        sq = sb("sq", [P, 2, HG, L])
        r = sb("r", [P, 2, HG, L])
        on = sb("on", [P, 2, HG, L])
        stats = sb("stats", [P, NT, 6])
        p_ms = [ps(f"p_ms{g}", [P, L]) for g in range(HG)]
        p_y = [ps(f"p_y{t}", [P, 512]) for t in range(TB)]
        block = ctx.enter_context(nc.Block())

        def outputs(b, g):
            return ot[:, g, ds(b, 1), :].rearrange("p o l -> p (o l)")

        def result(n):
            return y[:, ds(n, 1), :].rearrange("p o d -> p (o d)")

        @block.sync
        def _(sp):
            sp.dma_start(wo[:, :, :], wo_in).then_inc(w_ld, 16)
            sp.dma_start(onw[:, :], onw_in).then_inc(w_ld, 16)
            sp.wait_ge(w_ld, 32)

        @block.scalar
        def _(act):
            act.sem_inc(root, HG)
            act.wait_ge(eps_ok, 1)

            def square(b, u):
                for g in range(HG):
                    act.wait_ge(ms_ps, HG * b + g + 1)
                    act.activation(sq[:, u, g, :], outputs(b, g), ACT.Square).then_inc(sq_ok, 1)

            def take_root(b, u):
                for g in range(HG):
                    act.wait_ge(ms_ps, HG * b + g + 2 * HG + 1)
                    act.wait_ge(on_ok, HG * b + g + 1)
                    act.activation(r[:, u, g, :], p_ms[g][:, :], ACT.Sqrt, bias=eps[:, :]).then_inc(root, 1)

            def take_y(b, u):
                for t in range(TB):
                    act.wait_ge(y_ps, TB * b + 2 * TB + t + 1)
                    act.activation(result(TB * b + t), p_y[t][:, 0:D], ACT.Copy).then_inc(y_ok, 1)

            pipeline(act, B, 2, (0, square), (0, take_root), (1, take_y))

        @block.vector
        def _(dve):
            dve.sem_inc(on_ok, 2 * HG)
            dve.memset(eps[:, :], EPS).then_inc(eps_ok, 1)
            dve.wait_ge(w_ld, 32)

            def normalise(b, u):
                for g in range(HG):
                    dve.wait_ge(root, HG * b + g + HG + 1)
                    dve.reciprocal(r[:, u, g, :], r[:, u, g, :]).then_inc(rec, 1)
                for g in range(HG):
                    dve.wait_ge(rec, HG * b + g + 1)
                    dve.wait_ge(y_ps, TB * b + TB)
                    dve.scalar_tensor_tensor(on[:, u, g, :], outputs(b, g), onw[:, 0:1], r[:, u, g, :],
                                             ALU.mult, ALU.mult).then_inc(on_ok, 1)

            def take_stats(b, u):
                for t in range(TB):
                    dve.wait_ge(y_ok, TB * b + TB + t + 1)
                    dve.bn_stats(stats[:, ds(TB * b + t, 1), :].rearrange("p o s -> p (o s)"),
                                 result(TB * b + t)).then_inc(stat, 1)

            pipeline(dve, B, 2, (0, normalise), (1, take_stats))
            dve.wait_ge(stat, NT)
            for n in range(NT):
                dve.bn_aggr(st.mv[:, n, :], stats[:, n, :]).then_inc(agg, 1)

        @block.tensor
        def _(pe):
            pe.sem_inc(ms_ps, 2 * HG)
            pe.sem_inc(y_ps, 2 * TB)
            pe.sem_inc(y_ok, TB)
            pe.wait_ge(w_ld, 32)

            def mean_squares(b, u):
                for g in range(HG):
                    pe.wait_ge(sq_ok, HG * b + g + 1)
                    pe.wait_ge(root, HG * b + g + 1)
                    pe.matmul(p_ms[g][:, :], st.c("mean_blk"), sq[:, u, g, :], start=True, stop=True).then_inc(ms_ps, 1)

            def project(b, u):
                pe.wait_ge(on_ok, HG * b + 3 * HG)
                for t in range(TB):
                    pe.wait_ge(y_ok, TB * b + t + 1)
                    for g in range(HG):
                        last = pe.matmul(p_y[t][:, 0:D], on[:, u, g, t * P:(t + 1) * P], wo[:, g, :],
                                         start=g == 0, stop=g == HG - 1)
                    last.then_inc(y_ps, 1)

            pipeline(pe, B, 2, (0, mean_squares), (1, project))


class Routing:

    def __init__(self, nc, ctx):
        def sb(name, shape, dt=F32):
            return ctx.enter_context(nc.sbuf_tensor(f"rt_{name}", shape, dt))

        self.top = sb("top", [P, NT, 8])
        self.hot = sb("hot", [P, NT, TOPK, NE], BF16)
        self.sel = sb("sel", [P, NT, NE], BF16)
        self.cum = sb("cum", [P, NT + 1, NE], BF16)
        self.pos = sb("pos", [P, NT, 8], U32)
        self.erow = sb("erow", [1, MT], I32)
        self.new = sb("new", [1, MT], I32)
        self.slot = sb("slot", [1, MT], I32)


def phase_route(nc, st, rt, wr_in, xna):
    with ExitStack() as ctx:
        sb, ps, sem = opener(nc, ctx, "ro")
        w_ld, eps, root, rstd = sem("w_ld"), sem("eps"), sem("root"), sem("rstd")
        xn_ok, xs_ok, xt_ps, xt_ok, l_ps, mx_ok, e_ok, rec, sc_ok, begun, top_ok, kept, idx_ok, idf_ok, hot_ok, sel_ok, cum_ok = (
            sem(n) for n in ("xn", "xs", "xt_ps", "xt", "l_ps", "mx", "e", "rec", "sc", "begun", "top", "kept", "idx", "idf", "hot",
                             "sel", "cum"))
        wr = sb("wr", [P, KD, NE])
        xn = sb("xn", [P, 2, D])
        xt = sb("xt", [P, 2, KD, P])
        nm = sb("nm", [P, 2, 1])
        e = sb("e", [P, 2, NE])
        se = sb("se", [P, 2, 1])
        sc = sb("sc", [P, 2, NE])
        top = sb("top", [P, 2, 8])
        idx = sb("idx", [P, 2, 8], U32)
        idf = sb("idf", [P, 2, 8])
        p_t = [ps(f"p_t{i}", [P, 4, P]) for i in range(2)]
        p_l = [ps(f"p_l{i}", [P, 512]) for i in range(2)]
        block = ctx.enter_context(nc.Block())

        def tile(t, ap):
            return ap[:, ds(t, 1)]

        @block.sync
        def _(sp):
            sp.dma_start(wr[:, :, :], wr_in).then_inc(w_ld, 16)
            sp.wait_ge(w_ld, 16)

        @block.vector
        def _(dve):
            dve.sem_inc(mx_ok, 2)
            dve.sem_inc(sc_ok, 2)
            dve.sem_inc(xt_ps, 2)
            finish_stats(nc, st, None, dve, eps, root, rstd)
            dve.memset(rt.cum[:, 0, :], 0.0).then_inc(cum_ok, 1)
            with dve.Fori(0, NT // 4) as q:
                for k in range(4):
                    n, u = 4 * q + k, k % 2
                    dve.wait_ge(xt_ps, n + 1)
                    dve.wait_ge(xs_ok, n + 1)
                    dve.tensor_scalar(xn[:, u, :], tile(n, st.x), st.mv[:, ds(n, 1), 0], st.rstd[:, ds(n, 1)],
                                      ALU.subtract, ALU.mult).then_inc(xn_ok, 1)
                for k in range(4):
                    n, u = 4 * q + k, k % 2
                    dve.wait_ge(l_ps, n + 1)
                    dve.wait_ge(e_ok, n + 1)
                    dve.tensor_reduce(nm[:, u, :], p_l[u][:, 0:NE], AX.X, ALU.max, negate=True).then_inc(mx_ok, 1)
                    dve.wait_ge(e_ok, n + 3)
                    dve.reciprocal(se[:, u, :], se[:, u, :]).then_inc(rec, 1)
                    dve.wait_ge(rec, n + 1)
                    dve.tensor_scalar(sc[:, u, :], e[:, u, :], se[:, u, :], None, ALU.mult).then_inc(sc_ok, 1)
                    dve.wait_ge(sc_ok, n + 3)
                    dve.sem_inc(begun, 1)
                    dve.max(top[:, u, :], sc[:, u, :]).then_inc(top_ok, 1)
                    dve.wait_ge(top_ok, n + 1)
                    dve.tensor_scalar(tile(n, rt.top).rearrange("p o k -> p (o k)"), top[:, u, :], 1.0, None,
                                      ALU.mult).then_inc(kept, 1)
                    dve.max_index(idx[:, u, :], top[:, u, :], sc[:, u, :]).then_inc(idx_ok, 1)
                    dve.wait_ge(idx_ok, n + 1)
                    dve.tensor_copy(idf[:, u, :], idx[:, u, :]).then_inc(idf_ok, 1)
                    dve.wait_ge(idf_ok, n + 1)
                    hot = tile(n, rt.hot).rearrange("p o k e -> p (o k) e")
                    dve.tensor_tensor(hot, idf[:, u, 0:TOPK].unsqueeze(2).to_broadcast([P, TOPK, NE]),
                                      st.c("iota_e").unsqueeze(1).to_broadcast([P, TOPK, NE]),
                                      ALU.is_equal).then_inc(hot_ok, 1)
                    dve.wait_ge(hot_ok, n + 1)
                    with nc.allow_low_precision("zeros and ones"):
                        dve.tensor_reduce(tile(n, rt.sel).rearrange("p o e -> p (o e)"),
                                          hot.rearrange("p k e -> p e k"), AX.X, ALU.add).then_inc(sel_ok, 1)
                    dve.wait_ge(sel_ok, n + 1)
                    dve.wait_ge(cum_ok, n + 1)
                    dve.tensor_tensor(tile(n + 1, rt.cum), tile(n, rt.cum), tile(n, rt.sel),
                                      ALU.add).then_inc(cum_ok, 1)

        @block.gpsimd
        def _(pool):
            pool.sem_inc(xs_ok, 2)
            with pool.Fori(0, NT // 4) as q:
                for k in range(4):
                    n, u = 4 * q + k, k % 2
                    pool.wait_ge(xn_ok, n + 1)
                    pool.tensor_copy(xna[:, ds(n, 1), :].rearrange("p o d -> p (o d)"), xn[:, u, :]).then_inc(xs_ok, 1)

        @block.tensor
        def _(pe):
            pe.wait_ge(w_ld, 16)
            with pe.Fori(0, NT // 4) as q:
                def transposes(k):
                    n, u = 4 * q + k, k % 2
                    pe.wait_ge(xn_ok, n + 1)
                    pe.wait_ge(xt_ok, n + 1)
                    for c in range(KD):
                        last = pe.transpose(p_t[u][:, c, :], xn[:, u, c * P:(c + 1) * P], st.c("ident"))
                    last.then_inc(xt_ps, 1)

                transposes(0)
                for k in range(4):
                    n, u = 4 * q + k, k % 2
                    if k < 3:
                        transposes(k + 1)
                    pe.wait_ge(xt_ok, n + 3)
                    pe.wait_ge(mx_ok, n + 1)
                    pe.wait_ge(e_ok, n + 1)
                    for c in range(KD):
                        last = pe.matmul(p_l[u][:, 0:NE], xt[:, u, c, :], wr[:, c, :], start=c == 0, stop=c == KD - 1)
                    last.then_inc(l_ps, 1)

        @block.scalar
        def _(act):
            finish_stats(nc, st, act, None, eps, root, rstd)
            act.sem_inc(xt_ok, 2)
            act.sem_inc(e_ok, 2)
            with act.Fori(0, NT // 4) as q:
                def take_xt(k):
                    n, u = 4 * q + k, k % 2
                    act.wait_ge(xt_ps, n + 3)
                    act.wait_ge(mx_ok, n + 1)
                    act.activation(xt[:, u], p_t[u][:, 0:KD, :], ACT.Copy).then_inc(xt_ok, 1)

                take_xt(0)
                for k in range(4):
                    n, u = 4 * q + k, k % 2
                    if k < 3:
                        take_xt(k + 1)
                    act.wait_ge(mx_ok, n + 3)
                    act.wait_ge(sc_ok, n + 1)
                    act.activation(e[:, u, :], p_l[u][:, 0:NE], ACT.Exp, bias=nm[:, u, :],
                                   accum_out=se[:, u, :]).then_inc(e_ok, 1)


def phase_dispatch(nc, st, rt, xna, xs_dram, zero_sem, n_zero):
    with ExitStack() as ctx:
        sb, ps, sem = opener(nc, ctx, "dp2")
        cnt_ps, gt_ok, til_ok, scan_ok, base_ok, cmp_ok, ecol_ok, erow_ps, erf_ok, er_ok = (
            sem(n) for n in ("cnt", "gt", "til", "scan", "base", "cmp", "ecol", "erow_ps", "erf", "er"))
        begun, r_ps, posf_ok, prod_ok, pos_ok, posu_ok, stg_ok, sent, sh_d = (
            sem(n) for n in ("begun", "r_ps", "posf", "prod", "pos", "posu", "stg", "sent", "sh"))
        scat = [sem(f"scat{i}") for i in range(2)]
        gt = sb("gt", [P, NE, 16])
        til = sb("til", [P, NE])
        scan = sb("scan", [P, NE])
        base = sb("base", [P, NE])
        cmp_ = sb("cmp", [P, 2, NE])
        ecol = sb("ecol", [P, 2])
        erf = sb("erf", [1, MT])
        new = sb("new", [1, MT])
        run_ = sb("run", [1, MT])
        runi = sb("runi", [1, MT], I32)
        one = sb("one", [1, MT])
        new_ok = sem("new")
        posf = sb("posf", [P, 2, NE])
        prod = sb("prod", [P, 2, TOPK, NE])
        pos = sb("pos", [P, 2, 8])
        posu = [sb(f"posu{i}", [P, 8], U32) for i in range(2)]
        stg = [sb(f"stg{i}", [P, D]) for i in range(2)]
        p_c = ps("p_c", [P, 512])
        p_e = ps("p_e", [P, 512])
        p_r = [ps(f"p_r{i}", [P, 512]) for i in range(2)]
        block = ctx.enter_context(nc.Block())

        @block.sync
        def _(sp):
            sp.dma_start(xs_dram[XT * P:MT * P, :].rearrange("(t p) d -> p t d", p=P), xna[:, :, :]).then_inc(sh_d, 16)
            sp.wait_ge(sh_d, 16)

        @block.tensor
        def _(pe):
            pe.sem_inc(posf_ok, 2)
            pe.sem_inc(sent, 2)
            pe.matmul(p_c[:, 0:NE], st.cb[:, 3, :], rt.cum[:, NT, :], start=True, stop=True).then_inc(cnt_ps, 1)
            pe.wait_ge(ecol_ok, 2)
            for i in range(2):
                last = pe.matmul(p_e[0:1, i * P:(i + 1) * P], ecol[:, i:i + 1], st.c("ident"), start=True, stop=True)
            last.then_inc(erow_ps, 1)
            with pe.Fori(0, NT // 2) as q:
                for u in range(2):
                    n = 2 * q + u
                    pe.wait_ge(posf_ok, n + 1)
                    pe.matmul(p_r[u][:, 0:NE], st.cb[:, 3, :], rt.cum[:, ds(n, 1), :].rearrange("p o e -> p (o e)"),
                              start=True, stop=False)
                    pe.matmul(p_r[u][:, 0:NE], st.cb[:, 2, :], rt.sel[:, ds(n, 1), :].rearrange("p o e -> p (o e)"),
                              start=False, stop=True).then_inc(r_ps, 1)

        @block.vector
        def _(dve):
            dve.wait_ge(cnt_ps, 1)
            dve.tensor_tensor(gt[:, :, :], p_c[:, 0:NE].unsqueeze(2).to_broadcast([P, NE, 16]),
                              st.c("k128").unsqueeze(1).to_broadcast([P, NE, 16]), ALU.is_gt).then_inc(gt_ok, 1)
            dve.wait_ge(gt_ok, 1)
            dve.tensor_reduce(til[:, :], gt[:, :, :], AX.X, ALU.add).then_inc(til_ok, 1)
            dve.wait_ge(til_ok, 1)
            dve.tensor_tensor_scan(scan[:, :], st.c("ones")[:, 0:NE], til[:, :], 0.0, ALU.mult,
                                   ALU.add).then_inc(scan_ok, 1)
            dve.wait_ge(scan_ok, 1)
            dve.tensor_tensor(base[:, :], scan[:, :], til[:, :], ALU.subtract).then_inc(base_ok, 1)
            dve.wait_ge(base_ok, 1)
            dve.tensor_scalar(base[:, :], base[:, :], float(P), None, ALU.mult).then_inc(base_ok, 1)
            for i in range(2):
                dve.tensor_scalar(cmp_[:, i, :], scan[:, :], st.c("iota_p")[:, i:i + 1], None,
                                  ALU.is_le).then_inc(cmp_ok, 1)
                dve.wait_ge(cmp_ok, i + 1)
                dve.tensor_reduce(ecol[:, i:i + 1], cmp_[:, i, :], AX.X, ALU.add).then_inc(ecol_ok, 1)
            dve.memset(erf[:, XT:MT], float(NE)).then_inc(erf_ok, 1)
            dve.wait_ge(erow_ps, 1)
            dve.tensor_scalar(erf[:, 0:XT], p_e[0:1, 0:XT], float(NE - 1), None, ALU.min).then_inc(erf_ok, 1)
            dve.wait_ge(erf_ok, 2)
            dve.tensor_copy(rt.erow[:, :], erf[:, :]).then_inc(er_ok, 1)
            dve.memset(new[:, 0:1], 1.0).then_inc(new_ok, 1)
            dve.tensor_tensor(new[:, 1:MT], erf[:, 1:MT], erf[:, 0:MT - 1], ALU.not_equal).then_inc(new_ok, 1)
            dve.wait_ge(new_ok, 2)
            dve.tensor_copy(rt.new[:, :], new[:, :]).then_inc(er_ok, 1)
            dve.memset(one[:, :], 1.0).then_inc(new_ok, 1)
            dve.wait_ge(new_ok, 3)
            dve.tensor_tensor_scan(run_[:, :], one[:, :], new[:, :], 0.0, ALU.mult, ALU.add).then_inc(new_ok, 1)
            dve.wait_ge(new_ok, 4)
            dve.tensor_copy(runi[:, :], run_[:, :]).then_inc(new_ok, 1)
            dve.wait_ge(new_ok, 5)
            dve.tensor_scalar(rt.slot[:, :], runi[:, :], NW - 1, None, ALU.bitwise_and).then_inc(er_ok, 1)
            dve.wait_ge(base_ok, 2)
            with dve.Fori(0, NT // 2) as q:
                for u in range(2):
                    n = 2 * q + u
                    dve.wait_ge(r_ps, n + 1)
                    dve.tensor_tensor(posf[:, u, :], p_r[u][:, 0:NE], base[:, :], ALU.add).then_inc(posf_ok, 1)
                    dve.wait_ge(posf_ok, n + 3)
                    dve.tensor_tensor(prod[:, u], rt.hot[:, ds(n, 1)].rearrange("p o k e -> p (o k) e"),
                                      posf[:, u, :].unsqueeze(1).to_broadcast([P, TOPK, NE]),
                                      ALU.mult).then_inc(prod_ok, 1)
                    dve.wait_ge(prod_ok, n + 1)
                    dve.tensor_reduce(pos[:, u, 0:TOPK], prod[:, u], AX.X, ALU.add).then_inc(pos_ok, 1)
                    dve.wait_ge(pos_ok, n + 1)
                    dve.wait_ge(sent, n + 1)
                    dve.tensor_copy(posu[u][:, 0:TOPK], pos[:, u, 0:TOPK]).then_inc(posu_ok, 1)
                    dve.tensor_copy(rt.pos[:, ds(n, 1), 0:TOPK].rearrange("p o k -> p (o k)"),
                                    pos[:, u, 0:TOPK]).then_inc(posu_ok, 1)

        @block.scalar
        def _(act):
            with act.Fori(0, NT // 2) as q:
                for u in range(2):
                    n = 2 * q + u
                    act.wait_ge(sent, n + 1)
                    act.activation(stg[u][:, :], xna[:, ds(n, 1), :].rearrange("p o d -> p (o d)"),
                                   ACT.Copy).then_inc(stg_ok, 1)

        @block.gpsimd
        def _(pool):
            pool.wait_ge(zero_sem, 16 * n_zero)
            with pool.Fori(0, NT // 2) as q:
                for u in range(2):
                    n = 2 * q + u
                    pool.wait_ge(posu_ok, 2 * n + 1)
                    pool.wait_ge(stg_ok, n + 1)
                    pool.sem_inc(begun, 1)
                    for k in range(TOPK):
                        pool.indirect_dma_start(xs_dram[0:XT * P, :],
                                                bass.IndirectOffsetOnAxis(posu[u][:, k:k + 1], 0),
                                                stg[u][:, :], None).then_inc(scat[u], 16)
                for u in range(2):
                    pool.wait_ge(scat[u], 16 * TOPK * (q + 1))
                    pool.sem_inc(sent, 1)


def phase_experts(nc, st, rt, xs_dram, ys_dram, w_in):
    NB = 4
    with ExitStack() as ctx:
        sb, ps, sem = opener(nc, ctx, "ex")
        ld_w = [sem(f"ld_w{i}") for i in range(NW)]
        ld_x = [sem(f"ld_x{i}") for i in range(NB)]
        stored = [sem(f"stored{i}") for i in range(NB)]
        xt_ps, xt_ok, gv_ps, sg_ok, h_ok, ht_ps, ht_ok, y_ps, y_ok, pad_ok = (
            sem(n) for n in ("xt_ps", "xt", "gv_ps", "sg", "h", "ht_ps", "ht", "y_ps", "y", "pad"))
        xs = sb("xs", [P, NB, D])
        w_ = sb("w", [P, NW, WX])
        xt = sb("xt", [P, 2, KD, P])
        sg = sb("sg", [P, 2, FE])
        h = sb("h", [P, 2, KF * P])
        ht = sb("ht", [P, 2, KF, P])
        y = sb("y", [P, NB, D])
        p_x, p_gv, p_h, p_y = ([ps(f"p_{m}{i}", [P, 512]) for i in range(2)] for m in ("x", "gv", "h", "y"))
        block = ctx.enter_context(nc.Block())

        def slot(eng, n):
            return eng.value_load(rt.slot[0:1, ds(n, 1)], min_val=0, max_val=NW - 1)

        @block.gpsimd
        def _(pool):
            pool.sem_inc(xt_ps, NB)
            pool.memset(h[:, :, FE:KF * P], 0.0).then_inc(pad_ok, 1)

            def load(n, k):
                pool.wait_ge(xt_ps, n + 1)
                pool.dma_start(xs[:, k, :], xs_dram[ds(n * P, P), :]).then_inc(ld_x[k], 16)

            pipeline(pool, MT, NB, (0, load))

        @block.sync
        def _(sp):
            sp.sem_inc(y_ps, NW)

            def load(n, k):
                e = sp.value_load(rt.erow[0:1, ds(n, 1)], min_val=0, max_val=NE)
                new = sp.value_load(rt.new[0:1, ds(n, 1)], min_val=0, max_val=1)
                w = slot(sp, n)
                sp.wait_ge(y_ps, n + 1)
                sp.dma_start(w_[:, ds(w, 1), :].rearrange("p o f -> p (o f)"),
                             w_in[ds(e, 1)].rearrange("o p f -> p (o f)"), cond=new).then_inc(ld_w[k], 16)

            pipeline(sp, MT, NW, (0, load))

        @block.tensor
        def _(pe):
            def h_part(n, k):
                pe.wait_ge(h_ok, n + 1)
                for c in range(KF):
                    last = pe.transpose(p_h[k % 2][:, c * P:(c + 1) * P], h[:, k % 2, c * P:(c + 1) * P], st.c("ident"))
                last.then_inc(ht_ps, 1)

            def x_part(n, k):
                pe.wait_ge(ld_x[k % NB], 4 * (n - k % NB) + 16)
                for c in range(KD):
                    last = pe.transpose(p_x[k % 2][:, c * P:(c + 1) * P], xs[:, k % NB, c * P:(c + 1) * P],
                                        st.c("ident"))
                last.then_inc(xt_ps, 1)

            def gv_part(n, k):
                w = slot(pe, n)
                pe.wait_ge(ld_w[k], 2 * (n - k) + 16)
                pe.wait_ge(xt_ok, n + 1)
                for c in range(KD):
                    last = pe.matmul(p_gv[k % 2][:, 0:2 * FE], xt[:, k % 2, c, :],
                                     w_[:, ds(w, 1), c * 2 * FE:(c + 1) * 2 * FE].rearrange("p o f -> p (o f)"),
                                     start=c == 0, stop=c == KD - 1)
                last.then_inc(gv_ps, 1)

            def y_part(n, k):
                w = slot(pe, n)
                pe.wait_ge(ht_ok, n + 1)
                pe.wait_ge(y_ok, n + 1)
                for c in range(KF):
                    own = slice(KD * 2 * FE + c * D, KD * 2 * FE + (c + 1) * D)
                    last = pe.matmul(p_y[k % 2][:, 0:D], ht[:, k % 2, c, :],
                                     w_[:, ds(w, 1), own].rearrange("p o f -> p (o f)"),
                                     start=c == 0, stop=c == KF - 1)
                last.then_inc(y_ps, 1)

            pipeline(pe, MT, NW, (3, h_part), (0, x_part), (1, gv_part), (4, y_part))

        @block.scalar
        def _(act):
            def take_x(n, k):
                act.wait_ge(xt_ps, n + NB + 1)
                act.activation(xt[:, k % 2], p_x[k % 2][:, 0:D].rearrange("p (c t) -> p c t", c=KD),
                               ACT.Copy).then_inc(xt_ok, 1)

            def gate(n, k):
                act.wait_ge(gv_ps, n + 1)
                act.activation(sg[:, k % 2, :], p_gv[k % 2][:, 0:FE], ACT.Silu).then_inc(sg_ok, 1)

            def take_h(n, k):
                act.wait_ge(ht_ps, n + 3)
                act.wait_ge(y_ps, n + NW - 1)
                act.activation(ht[:, k % 2], p_h[k % 2][:, 0:KF * P].rearrange("p (c t) -> p c t", c=KF),
                               ACT.Copy).then_inc(ht_ok, 1)

            def store(n, k):
                act.wait_ge(y_ok, n + 3)
                act.dma_start(ys_dram[ds(n * P, P), :], y[:, k, :]).then_inc(stored[k], 16)

            pipeline(act, MT, NB, (3, take_h), (0, take_x), (1, gate), (5, store))
            for done in stored:
                act.wait_ge(done, 16 * (MT // NB) + 16)

        @block.vector
        def _(dve):
            dve.sem_inc(ht_ps, 2)
            dve.sem_inc(y_ok, 2)
            for done in stored:
                dve.sem_inc(done, 16)
            dve.wait_ge(pad_ok, 1)

            def gate(n, k):
                dve.wait_ge(sg_ok, n + 1)
                dve.wait_ge(ht_ps, n + 1)
                dve.tensor_tensor(h[:, k % 2, 0:FE], sg[:, k % 2, :], p_gv[k % 2][:, FE:2 * FE], ALU.mult).then_inc(h_ok, 1)

            def take_y(n, k):
                dve.wait_ge(y_ps, n + NW + 1)
                dve.wait_ge(stored[k], 4 * (n - k) + 16)
                dve.tensor_copy(y[:, k, :], p_y[k % 2][:, 0:D]).then_inc(y_ok, 1)

            pipeline(dve, MT, NB, (1, gate), (4, take_y))


def phase_combine(nc, st, rt, ys_dram, yout):
    with ExitStack() as ctx:
        sb, ps, sem = opener(nc, ctx, "cb")
        begun, pos_ok, w_ok, sh_d, y_ok, stat, agg = (
            sem(n) for n in ("begun", "pos", "w", "sh", "y", "stat", "agg"))
        g_d = [sem(f"g{i}") for i in range(2)]
        posu = [sb(f"posu{i}", [P, 8], U32) for i in range(2)]
        w = sb("w", [P, 2, 8])
        g = [[sb(f"g{i}_{k}", [P, D]) for k in range(TOPK)] for i in range(2)]
        acc = sb("acc", [P, 2, 2, D])
        stats = sb("stats", [P, NT, 6])
        block = ctx.enter_context(nc.Block())
        S = TOPK

        @block.sync
        def _(sp):
            sp.dma_start(yout[:, :, :], ys_dram[XT * P:MT * P, :].rearrange("(t p) d -> p t d", p=P)).then_inc(sh_d, 16)
            sp.wait_ge(sh_d, 16)

        @block.vector
        def _(dve):
            dve.sem_inc(y_ok, S + 1)
            dve.wait_ge(sh_d, 16)
            with dve.Fori(0, NT // 2) as q:
                for u in range(2):
                    n = 2 * q + u
                    dve.tensor_copy(w[:, u, :], rt.top[:, ds(n, 1), :].rearrange("p o k -> p (o k)")).then_inc(w_ok, 1)
                    dve.wait_ge(w_ok, n + 1)
                    dve.wait_ge(g_d[u], 16 * TOPK * q + 16 * TOPK)
                    for k in range(TOPK):
                        dve.wait_ge(y_ok, S * n + S + k + 1)
                        src = yout[:, ds(n, 1), :].rearrange("p o d -> p (o d)") if k == 0 else acc[:, u, k % 2, :]
                        dst = yout[:, ds(n, 1), :].rearrange("p o d -> p (o d)") if k == TOPK - 1 \
                            else acc[:, u, (k + 1) % 2, :]
                        dve.scalar_tensor_tensor(dst, g[u][k][:, :], w[:, u, k:k + 1], src,
                                                 ALU.mult, ALU.add).then_inc(y_ok, 1)
                    dve.wait_ge(y_ok, S * n + 2 * S + 1)
                    dve.bn_stats(stats[:, ds(n, 1), :].rearrange("p o d -> p (o d)"),
                                 yout[:, ds(n, 1), :].rearrange("p o d -> p (o d)")).then_inc(stat, 1)
            dve.wait_ge(stat, NT)
            for n in range(NT):
                dve.bn_aggr(st.mv[:, n, :], stats[:, n, :]).then_inc(agg, 1)

        @block.scalar
        def _(act):
            for u in range(2):
                act.activation(posu[u][:, 0:TOPK], rt.pos[:, u, 0:TOPK], ACT.Copy).then_inc(pos_ok, 1)
            with act.Fori(0, NT // 2 - 1) as q:
                for u in range(2):
                    n = 2 * q + u
                    act.wait_ge(g_d[u], 16 * TOPK * q + 16 * TOPK)
                    act.activation(posu[u][:, 0:TOPK], rt.pos[:, ds(n + 2, 1), 0:TOPK].rearrange("p o k -> p (o k)"),
                                   ACT.Copy).then_inc(pos_ok, 1)

        @block.gpsimd
        def _(pool):
            with pool.Fori(0, NT // 2) as q:
                for u in range(2):
                    n = 2 * q + u
                    pool.wait_ge(pos_ok, n + 1)
                    pool.wait_ge(y_ok, S * n + 1)
                    pool.sem_inc(begun, 1)
                    for k in range(TOPK):
                        pool.indirect_dma_start(g[u][k][:, :], None, ys_dram[0:XT * P, :],
                                                bass.IndirectOffsetOnAxis(posu[u][:, k:k + 1], 0)).then_inc(g_d[u], 16)


class AttentionData:

    def __init__(self, nc, ctx):
        def sb(name, shape):
            return ctx.enter_context(nc.sbuf_tensor(f"ad_{name}", shape, F32))

        self.qt = sb("qt", [P, HG, T])
        self.kt = sb("kt", [P, HG, T])
        self.v = sb("v", [P, NT, H, DH])


def phase_attention_project(nc, st, ad, w_in):
    with ExitStack() as ctx:
        sb, ps, sem = opener(nc, ctx, "ap")
        w_ld, eps, root, rstd = (sem(n) for n in ("w_ld", "eps", "root", "rstd"))
        xn_ok, xt_ps, xt_ok, qk_ps, rot_in, rot_ok, qkt_ps, v_out, qkt_out = (
            sem(n) for n in ("xn", "xt_ps", "xt", "qk_ps", "rot_in", "rot", "qkt_ps", "v_out", "qkt_out"))
        w = sb("w", [P, KD, 3 * D])
        xn = sb("xn", [P, 2, D])
        xt = sb("xt", [P, 2, KD, P])
        rc = sb("rc", [P, 2, 2 * D])
        rs = sb("rs", [P, 2, 2 * D])
        qk = sb("qk", [P, 2, 2 * D])
        p_x, p_qk, p_v, p_t = ([ps(f"p_{m}{i}", [P, 512]) for i in range(2)] for m in ("x", "qk", "v", "t"))
        block = ctx.enter_context(nc.Block())

        @block.sync
        def _(sp):
            sp.dma_start(w[:, :, :], w_in).then_inc(w_ld, 16)
            sp.wait_ge(w_ld, 16)

        @block.vector
        def _(dve):
            finish_stats(nc, st, None, dve, eps, root, rstd)

            def normalise(n, k):
                dve.wait_ge(xt_ps, n + 1)
                dve.tensor_scalar(xn[:, k % 2, :], st.x[:, ds(n, 1), :], st.mv[:, ds(n, 1), 0],
                                  st.rstd[:, ds(n, 1)], ALU.subtract, ALU.mult).then_inc(xn_ok, 1)

            def rotate(n, k):
                dve.wait_ge(qk_ps, n + 3)
                dve.wait_ge(rot_ok, 2 * n + 2)
                src = p_qk[k % 2][:, :].rearrange("p (h j s) -> p h j s", h=2 * H, s=2)
                for dst, name in ((rc, "cos"), (rs, "sin")):
                    table = st.c(name)[:, k * DH // 2:(k + 1) * DH // 2]
                    for s in range(2):
                        dve.tensor_tensor(dst[:, k % 2, :].rearrange("p (h j s) -> p h j s", h=2 * H, s=2)[..., s],
                                          src[..., s], table.unsqueeze(1).to_broadcast([P, 2 * H, DH // 2]),
                                          ALU.mult).then_inc(rot_in, 1)

            pipeline(dve, NT, TB, (0, normalise), (2, rotate))

        @block.gpsimd
        def _(pool):
            pool.sem_inc(rot_ok, 4)

            def combine(n, k):
                pool.wait_ge(rot_in, 4 * n + 12)
                pool.wait_ge(qkt_ps, n + 1)
                c, s, o = (a[:, k % 2, :].rearrange("p (m e) -> p m e", e=2) for a in (rc, rs, qk))
                pool.tensor_tensor(o[:, :, 0], c[:, :, 0], s[:, :, 1], ALU.subtract).then_inc(rot_ok, 1)
                pool.tensor_tensor(o[:, :, 1], s[:, :, 0], c[:, :, 1], ALU.add).then_inc(rot_ok, 1)

            pipeline(pool, NT, TB, (0, combine))

        @block.scalar
        def _(act):
            finish_stats(nc, st, act, None, eps, root, rstd)
            act.sem_inc(xt_ok, 2)
            act.sem_inc(v_out, 2)
            act.sem_inc(qkt_out, 4)

            def take_x(n, k):
                act.wait_ge(xt_ps, n + 3)
                act.wait_ge(qk_ps, n + 1)
                act.activation(xt[:, k % 2], p_x[k % 2][:, 0:D].rearrange("p (c t) -> p c t", c=KD),
                               ACT.Copy).then_inc(xt_ok, 1)

            def take_v(n, k):
                act.wait_ge(qk_ps, n + 3)
                act.activation(ad.v[:, ds(n, 1)].rearrange("p o h d -> p (o h d)"), p_v[k % 2][:, 0:D],
                               ACT.Copy).then_inc(v_out, 1)

            def take_qk(n, k):
                act.wait_ge(qkt_ps, n + 3)
                src = p_t[k % 2][:, :].rearrange("p (m t) -> p m t", m=4)
                cols = ds(n * P, P)
                act.activation(ad.qt[:, :, cols], src[:, 0:2], ACT.Copy).then_inc(qkt_out, 1)
                act.activation(ad.kt[:, :, cols], src[:, 2:4], ACT.Copy).then_inc(qkt_out, 1)

            pipeline(act, NT, TB, (0, take_x), (1, take_v), (3, take_qk))

        @block.tensor
        def _(pe):
            pe.sem_inc(xt_ps, 2)
            pe.sem_inc(qk_ps, 2)
            pe.sem_inc(qkt_ps, 2)
            pe.sem_inc(rot_in, 8)
            pe.wait_ge(w_ld, 16)

            def x_part(n, k):
                pe.wait_ge(xn_ok, n + 1)
                pe.wait_ge(xt_ok, n + 1)
                for c in range(KD):
                    last = pe.transpose(p_x[k % 2][:, c * P:(c + 1) * P], xn[:, k % 2, c * P:(c + 1) * P], st.c("ident"))
                last.then_inc(xt_ps, 1)

            def qkv_part(n, k):
                pe.wait_ge(xt_ok, n + 3)
                pe.wait_ge(rot_in, 4 * n + 4)
                pe.wait_ge(v_out, n + 1)
                for c in range(KD):
                    pe.matmul(p_qk[k % 2][:, :], xt[:, k % 2, c, :], w[:, c, 0:2 * D], start=c == 0, stop=c == KD - 1)
                for c in range(KD):
                    last = pe.matmul(p_v[k % 2][:, 0:D], xt[:, k % 2, c, :], w[:, c, 2 * D:3 * D],
                                     start=c == 0, stop=c == KD - 1)
                last.then_inc(qk_ps, 1)

            def qkt_part(n, k):
                pe.wait_ge(rot_ok, 2 * n + 6)
                pe.wait_ge(qkt_out, 2 * n + 2)
                for m in range(4):
                    last = pe.transpose(p_t[k % 2][:, m * P:(m + 1) * P], qk[:, k % 2, m * P:(m + 1) * P], st.c("ident"))
                last.then_inc(qkt_ps, 1)

            pipeline(pe, NT, TB, (0, x_part), (1, qkv_part), (3, qkt_part))


def phase_attention(nc, st, ad, wo_in, y):
    SQ = 2
    UN = SQ * TB * H
    QT = SQ * TB
    SB, PB = 3, 4
    LT, LC, LV = 2, 3, 4
    with ExitStack() as ctx:
        sb, ps, sem = opener(nc, ctx, "at")
        w_ld, pad_ok, in_ok = sem("w_ld"), sem("pad"), sem("in")
        s_ps, max_ok, exp_ok, pt_ps, o_ps = (sem(n) for n in ("s_ps", "max", "exp", "pt_ps", "o_ps"))
        pt_ok = [sem("pt_dve"), sem("pt_act")]
        rec_ok, o_out, turned, norm_ok, back, on_ok, y_ps, y_ok, stat, agg = (
            sem(n) for n in ("rec", "o_out", "turned", "norm", "back", "on", "y_ps", "y", "stat", "agg"))
        wo = sb("wo", [P, HG, D])
        kt = sb("kt", [P, SQ, HG, L])
        qz = sb("qz", [P, SQ, HG, HP, L])
        vp = sb("vp", [P, SQ, TB, H, 2 * DH])
        nm = sb("nm", [P, SB, 1])
        se = sb("se", [P, 2, H])
        rec = sb("rec", [P, H])
        pr = sb("pr", [P, PB, L])
        pt = sb("pt", [P, 2, L])
        o = sb("o", [P, HG, P])
        oq = sb("oq", [P, D])
        on = sb("on", [P, HG, P])
        stats = sb("stats", [P, NT, 6])
        p_s = [ps(f"p_s{i}", [P, L]) for i in range(SB)]
        p_t = [ps(f"p_t{i}", [P, L]) for i in range(2)]
        p_o = [ps(f"p_o{i}", [P, 4, P]) for i in range(2)]
        p_y = ps("p_y", [P, L])
        block = ctx.enter_context(nc.Block())

        def of(i):
            return i // (TB * H), i // H % TB, i % H

        def at(i, lag):
            j, r = divmod(i - LV - lag, H)
            return j - 1 if r == 0 and 1 <= j <= QT else None

        STEPS = UN + LV + 7

        @block.sync
        def _(sp):
            sp.dma_start(wo[:, :, :], wo_in).then_inc(w_ld, 16)
            sp.wait_ge(w_ld, 16)

        @block.gpsimd
        def _(pool):
            pool.memset(vp[:, :, :, :, :], 0.0).then_inc(pad_ok, 1)
            pool.wait_ge(pad_ok, 1)
            for s in range(B):
                u = s % SQ
                if s >= SQ:
                    pool.wait_ge(o_ps, TB * H * (s - SQ + 1) + 2)
                for t in range(TB):
                    n, own, cols = s * TB + t, slice(t * P, (t + 1) * P), slice((s * TB + t) * P, (s * TB + t + 1) * P)
                    pool.tensor_copy(kt[:, u, :, own], ad.kt[:, :, cols]).then_inc(in_ok, 1)
                    for g in range(HG):
                        pool.tensor_tensor(qz[:, u, g, :, own], ad.qt[:, g, cols].unsqueeze(1).to_broadcast([P, HP, P]),
                                           st.c("heads").unsqueeze(2).to_broadcast([P, HP, P]),
                                           ALU.mult).then_inc(in_ok, 1)
                    for k in range(2):
                        pool.tensor_copy(vp[:, u, t, k:H:2, k * DH:(k + 1) * DH], ad.v[:, n, k:H:2, :]).then_inc(in_ok, 1)

        @block.vector
        def _(dve):
            dve.sem_inc(pt_ok[0], 1)
            dve.sem_inc(rec_ok, 2)
            with dve.Fori(0, B // SQ) as b:
                for i in range(STEPS):
                    if LC <= i < UN + LC and (i - LC) % 2 == 0:
                        k = i - LC
                        n = UN * b + k
                        nk = of(k)[1] + 1
                        dve.wait_ge(pt_ps, n + PB + 1)
                        dve.wait_ge(o_ps, n + 1)
                        dve.tensor_copy(pt[:, 0, 0:nk * P], p_t[0][:, 0:nk * P]).then_inc(pt_ok[0], 1)
                    if i < UN:
                        n = UN * b + i
                        dve.wait_ge(s_ps, n + 1)
                        dve.wait_ge(exp_ok, n + 1)
                        nk = of(i)[1] + 1
                        dve.tensor_reduce(nm[:, i % SB, :], p_s[i % SB][:, 0:nk * P], AX.X, ALU.max,
                                          negate=True).then_inc(max_ok, 1)
                    j = at(i, 1)
                    if j is not None:
                        n = QT * b + j
                        dve.wait_ge(exp_ok, UN * b + H * (j + 1) + SB)
                        dve.reciprocal(rec[:, :], se[:, j % 2, :]).then_inc(rec_ok, 1)
                        dve.wait_ge(rec_ok, n + 3)
                        dve.wait_ge(turned, n + 1)
                        dve.tensor_tensor(oq[:, :].rearrange("p (h d) -> p h d", d=DH),
                                          p_y[:, 0:D].rearrange("p (h d) -> p h d", d=DH),
                                          rec[:, :].unsqueeze(2).to_broadcast([P, H, DH]), ALU.mult).then_inc(norm_ok, 1)
                    j = at(i, 6)
                    if j is not None:
                        n = QT * b + j
                        dve.wait_ge(y_ok, n + 2)
                        dve.bn_stats(stats[:, ds(n, 1), :].rearrange("p o s -> p (o s)"),
                                     y[:, ds(n, 1), :].rearrange("p o d -> p (o d)")).then_inc(stat, 1)
            dve.wait_ge(stat, NT)
            for n in range(NT):
                dve.bn_aggr(st.mv[:, n, :], stats[:, n, :]).then_inc(agg, 1)

        @block.scalar
        def _(act):
            act.sem_inc(exp_ok, SB)
            act.sem_inc(pt_ok[1], 1)
            act.sem_inc(o_out, 2)
            act.sem_inc(y_ok, 1)
            with act.Fori(0, B // SQ) as b:
                for i in range(STEPS):
                    if LC <= i < UN + LC and (i - LC) % 2 == 1:
                        k = i - LC
                        n = UN * b + k
                        nk = of(k)[1] + 1
                        act.wait_ge(pt_ps, n + PB + 1)
                        act.wait_ge(o_ps, n + 1)
                        act.activation(pt[:, 1, 0:nk * P], p_t[1][:, 0:nk * P], ACT.Copy).then_inc(pt_ok[1], 1)
                    if i < UN:
                        n = UN * b + i
                        nk = of(i)[1] + 1
                        j = i // H
                        if i % H == 0:
                            act.wait_ge(rec_ok, QT * b + j + 1)
                        act.wait_ge(max_ok, n + 1)
                        act.wait_ge(pt_ps, n + 1)
                        act.activation(pr[:, i % PB, 0:nk * P], p_s[i % SB][:, 0:nk * P], ACT.Exp,
                                       bias=nm[:, i % SB, :], accum_out=se[:, j % 2, i % H:i % H + 1]).then_inc(exp_ok, 1)
                    j = at(i, 0)
                    if j is not None:
                        n = QT * b + j
                        act.wait_ge(o_ps, UN * b + H * (j + 1) + 2)
                        act.activation(o[:, :, :], p_o[j % 2][:, 0:HG, :], ACT.Copy).then_inc(o_out, 1)
                    j = at(i, 3)
                    if j is not None:
                        n = QT * b + j
                        act.wait_ge(back, n + 1)
                        act.activation(on[:, :, :], p_y[:, D:2 * D].rearrange("p (g t) -> p g t", g=HG),
                                       ACT.Copy).then_inc(on_ok, 1)
                    j = at(i, 5)
                    if j is not None:
                        n = QT * b + j
                        act.wait_ge(y_ps, n + 1)
                        act.activation(y[:, ds(n, 1), :].rearrange("p o d -> p (o d)"), p_y[:, 0:D],
                                       ACT.Copy).then_inc(y_ok, 1)

        @block.tensor
        def _(pe):
            pe.sem_inc(pt_ps, PB)
            pe.sem_inc(o_ps, 2)
            pe.wait_ge(w_ld, 16)

            def scores(b, i):
                n, (s, t, h) = UN * b + i, of(i)
                nk, hg = t + 1, h // HP
                if h == 0:
                    pe.wait_ge(in_ok, 5 * (QT * b + i // H) + 5)
                pe.wait_ge(exp_ok, n + 1)
                pe.matmul(p_s[i % SB][:, 0:nk * P], qz[:, s, hg, h % HP, t * P:(t + 1) * P], kt[:, s, hg, 0:nk * P],
                          start=True, stop=False)
                pe.matmul(p_s[i % SB][:, t * P:nk * P], st.cb[:, 0, :], st.cb[:, 1, :],
                          start=False, stop=True).then_inc(s_ps, 1)

            def transposes(b, i):
                n, nk = UN * b + i, of(i)[1] + 1
                pe.wait_ge(exp_ok, n + SB + 1)
                pe.wait_ge(pt_ok[i % 2], UN // 2 * b + i // 2 + 1)
                for c in range(nk):
                    last = pe.transpose(p_t[i % 2][:, c * P:(c + 1) * P], pr[:, i % PB, c * P:(c + 1) * P],
                                        st.c("ident"))
                last.then_inc(pt_ps, 1)

            def values(b, i):
                s, t, h = of(i)
                j, nk, hg, r = i // H, t + 1, h // HP, (h % HP) // 2 * 2 * DH
                if h == 0:
                    pe.wait_ge(o_out, QT * b + j + 1)
                pe.wait_ge(pt_ok[i % 2], UN // 2 * b + i // 2 + 2)
                for c in range(nk):
                    last = pe.matmul(p_o[j % 2][r:r + 2 * DH, hg, :], vp[:, s, c, h, :], pt[:, i % 2, c * P:(c + 1) * P],
                                     start=c == 0 and h % 2 == 0, stop=c == nk - 1 and h % 2 == 1)
                last.then_inc(o_ps, 1)

            with pe.Fori(0, B // SQ) as b:
                for i in range(STEPS):
                    if i < UN:
                        scores(b, i)
                    if LT <= i < UN + LT:
                        transposes(b, i - LT)
                    if LV <= i < UN + LV:
                        values(b, i - LV)
                    j = at(i, 1)
                    if j is not None:
                        pe.wait_ge(o_out, QT * b + j + 3)
                        pe.wait_ge(y_ok, QT * b + j + 1)
                        for g in range(HG):
                            last = pe.transpose(p_y[:, g * P:(g + 1) * P], o[:, g, :], st.c("ident"))
                        last.then_inc(turned, 1)
                    j = at(i, 3)
                    if j is not None:
                        pe.wait_ge(norm_ok, QT * b + j + 1)
                        for g in range(HG):
                            last = pe.transpose(p_y[:, D + g * P:D + (g + 1) * P], oq[:, g * P:(g + 1) * P],
                                                st.c("ident"))
                        last.then_inc(back, 1)
                    j = at(i, 5)
                    if j is not None:
                        pe.wait_ge(on_ok, QT * b + j + 1)
                        for g in range(HG):
                            last = pe.matmul(p_y[:, 0:D], on[:, g, :], wo[:, g, :], start=g == 0, stop=g == HG - 1)
                        last.then_inc(y_ps, 1)


def phase_ffn(nc, st, wgu_in, wd_in, y):
    FQ = FF // 4
    with ExitStack() as ctx:
        sb, ps, sem = opener(nc, ctx, "ff")
        w_ld, wd_ld, eps, root, rstd, stat, agg = (sem(n) for n in ("w_ld", "wd_ld", "eps", "root", "rstd", "stat", "agg"))
        xn_ok, xt_ps, xt_ok, g_ps, u_ps, sg_ok, h_ok, abs_ok, c_ok, ef_ok, s_ok, k_ok, ht_ps, ht_ok, y_ps, y_ok = (
            sem(n) for n in ("xn", "xt_ps", "xt", "g_ps", "u_ps", "sg", "h", "abs", "c", "ef", "s", "k",
                             "ht_ps", "ht", "y_ps", "y"))
        wgu = sb("wgu", [P, KD, 2, FF])
        wd = sb("wd", [P, FF // P, D])
        xn = sb("xn", [P, 2, D])
        xt = sb("xt", [P, 2, KD, P])
        sg = sb("sg", [P, 2, 512])
        h = sb("h", [P, 2, FF])
        a = sb("a", [P, 2, FF])
        cm = sb("cm", [P, 2, 3, 2, FQ], BF16)
        ef = sb("ef", [P, 2, 2, 2, FQ], BF16)
        sm = sb("sm", [P, 2, 4, FQ], BF16)
        hk = sb("hk", [P, 2, FF])
        ht = sb("ht", [P, 2, FF // P, P])
        stats = sb("stats", [P, NT, 6])
        p_t = ps("p_t", [P, 512])
        p_g = [ps(f"p_g{i}", [P, 512]) for i in range(2)]
        p_u = [ps(f"p_u{i}", [P, 512]) for i in range(2)]
        p_h = [ps(f"p_h{i}", [P, 512]) for i in range(2)]
        p_y = ps("p_y", [P, 512])
        block = ctx.enter_context(nc.Block())

        def quads(ap):
            return ap.rearrange("p (m s) -> p s m", s=4)

        @block.sync
        def _(sp):
            sp.dma_start(wgu[:, :, :, :], wgu_in).then_inc(w_ld, 16)
            sp.dma_start(wd[:, :, :], wd_in).then_inc(wd_ld, 16)
            sp.wait_ge(w_ld, 16)
            sp.wait_ge(wd_ld, 16)

        @block.vector
        def _(dve):
            dve.sem_inc(xt_ps, 2)
            dve.sem_inc(abs_ok, 2)
            dve.sem_inc(ef_ok, 4)
            dve.sem_inc(s_ok, 5)
            dve.sem_inc(ht_ps, 3)
            finish_stats(nc, st, None, dve, eps, root, rstd)

            def normalise(n, u):
                dve.wait_ge(xt_ps, n + 1)
                dve.tensor_scalar(xn[:, u, :], st.x[:, ds(n, 1), :], st.mv[:, ds(n, 1), 0], st.rstd[:, ds(n, 1)],
                                  ALU.subtract, ALU.mult).then_inc(xn_ok, 1)

            def gate(n, u):
                for j in range(2):
                    dve.wait_ge(sg_ok, 2 * n + j + 1)
                    dve.wait_ge(u_ps, 2 * n + j + 4)
                    dve.tensor_tensor(h[:, u, j * 512:(j + 1) * 512], sg[:, j, :], p_u[j][:, :],
                                      ALU.mult).then_inc(h_ok, 1)

            def compare(n, u):
                dve.wait_ge(abs_ok, 2 * n + 4)
                dve.wait_ge(s_ok, 4 * n + 1)
                v = quads(a[:, u, :])
                dve.tensor_tensor(cm[:, u, 0], v[:, 0:4:2], v[:, 1:4:2], ALU.is_ge).then_inc(c_ok, 1)
                dve.tensor_tensor(cm[:, u, 1], v[:, 0:2], v[:, 2:4], ALU.is_ge).then_inc(c_ok, 1)
                for s in range(2):
                    dve.tensor_tensor(cm[:, u, 2, s], v[:, s], v[:, 3 - s], ALU.is_ge).then_inc(c_ok, 1)

            def select(n, u):
                hv, kv = quads(h[:, u, :]), quads(hk[:, u, :])
                dve.wait_ge(ht_ps, 2 * n + 1)
                for s, (least, op) in enumerate(((2.0, ALU.is_ge), (1.0, ALU.is_ge), (0.0, ALU.is_ge),
                                                 (1.0, ALU.is_le))):
                    dve.wait_ge(s_ok, 4 * n + s + 6)
                    dve.scalar_tensor_tensor(kv[:, s], sm[:, u, s], least, hv[:, s], op, ALU.mult).then_inc(k_ok, 1)

            def take_stats(n, u):
                dve.wait_ge(y_ok, n + 2)
                dve.bn_stats(stats[:, ds(n, 1), :].rearrange("p o s -> p (o s)"),
                             y[:, ds(n, 1), :].rearrange("p o d -> p (o d)")).then_inc(stat, 1)

            pipeline(dve, NT, 2, (0, normalise), (3, compare), (2, gate), (3, select), (5, take_stats))
            dve.wait_ge(stat, NT)
            for n in range(NT):
                dve.bn_aggr(st.mv[:, n, :], stats[:, n, :]).then_inc(agg, 1)

        @block.gpsimd
        def _(pool):
            pool.sem_inc(k_ok, 5)

            def sums(n, u):
                c, e = cm[:, u], ef[:, u]
                pool.wait_ge(c_ok, 4 * n + 9)
                pool.tensor_tensor(e[:, 0], c[:, 1], c[:, 2], ALU.add).then_inc(ef_ok, 1)
                for s in range(2):
                    pool.tensor_tensor(e[:, 1, s], c[:, 1, s], c[:, 2, 1 - s], ALU.add).then_inc(ef_ok, 1)
                pool.wait_ge(ef_ok, 3 * n + 7)
                pool.wait_ge(k_ok, 4 * n + 1)
                pool.tensor_tensor(sm[:, u, 0], c[:, 0, 0], e[:, 0, 0], ALU.add).then_inc(s_ok, 1)
                pool.tensor_tensor(sm[:, u, 1], e[:, 0, 1], c[:, 0, 0], ALU.subtract).then_inc(s_ok, 1)
                pool.tensor_tensor(sm[:, u, 2], c[:, 0, 1], e[:, 1, 0], ALU.subtract).then_inc(s_ok, 1)
                pool.tensor_tensor(sm[:, u, 3], c[:, 0, 1], e[:, 1, 1], ALU.add).then_inc(s_ok, 1)

            pipeline(pool, NT, 2, (3, sums))

        @block.scalar
        def _(act):
            act.sem_inc(y_ok, 1)
            finish_stats(nc, st, act, None, eps, root, rstd)
            act.sem_inc(xt_ok, 1)
            act.sem_inc(h_ok, 2)
            act.sem_inc(c_ok, 5)
            act.sem_inc(u_ps, 3)
            act.sem_inc(ht_ok, 2)
            act.sem_inc(y_ps, 2)

            def take_x(n, u):
                act.wait_ge(xt_ps, n + 3)
                act.wait_ge(u_ps, 2 * n + 1)
                act.activation(xt[:, u], p_t[:, 0:D].rearrange("p (c t) -> p c t", c=KD), ACT.Copy).then_inc(xt_ok, 1)

            def take_h(n, u):
                for j in range(2):
                    act.wait_ge(ht_ps, 2 * n + j + 4)
                    act.wait_ge(y_ps, n + 1)
                    act.activation(ht[:, u, 4 * j:4 * j + 4, :], p_h[j][:, :].rearrange("p (c t) -> p c t", t=P),
                                   ACT.Copy).then_inc(ht_ok, 1)

            def gate(n, u):
                for j in range(2):
                    act.wait_ge(g_ps, 2 * n + j + 1)
                    act.wait_ge(h_ok, 2 * n + j + 1)
                    act.activation(sg[:, j, :], p_g[j][:, :], ACT.Silu).then_inc(sg_ok, 1)

            def magnitudes(n, u):
                for j in range(2):
                    act.wait_ge(h_ok, 2 * n + j + 3)
                    act.wait_ge(c_ok, 4 * n + 1)
                    act.activation(a[:, u, j * 512:(j + 1) * 512], h[:, u, j * 512:(j + 1) * 512],
                                   ACT.Abs).then_inc(abs_ok, 1)

            def take_y(n, u):
                act.wait_ge(y_ps, n + 3)
                act.activation(y[:, ds(n, 1), :].rearrange("p o d -> p (o d)"), p_y[:, 0:D], ACT.Copy).then_inc(y_ok, 1)

            pipeline(act, NT, 2, (1, take_x), (4, take_h), (2, gate), (2, magnitudes), (4, take_y))

        @block.tensor
        def _(pe):
            pe.wait_ge(w_ld, 16)
            pe.wait_ge(wd_ld, 16)

            def x_part(n, u):
                pe.wait_ge(xn_ok, n + 1)
                pe.wait_ge(xt_ok, n + 1)
                for c in range(KD):
                    last = pe.transpose(p_t[:, c * P:(c + 1) * P], xn[:, u, c * P:(c + 1) * P], st.c("ident"))
                last.then_inc(xt_ps, 1)

            def gu_part(n, u):
                pe.wait_ge(xt_ok, n + 2)
                for j in range(2):
                    pe.wait_ge(h_ok, 2 * n + j + 1)
                    for m, (bank, done) in enumerate(((p_g[j], g_ps), (p_u[j], u_ps))):
                        for c in range(KD):
                            last = pe.matmul(bank[:, :], xt[:, u, c, :], wgu[:, c, m, j * 512:(j + 1) * 512],
                                             start=c == 0, stop=c == KD - 1)
                        last.then_inc(done, 1)

            def h_part(n, u):
                pe.wait_ge(k_ok, 4 * n + 9)
                for j in range(2):
                    pe.wait_ge(ht_ok, 2 * n + j + 1)
                    for c in range(4):
                        last = pe.transpose(p_h[j][:, c * P:(c + 1) * P],
                                            hk[:, u, (4 * j + c) * P:(4 * j + c + 1) * P], st.c("ident"))
                    last.then_inc(ht_ps, 1)

            def y_part(n, u):
                pe.wait_ge(ht_ok, 2 * n + 4)
                pe.wait_ge(y_ok, n + 1)
                for c in range(FF // P):
                    last = pe.matmul(p_y[:, 0:D], ht[:, u, c, :], wd[:, c, :], start=c == 0, stop=c == FF // P - 1)
                last.then_inc(y_ps, 1)

            pipeline(pe, NT, 2, (1, x_part), (4, h_part), (2, gu_part), (4, y_part))


def phase_last(nc, st, y, out):
    with ExitStack() as ctx:
        sb, ps, sem = opener(nc, ctx, "la")
        eps, root, rstd, yn, xs, o_d, cp = (sem(n) for n in ("eps", "root", "rstd", "yn", "x", "out", "copied"))
        block = ctx.enter_context(nc.Block())

        @block.scalar
        def _(act):
            finish_stats(nc, st, act, None, eps, root, rstd)

        @block.vector
        def _(dve):
            finish_stats(nc, st, None, dve, eps, root, rstd)
            for t in range(NT):
                dve.tensor_scalar(y[:, t, :], y[:, t, :], st.mv[:, t, 0:1], st.rstd[:, t:t + 1],
                                  ALU.subtract, ALU.mult).then_inc(yn, 1)
                dve.wait_ge(yn, t + 1)
                dve.tensor_tensor(st.x[:, t, :], st.x[:, t, :], y[:, t, :], ALU.add).then_inc(xs, 1)

        @block.sync
        def _(sp):
            for b in range(B):
                sp.wait_ge(xs, TB * (b + 1))
                sp.dma_start(out[b].rearrange("(t p) d -> p t d", p=P),
                             st.x[:, b * TB:(b + 1) * TB, :]).then_inc(o_d, 16)
            sp.wait_ge(o_d, 16 * B)


def build(nc, x, cst, w_dp, wo_d, onw, w_r, w_x, w_at, wo_a, w_gu, w_down, out):
    kvb_dram = nc.dram_tensor("kvb_dram", (T, H, KVW), F32, kind="Internal").ap()
    xs_dram = nc.dram_tensor("xs_dram", (MT * P, D), F32, kind="Internal").ap()
    ys_dram = nc.dram_tensor("ys_dram", (MT * P, D), F32, kind="Internal").ap()
    with ExitStack() as ctx:
        def sb(c, name, shape, dt=F32):
            return c.enter_context(nc.sbuf_tensor(name, shape, dt))

        st = State(nc, ctx)
        phase_load(nc, st, x, cst)
        with ExitStack() as until_dispatch:
            zeros = sb(until_dispatch, "zeros", [P, 1024])
            zero_sem = until_dispatch.enter_context(nc.semaphore("slots_zeroed"))
            n_zero = XT * D // 1024
            att = sb(until_dispatch, "att", [P, C, NC_ * G])
            with ExitStack() as delta:
                mkv = sb(delta, "mkv", [P, NC_, G, C + KVW])
                kqt = sb(delta, "kqt", [P, NC_, G, 2, C])
                with ExitStack() as raw:
                    qr = sb(raw, "q_raw", [P, NT, D])
                    kvb = sb(raw, "kvb", [P, NT, H, KVW])
                    norms = sb(raw, "norms", [P, NT, 2 * H])
                    wall = sb(raw, "w_qkvb", [P, KD, 3 * D + H])
                    phase_delta_project(nc, st, w_dp, qr, kvb, norms, wall, zeros)
                    phase_delta_layout(nc, st, qr, kvb, norms, kqt, kvb_dram)
                phase_delta_scores(nc, st, kqt, kvb_dram, mkv, att)
                phase_delta_invert(nc, st, mkv, att, zeros, xs_dram, zero_sem, n_zero)
                xt = sb(delta, "xt", [P, NC_, G, 2, C])
                phase_delta_wy(nc, st, kqt, mkv, att, xt)
                ot = att[:, :, :].rearrange("p a b -> p (a b)").rearrange("p (g b l) -> p g b l", g=HG, b=B)
                phase_delta_chain(nc, st, mkv, xt, ot)
            y = sb(until_dispatch, "y_first", [P, NT, D])
            phase_delta_out(nc, st, ot, wo_d, onw, y)
            phase_update(nc, st, y, "up1")
            rt = Routing(nc, until_dispatch)
            phase_route(nc, st, rt, w_r, y)
            phase_dispatch(nc, st, rt, y, xs_dram, zero_sem, n_zero)
            phase_experts(nc, st, rt, xs_dram, ys_dram, w_x)
            phase_combine(nc, st, rt, ys_dram, y)
            phase_update(nc, st, y, "up2")
        y = sb(ctx, "y", [P, NT, D])
        with ExitStack() as attention:
            ad = AttentionData(nc, attention)
            phase_attention_project(nc, st, ad, w_at)
            phase_attention(nc, st, ad, wo_a, y)
        phase_update(nc, st, y, "up3")
        phase_ffn(nc, st, w_gu, w_down, y)
        phase_last(nc, st, y, out)


def rows(w, k):
    return np.ascontiguousarray(np.moveaxis(w.reshape(w.shape[:-2] + (k, w.shape[-2] // k, w.shape[-1])), -3, -2))


def flat(w):
    return w.reshape(w.shape[:2] + (-1,))


def kernel(**inputs):
    import concourse.bacc as _bacc
    from concourse.bass_utils import run_bass_kernel_spmd as _run

    a = {k: np.asarray(v) for k, v in inputs.items()}
    l0, lf, l1, lg = "L0_attn_", "L0_ffn_", "L1_attn_", "L1_ffn_"

    def with_shared(name):
        return np.concatenate([a[lf + name], a[lf + "s" + name][None]])

    arrays = {
        "x": a[l0 + "hidden_states"],
        "cst": constants(),
        "w_dp": rows(np.concatenate([a[l0 + n] for n in ("Wq", "Wk", "Wv", "Wb")], 1), KD),
        "wo_d": rows(a[l0 + "Wo"], HG),
        "onw": np.ascontiguousarray(np.tile(a[l0 + "o_norm_weight"], HP)[:, None]),
        "w_r": rows(a[lf + "w_router"].T, KD),
        "w_x": np.concatenate([flat(rows(np.concatenate([with_shared("wg"), with_shared("wv")], 2), KD)),
                               flat(rows(np.pad(with_shared("wo"), ((0, 0), (0, KF * P - FE), (0, 0))), KF))], 2),
        "w_at": rows(np.concatenate([a[l1 + n].T for n in ("Wq", "Wk", "Wv")], 1), KD),
        "wo_a": rows(a[l1 + "Wo"].T, HG),
        "w_gu": np.ascontiguousarray(np.stack([rows(a[lg + "w_gate"], KD), rows(a[lg + "w_up"], KD)], 2)),
        "w_down": rows(a[lg + "w_down"], FF // P),
    }
    nc = _bacc.Bacc("TRN2", target_bir_lowering=False, num_devices=1)
    args = [nc.dram_tensor(f"in_{k}", v.shape, mybir.dt.from_np(v.dtype), kind="ExternalInput").ap()
            for k, v in arrays.items()]
    out = nc.dram_tensor("out", (B, L, D), F32, kind="ExternalOutput").ap()
    build(nc, *args, out)
    r = _run(nc, [{f"in_{k}": v for k, v in arrays.items()}], core_ids=[0])
    return r.results[0]["out"]
```

```python
from contextlib import ExitStack

import concourse.bass as bass
import numpy as np
from concourse import mybir

F32 = mybir.dt.float32
BF16 = mybir.dt.bfloat16
I32 = mybir.dt.int32
U32 = mybir.dt.uint32
ALU = mybir.AluOpType
ACT = mybir.ActivationFunctionType
AX = mybir.AxisListType
ds = bass.ds

B, L, D = 4, 512, 256
T = B * L
P = 128
NT = T // P
TB = L // P
KD = D // P
H, DH = 16, 16
HG = H * DH // P
HP = P // DH
G = B * HG
C = 16
NC_ = L // C
CT = P // C
EPS = 1e-5
NE, TOPK, FE = 64, 6, 176
KF = -(-FE // P)
WX = KD * 2 * FE + KF * D
XT = 160
NW = 8
ZW = 1076
XW = D + 1 + 2 * TOPK
FF = 1024
Q = 32
KVW = 2 * DH + 2

_C = {}
_off = 0
for _name, _w in (("ident", P), ("pair", 2), ("eye16", DH), ("mask_a", C), ("mask_m", C), ("mean_blk", P),
                  ("heads", HP), ("causal", P), ("tri", P), ("ones", P), ("iota_e", NE), ("iota_p", 2),
                  ("k128", 16), ("cos", TB * DH // 2), ("sin", TB * DH // 2), ("number", NT), ("slots", XT),
                  ("beyond", 1)):
    _C[_name] = (_off, _off + _w)
    _off += _w
CW = _off


def constants():
    c = np.zeros((P, CW), np.float32)
    p = np.arange(P)

    def put(name, v):
        c[:, _C[name][0]:_C[name][1]] = v

    put("ident", np.eye(P))
    put("pair", p[:, None] // DH % 2 == np.arange(2)[None])
    put("eye16", p[:, None] % DH == np.arange(DH)[None])
    put("mask_a", -1.0 * (np.arange(C)[None] < p[:, None] % C))
    put("mask_m", np.arange(C)[None] >= p[:, None] % C)
    put("mean_blk", (p[:, None] // DH == p[None] // DH) / DH)
    put("heads", (p[:, None] // DH == np.arange(HP)[None]) * DH ** -0.5)
    put("causal", np.where(p[None] > p[:, None], -1e30, 0.0))
    put("tri", p[:, None] < p[None])
    put("ones", 1.0)
    put("iota_e", np.arange(NE)[None])
    put("iota_p", p[:, None] + P * np.arange(2)[None])
    put("k128", P * np.arange(16)[None])
    theta = np.float32(10000.0) ** (-2.0 * np.arange(DH // 2, dtype=np.float32) / DH)
    ang = (p[:, None, None] + P * np.arange(TB)[None, :, None]).astype(np.float32) * theta.astype(np.float32)
    put("cos", np.cos(ang).reshape(P, -1))
    put("sin", np.sin(ang).reshape(P, -1))
    put("number", p[:, None] + P * np.arange(NT)[None] + 1)
    put("slots", p[:, None] + P * np.arange(XT)[None])
    put("beyond", T + 1 + p[:, None])
    return c


class State:

    def __init__(self, nc, ctx):
        self.nc = nc
        self.n = 0
        self.x = ctx.enter_context(nc.sbuf_tensor("x_res", [P, NT, D], F32))
        self.cst = ctx.enter_context(nc.sbuf_tensor("cst", [P, CW], F32))
        self.cb = ctx.enter_context(nc.sbuf_tensor("cst_bf16", [P, 4, P], BF16))
        self.mv = ctx.enter_context(nc.sbuf_tensor("mean_var", [P, NT, 2], F32))
        self.rstd = ctx.enter_context(nc.sbuf_tensor("rstd", [P, NT], F32))

    def c(self, name):
        return self.cst[:, _C[name][0]:_C[name][1]]


def opener(nc, ctx, phase):
    sems = []

    def give_back():
        nc.clear_and_free_semaphores(sems)
        nc.all_engine_barrier()

    ctx.callback(give_back)

    def sb(name, shape, dt=F32):
        return ctx.enter_context(nc.sbuf_tensor(f"{phase}_{name}", shape, dt))

    def ps(name, shape, dt=F32):
        return ctx.enter_context(nc.psum_tensor(f"{phase}_{name}", shape, dt))

    def sem(name):
        sems.append(nc.alloc_semaphore(f"{phase}_{name}"))
        return sems[-1]

    return sb, ps, sem


def pipeline(eng, count, unroll, *stages):
    behind = max(lag for lag, _ in stages)
    first = -(-behind // unroll) * unroll
    passes = (count - first) // unroll

    def step(k, base):
        for lag, stage in stages:
            if 0 <= k - lag < count:
                stage(base + (k - lag), (k - lag) % unroll)

    for k in range(first):
        step(k, 0)
    with eng.Fori(0, passes) as c:
        for k in range(first, first + unroll):
            step(k, unroll * c)
    for k in range(first + unroll * passes, count + behind):
        step(k, 0)


def phase_load(nc, st, x_in, cst_in):
    with ExitStack() as ctx:
        sb, ps, sem = opener(nc, ctx, "ld")
        x_in_sem, cst_sem, cast, stat, agg = sem("x"), sem("c"), sem("cast"), sem("stat"), sem("agg")
        stats = sb("stats", [P, NT, 6])
        block = ctx.enter_context(nc.Block())

        @block.sync
        def _(sp):
            for b in range(B):
                sp.dma_start(st.x[:, b * TB:(b + 1) * TB, :],
                             x_in[b].rearrange("(t p) d -> p t d", p=P)).then_inc(x_in_sem, 16)
            sp.wait_ge(x_in_sem, 16 * B)

        @block.scalar
        def _(act):
            act.dma_start(st.cst[:, :], cst_in).then_inc(cst_sem, 16)
            act.wait_ge(cst_sem, 16)
            for k, name in enumerate(("ident", "causal", "tri", "ones")):
                act.activation(st.cb[:, k, :], st.c(name), ACT.Copy).then_inc(cast, 1)

        @block.vector
        def _(dve):
            dve.wait_ge(x_in_sem, 16 * B)
            for t in range(NT):
                dve.bn_stats(stats[:, t, :], st.x[:, t, :]).then_inc(stat, 1)
            for t in range(NT):
                dve.wait_ge(stat, t + 1)
                dve.bn_aggr(st.mv[:, t, :], stats[:, t, :]).then_inc(agg, 1)


def finish_stats(nc, st, act, dve, eps_sem, root_sem, rstd_sem):
    if dve is not None:
        dve.tensor_scalar(st.rstd[:, :], st.mv[:, :, 1], EPS, None, ALU.add).then_inc(eps_sem, 1)
        dve.wait_ge(root_sem, 1)
        dve.reciprocal(st.rstd[:, :], st.rstd[:, :]).then_inc(rstd_sem, 1)
        dve.wait_ge(rstd_sem, 1)
    if act is not None:
        act.wait_ge(eps_sem, 1)
        act.activation(st.rstd[:, :], st.rstd[:, :], ACT.Sqrt).then_inc(root_sem, 1)


def find_shift(st, dve, shift, shifted):
    dve.scalar_tensor_tensor(shift[:, :], st.mv[:, :, 0], -1.0, st.rstd[:, :], ALU.mult, ALU.mult).then_inc(shifted, 1)


def normalise(st, act, y, shift, shifted, yn):
    act.wait_ge(shifted, 1)
    for t in range(NT):
        act.activation(y[:, t, :], y[:, t, :], ACT.Identity, bias=shift[:, t:t + 1],
                       scale=st.rstd[:, t:t + 1]).then_inc(yn, 1)


def phase_update(nc, st, y, tag):
    with ExitStack() as ctx:
        sb, ps, sem = opener(nc, ctx, tag)
        eps, root, rstd = sem("eps"), sem("root"), sem("rstd")
        shifted, yn, x_pool, x_dve, stat, agg = (sem(n) for n in ("shifted", "yn", "x_pool", "x_dve", "stat", "agg"))
        stats = sb("stats", [P, NT, 6])
        shift = sb("shift", [P, NT])
        block = ctx.enter_context(nc.Block())

        @block.scalar
        def _(act):
            finish_stats(nc, st, act, None, eps, root, rstd)
            normalise(st, act, y, shift, shifted, yn)

        @block.gpsimd
        def _(pool):
            for t in range(0, NT, 2):
                pool.wait_ge(yn, t + 1)
                pool.tensor_tensor(st.x[:, t, :], st.x[:, t, :], y[:, t, :], ALU.add).then_inc(x_pool, 1)

        @block.vector
        def _(dve):
            finish_stats(nc, st, None, dve, eps, root, rstd)
            find_shift(st, dve, shift, shifted)
            for t in range(NT):
                if t % 2:
                    dve.wait_ge(yn, t + 1)
                    dve.tensor_tensor(st.x[:, t, :], st.x[:, t, :], y[:, t, :], ALU.add).then_inc(x_dve, 1)
                else:
                    dve.wait_ge(x_pool, t // 2 + 1)
                if t > 0:
                    if (t - 1) % 2:
                        dve.wait_ge(x_dve, t // 2)
                    dve.bn_stats(stats[:, t - 1, :], st.x[:, t - 1, :]).then_inc(stat, 1)
            dve.wait_ge(x_dve, NT // 2)
            dve.bn_stats(stats[:, NT - 1, :], st.x[:, NT - 1, :]).then_inc(stat, 1)
            for t in range(NT):
                dve.wait_ge(stat, t + 1)
                dve.bn_aggr(st.mv[:, t, :], stats[:, t, :]).then_inc(agg, 1)
            dve.wait_ge(agg, NT)


def phase_delta_project(nc, st, w_in, qr, kvb, norms, wall, zeros):
    W = 3 * D + H
    VB = D + H
    with ExitStack() as ctx:
        sb, ps, sem = opener(nc, ctx, "dp")
        w_ld, eps, root, rstd = sem("w_ld"), sem("eps"), sem("root"), sem("rstd")
        xn_ok, xt_ps, xt_ok, proj = sem("xn"), sem("xt_ps"), sem("xt"), sem("proj")
        sq_ok, tanh_ok, q_out, k_out, v_out, b_out, ss_ok, pad_ok = (
            sem(n) for n in ("sq", "tanh", "q_out", "k_out", "v_out", "b_out", "ss", "pad"))
        xn = sb("xn", [P, 2, D])
        xt = sb("xt", [P, 2, KD, P])
        sq = sb("sq", [P, 2, 2 * D])
        th = sb("th", [P, 2, H])
        p_t = [ps(f"p_t{i}", [P, 4, P]) for i in range(2)]
        p_qk = [ps(f"p_qk{i}", [P, 2 * D]) for i in range(2)]
        p_vb = [ps(f"p_vb{i}", [P, 512]) for i in range(2)]
        block = ctx.enter_context(nc.Block())

        @block.sync
        def _(sp):
            sp.dma_start(wall[:, :, :], w_in).then_inc(w_ld, 16)
            sp.wait_ge(w_ld, 16)

        @block.vector
        def _(dve):
            dve.memset(kvb[:, :, :, KVW - 1:KVW], 0.0).then_inc(pad_ok, 1)
            dve.memset(zeros[:, :], 0.0).then_inc(pad_ok, 1)
            finish_stats(nc, st, None, dve, eps, root, rstd)

            def normalise(n, k):
                dve.wait_ge(xt_ps, n + 1)
                dve.tensor_scalar(xn[:, k % 2, :], st.x[:, ds(n, 1), :], st.mv[:, ds(n, 1), 0],
                                  st.rstd[:, ds(n, 1)], ALU.subtract, ALU.mult).then_inc(xn_ok, 1)

            def finish(n, k):
                dve.wait_ge(sq_ok, n + 1)
                dve.tensor_reduce(norms[:, ds(n, 1), :], sq[:, k % 2, :].rearrange("p (h d) -> p h d", d=DH),
                                  AX.X, ALU.add).then_inc(ss_ok, 1)
                dve.wait_ge(tanh_ok, n + 3)
                dve.tensor_scalar(kvb[:, ds(n, 1), :, 2 * DH], th[:, k % 2, :], 0.5, 0.5,
                                  ALU.mult, ALU.add).then_inc(b_out, 1)

            pipeline(dve, NT, 2, (0, normalise), (2, finish))

        @block.tensor
        def _(pe):
            pe.sem_inc(xt_ps, 2)
            pe.wait_ge(w_ld, 16)

            def transposes(n, k):
                pe.wait_ge(xn_ok, n + 1)
                pe.wait_ge(xt_ok, n + 1)
                for c in range(KD):
                    last = pe.transpose(p_t[k % 2][:, c, :], xn[:, k % 2, c * P:(c + 1) * P], st.c("ident"))
                last.then_inc(xt_ps, 1)

            def project(n, k):
                pe.wait_ge(xt_ok, n + 3)
                pe.wait_ge(k_out, n + 1)
                pe.wait_ge(tanh_ok, n + 1)
                for c in range(KD):
                    pe.matmul(p_qk[k % 2][:, :], xt[:, k % 2, c, :], wall[:, c, 0:2 * D], start=c == 0, stop=c == KD - 1)
                for c in range(KD):
                    last = pe.matmul(p_vb[k % 2][:, 0:VB], xt[:, k % 2, c, :], wall[:, c, 2 * D:W],
                                     start=c == 0, stop=c == KD - 1)
                last.then_inc(proj, 1)

            pipeline(pe, NT, 2, (0, transposes), (1, project))

        @block.scalar
        def _(act):
            finish_stats(nc, st, act, None, eps, root, rstd)
            for s in (xt_ok, k_out, ss_ok, b_out, tanh_ok, proj):
                act.sem_inc(s, 2)

            def take_xt(n, k):
                act.wait_ge(xt_ps, n + 3)
                act.wait_ge(proj, n + 1)
                act.activation(xt[:, k % 2], p_t[k % 2][:, 0:KD, :], ACT.Copy).then_inc(xt_ok, 1)

            def take(n, k):
                act.wait_ge(proj, n + 3)
                act.activation(kvb[:, ds(n, 1), :, DH:2 * DH],
                               p_vb[k % 2][:, 0:D].rearrange("p (h d) -> p h d", d=DH), ACT.Silu).then_inc(v_out, 1)
                act.wait_ge(b_out, n + 1)
                act.activation(th[:, k % 2, :], p_vb[k % 2][:, D:VB], ACT.Tanh, scale=0.5).then_inc(tanh_ok, 1)
                act.wait_ge(ss_ok, n + 1)
                act.activation(sq[:, k % 2, :], p_qk[k % 2][:, :], ACT.Square).then_inc(sq_ok, 1)
                act.activation(qr[:, ds(n, 1), :], p_qk[k % 2][:, 0:D], ACT.Copy).then_inc(q_out, 1)
                act.activation(kvb[:, ds(n, 1), :, 0:DH],
                               p_qk[k % 2][:, D:2 * D].rearrange("p (h d) -> p h d", d=DH), ACT.Copy).then_inc(k_out, 1)

            pipeline(act, NT, 2, (0, take_xt), (1, take))


def phase_delta_layout(nc, st, qr, kvb, norms, kqt, kvb_dram):
    with ExitStack() as ctx:
        sb, ps, sem = opener(nc, ctx, "dl")
        lim, root, rec, scal = sem("lim"), sem("root"), sem("rec"), sem("scal")
        n_ok, t_ps, k_back, st_d = (sem(n) for n in ("n", "t_ps", "k_back", "st"))
        taken = [sem("taken_act"), sem("taken_dve")]
        kq = sb("kq", [P, 2, 2, D])
        p_t = [[ps(f"p_t{i}{hg}", [P, 4, P]) for hg in range(HG)] for i in range(2)]
        flat = norms[:, :, :].rearrange("p t h -> p (t h)")
        block = ctx.enter_context(nc.Block())

        def take(eng, tb, b, hg):
            n, u = tb * B + b, b % 2
            eng.wait_ge(t_ps, n + 3)
            dst = kqt[:, ds(tb * CT, CT), b * HG + hg, :, :].rearrange("p c s i -> p s c i")
            src = p_t[u][hg][:, 0:2, :].rearrange("p s (c i) -> p s c i", i=C)
            for s in range(2):
                if hg == 0:
                    i = eng.activation(dst[:, s], src[:, s], ACT.Copy)
                else:
                    i = eng.tensor_copy(dst[:, s], src[:, s])
                i.then_inc(taken[hg], 1)

        @block.vector
        def _(dve):
            dve.tensor_scalar(flat, flat, 1e-24, None, ALU.max).then_inc(lim, 1)
            dve.wait_ge(root, 1)
            dve.reciprocal(flat, flat).then_inc(rec, 1)
            dve.wait_ge(rec, 1)
            dve.tensor_scalar(norms[:, :, 0:H], norms[:, :, 0:H], DH ** -0.5, None, ALU.mult).then_inc(scal, 1)
            dve.wait_ge(scal, 1)
            with dve.Fori(0, TB) as tb:
                for b in range(B):
                    n, u, t = tb * B + b, b % 2, tb + b * TB
                    dve.wait_ge(t_ps, n + 1)
                    dve.wait_ge(k_back, n + 1)
                    dve.tensor_tensor(kq[:, u, 0, :].rearrange("p (h d) -> p h d", d=DH),
                                      kvb[:, ds(t, 1), :, 0:DH],
                                      norms[:, ds(t, 1), H:2 * H].rearrange("p o h -> p (o h)").unsqueeze(2)
                                      .to_broadcast([P, H, DH]), ALU.mult).then_inc(n_ok, 1)
                    dve.tensor_tensor(kq[:, u, 1, :].rearrange("p (h d) -> p h d", d=DH),
                                      qr[:, ds(t, 1), :].rearrange("p o (h d) -> p (o h) d", d=DH),
                                      norms[:, ds(t, 1), 0:H].rearrange("p o h -> p (o h)").unsqueeze(2)
                                      .to_broadcast([P, H, DH]), ALU.mult).then_inc(n_ok, 1)
                    if b % 2:
                        for m in (b - 1, b):
                            take(dve, tb, m, 1)

        @block.tensor
        def _(pe):
            pe.sem_inc(t_ps, 2)
            with pe.Fori(0, TB) as tb:
                for b in range(B):
                    n, u = tb * B + b, b % 2
                    pe.wait_ge(n_ok, 2 * n + 2)
                    for s in taken:
                        pe.wait_ge(s, 2 * n + 1)
                    for s in range(2):
                        for hg in range(HG):
                            last = pe.transpose(p_t[u][hg][:, s, :], kq[:, u, s, hg * P:(hg + 1) * P], st.c("ident"))
                    last.then_inc(t_ps, 1)

        @block.scalar
        def _(act):
            act.sem_inc(taken[0], 3)
            act.sem_inc(taken[1], 3)
            act.wait_ge(lim, 1)
            act.activation(flat, flat, ACT.Sqrt).then_inc(root, 1)
            with act.Fori(0, TB) as tb:
                for b in range(B):
                    take(act, tb, b, 0)

        @block.gpsimd
        def _(pool):
            pool.sem_inc(k_back, 2)
            with pool.Fori(0, TB) as tb:
                for b in range(B):
                    n, u, t = tb * B + b, b % 2, tb + b * TB
                    pool.wait_ge(n_ok, 2 * n + 1)
                    pool.tensor_copy(kvb[:, ds(t, 1), :, 0:DH],
                                     kq[:, u, 0, :].rearrange("p (h d) -> p h d", d=DH)).then_inc(k_back, 1)

        @block.sync
        def _(sp):
            for tb in range(TB):
                sp.wait_ge(k_back, tb * B + B + 2)
                sp.dma_start(kvb_dram.rearrange("(b t p) h w -> p b t (h w)", b=B, p=P)[:, :, tb, :],
                             kvb[:, :, :, :].rearrange("p (b t) h w -> p b t (h w)", b=B)[:, :, tb, :]
                             ).then_inc(st_d, 16)
            sp.wait_ge(st_d, 16 * TB)


def tiles():
    for s in range(G):
        for q in range(P // Q):
            yield (2 * q + s) % G, slice(q * Q, (q + 1) * Q)


def expand(st, eng, dst, src, done):
    shape = [P, src.shape[1], 2, C]
    eng.tensor_tensor(dst, src.unsqueeze(2).to_broadcast(shape),
                      st.c("pair").unsqueeze(1).unsqueeze(3).to_broadcast(shape), ALU.mult).then_inc(done, 1)


def phase_delta_scores(nc, st, kqt, kvb_dram, mkv, att):
    with ExitStack() as ctx:
        sb, ps, sem = opener(nc, ctx, "ds")
        begun, ld_d, kbd_ok, kq_ok, s_ps, a_out, m_out, scaled = (
            sem(n) for n in ("begun", "ld", "kbd", "kq", "s_ps", "a_out", "m_out", "scaled"))
        kq = sb("kq", [P, 2, G, 2, C])
        kbd = sb("kbd", [P, 2, G, 2, C])
        p_s = [ps(f"p_s{i}", [P, G, 256]) for i in range(2)]
        att_c = att[:, :, :].rearrange("p j (c g) -> p g j c", g=G)
        block = ctx.enter_context(nc.Block())

        @block.sync
        def _(sp):
            rows = kvb_dram.rearrange("(b c j) (g h) w -> h j c b g w", b=B, j=C, g=HG)
            for h in range(HP):
                for b in range(B):
                    for hg in range(HG):
                        sp.dma_start(mkv[h * C:(h + 1) * C, :, b * HG + hg, C:C + KVW],
                                     rows[h, :, :, b, hg, :]).then_inc(ld_d, 16)
            sp.wait_ge(ld_d, 16 * HP * G)

        @block.scalar
        def _(act):
            def copy_kq(n, u):
                act.wait_ge(s_ps, n + 1)
                act.activation(kq[:, u], kqt[:, ds(n, 1), :, :, :].rearrange("p o g s i -> p (o g) s i"),
                               ACT.Copy).then_inc(kq_ok, 1)

            pipeline(act, NC_, 2, (0, copy_kq))

        @block.vector
        def _(dve):
            def expand_k(n, u):
                dve.wait_ge(s_ps, n + 1)
                expand(st, dve, kbd[:, u], kqt[:, ds(n, 1), :, 0, :].rearrange("p o g d -> p (o g) d"), kbd_ok)

            def take(n, u):
                dve.wait_ge(s_ps, n + 3)
                dve.tensor_tensor(att_c[:, :, :, ds(n, 1)].rearrange("p g j o -> p g (j o)"), p_s[u][:, :, 0:C],
                                  st.c("mask_a").unsqueeze(1).to_broadcast([P, G, C]), ALU.mult).then_inc(a_out, 1)
                dve.tensor_tensor(mkv[:, ds(n, 1), :, 0:C].rearrange("p o g i -> p (o g) i"), p_s[u][:, :, C:2 * C],
                                  st.c("mask_m").unsqueeze(1).to_broadcast([P, G, C]), ALU.mult).then_inc(m_out, 1)

            pipeline(dve, NC_, 2, (0, expand_k), (1, take))
            dve.wait_ge(a_out, NC_)
            dve.wait_ge(ld_d, 16 * HP * G)
            dve.tensor_tensor(att[:, :, :].rearrange("p j (c g) -> p j c g", g=G),
                              att[:, :, :].rearrange("p j (c g) -> p j c g", g=G),
                              mkv[:, :, :, C + 2 * DH].unsqueeze(1).to_broadcast([P, C, NC_, G]),
                              ALU.mult).then_inc(scaled, 1)

        @block.tensor
        def _(pe):
            pe.sem_inc(s_ps, 2)
            pe.sem_inc(m_out, 2)

            def scores(n, u):
                pe.wait_ge(kbd_ok, n + 1)
                pe.wait_ge(kq_ok, n + 1)
                pe.wait_ge(m_out, n + 1)
                pe.sem_inc(begun, 1)
                for g, q in tiles():
                    last = pe.matmul(p_s[u][q, g, 0:2 * C], kbd[q, u, g, :, :], kq[q, u, g, :, :],
                                     start=True, stop=True)
                last.then_inc(s_ps, 1)

            pipeline(pe, NC_, 2, (0, scores))


def phase_delta_invert(nc, st, mkv, att, zeros, xs_dram, sum_dram, zero_sem):
    JB = 4
    NB = C // JB
    HC = 2 * HP
    with ExitStack() as ctx:
        sb, ps, sem = opener(nc, ctx, "di")
        t_ps, out_a, out_v, one, back, b_out = (sem(n) for n in ("t_ps", "out_a", "out_v", "one", "back", "b_out"))
        products, rows, zero = sem("products"), sem("rows"), sem("zero")
        au = sb("au", [P, HC, C, C])
        tt = sb("tt", [P, C, HC, C])
        prod = sb("prod", [P, HC, C - 1, C - 1])
        bank = [ps(f"bank{i}", [P, JB, P]) for i in range(2 * NB)]
        block = ctx.enter_context(nc.Block())

        @block.sync
        def _(sp):
            slots = xs_dram[0:XT * P, :].rearrange("(p r) d -> p (r d)", p=P)
            w = zeros.shape[1]
            for i in range(XT * XW // w):
                sp.dma_start(slots[:, i * w:(i + 1) * w], zeros[:, :]).then_inc(zero_sem, 16)
            flat_ = sum_dram[1].rearrange("(p r) d -> p (r d)", p=P)
            for lo in range(0, flat_.shape[1], w):
                hi = min(lo + w, flat_.shape[1])
                sp.dma_start(flat_[:, lo:hi], zeros[:, 0:hi - lo]).then_inc(zero_sem, 16)
            sp.dma_start(sum_dram[0][T:T + P, :], zeros[:, 0:D]).then_inc(zero_sem, 16)

        @block.tensor
        def _(pe):
            for half in range(2):
                for jb in range(NB):
                    for j in range(JB):
                        last = pe.transpose(bank[half * NB + jb][:, j, :],
                                            att[:, jb * JB + j, half * P:(half + 1) * P], st.c("ident"))
                    last.then_inc(t_ps, 1)
            pe.wait_ge(rows, C - 1)
            pe.wait_ge(one, C)
            for half in range(2):
                pe.wait_ge(out_a, (half + 1) * NB // 2)
                pe.wait_ge(out_v, (half + 1) * NB // 2)
                for ib in range(NB):
                    for i in range(JB):
                        last = pe.transpose(bank[half * NB + ib][:, i, :],
                                            tt[:, ib * JB + i, half * HP:(half + 1) * HP, :], st.c("ident"))
                    last.then_inc(back, 1)

        def spread(eng, n, done):
            half, jb = n // NB, n % NB
            eng.wait_ge(t_ps, n + 1)
            dst = au[:, half * HP:(half + 1) * HP, :, jb * JB:(jb + 1) * JB].rearrange("p h i j -> p j (h i)")
            i = eng.activation(dst, bank[n][:, :, :], ACT.Copy) if done is out_a else eng.tensor_copy(
                dst, bank[n][:, :, :])
            i.then_inc(done, 1)

        @block.scalar
        def _(act):
            for n in range(0, 2 * NB, 2):
                spread(act, n, out_a)

        @block.gpsimd
        def _(pool):
            pool.memset(tt[:, :, :, :], 0.0).then_inc(zero, 1)
            pool.wait_ge(zero, 1)
            for i in range(C):
                pool.memset(tt[:, i, :, i], 1.0).then_inc(one, 1)

        @block.vector
        def _(dve):
            for n in range(1, 2 * NB, 2):
                spread(dve, n, out_v)
            dve.wait_ge(out_a, NB)
            dve.wait_ge(out_v, NB)
            dve.wait_ge(one, C)
            for i in range(1, C):
                terms = prod[:, :, 0:i, 0:i]
                if i > 1:
                    dve.wait_ge(rows, i - 1)
                dve.tensor_tensor(terms, au[:, :, i, 0:i].unsqueeze(2).to_broadcast([P, HC, i, i]),
                                  tt[:, 0:i, :, 0:i].rearrange("p m h j -> p h j m"), ALU.mult).then_inc(products, 1)
                dve.wait_ge(products, i)
                dve.tensor_reduce(tt[:, i, :, 0:i], terms, AX.X, ALU.add).then_inc(rows, 1)
            for n in range(2 * NB):
                half, ib = n // NB, n % NB
                dve.wait_ge(back, n + 1)
                beta = mkv[:, :, :, C + 2 * DH].rearrange("p c g -> p (c g)")[:, half * P:(half + 1) * P]
                dve.tensor_tensor(att[:, ib * JB:(ib + 1) * JB, half * P:(half + 1) * P], bank[n][:, :, :],
                                  beta.unsqueeze(1).to_broadcast([P, JB, P]), ALU.mult).then_inc(b_out, 1)


def phase_delta_wy(nc, st, kqt, mkv, att, xt):
    with ExitStack() as ctx:
        sb, ps, sem = opener(nc, ctx, "dw")
        begun, tb_ok, mk_ok, w_ps, w_out, wv_out, wk_ok, x_ps, q_out, i_out = (
            sem(n) for n in ("begun", "tb", "mk", "w_ps", "w_out", "wv_out", "wk", "x_ps", "q_out", "i_out"))
        mk = sb("mk", [P, 4, G, C + 2 * DH])
        tbd = sb("tbd", [P, 2, G, 2, C])
        wkd = sb("wkd", [P, 2, G, 2, C])
        wc = sb("wc", [P, 2, G, DH])
        p_w, p_x = (ps(n, [P, G, 256]) for n in ("p_w", "p_x"))
        att_c = att[:, :, :].rearrange("p j (c g) -> p g j c", g=G)

        block = ctx.enter_context(nc.Block())

        @block.gpsimd
        def _(pool):
            def expand_t(n, u):
                pool.wait_ge(w_ps, n + 1)
                expand(st, pool, tbd[:, u], att_c[:, :, :, ds(n, 1)].rearrange("p g j o -> p g (j o)"), tb_ok)

            pipeline(pool, NC_, 2, (0, expand_t))

        @block.scalar
        def _(act):
            act.sem_inc(wk_ok, 2)
            act.sem_inc(wv_out, 1)

            def copy_mk(n, u):
                act.wait_ge(x_ps, n + 1)
                act.activation(mk[:, u], mkv[:, ds(n, 1), :, 0:C + 2 * DH].rearrange("p o g w -> p (o g) w"),
                               ACT.Copy).then_inc(mk_ok, 1)

            def take_w(n, u):
                act.wait_ge(w_ps, n + 3)
                act.wait_ge(wk_ok, n + 1)
                act.activation(wc[:, u % 2], p_w[:, :, 0:DH], ACT.Copy).then_inc(w_out, 1)
                act.activation(mkv[:, ds(n, 1), :, C + DH:C + 2 * DH].rearrange("p o g v -> p (o g) v"),
                               p_w[:, :, DH:2 * DH], ACT.Copy).then_inc(wv_out, 1)

            pipeline(act, NC_, 4, (0, copy_mk), (1, take_w))

        @block.vector
        def _(dve):
            dve.sem_inc(x_ps, 4)

            def expand_w(n, u):
                dve.wait_ge(w_out, n + 1)
                dve.wait_ge(x_ps, n + 3)
                expand(st, dve, wkd[:, u % 2], wc[:, u % 2], wk_ok)

            def take_x(n, u):
                dve.wait_ge(x_ps, n + 5)
                dst = xt[:, ds(n, 1), :, :, :].rearrange("p o g s i -> p (o g) s i")
                dve.tensor_tensor(dst[:, :, 0, :], kqt[:, ds(n, 1), :, 1, :].rearrange("p o g i -> p (o g) i"),
                                  p_x[:, :, 0:C], ALU.subtract).then_inc(q_out, 1)
                dve.tensor_tensor(dst[:, :, 1, :], st.c("eye16").unsqueeze(1).to_broadcast([P, G, DH]),
                                  p_x[:, :, C:2 * C], ALU.subtract).then_inc(i_out, 1)

            pipeline(dve, NC_, 4, (1, expand_w), (2, take_x))

        @block.tensor
        def _(pe):
            pe.sem_inc(w_ps, 2)
            pe.sem_inc(i_out, 1)

            def w_part(n, u):
                pe.wait_ge(tb_ok, n + 1)
                pe.wait_ge(mk_ok, n + 1)
                pe.wait_ge(wv_out, n + 1)
                pe.sem_inc(begun, 1)
                for g, q in tiles():
                    last = pe.matmul(p_w[q, g, 0:2 * DH], tbd[q, u % 2, g, :, :], mk[q, u, g, C:C + 2 * DH],
                                     start=True, stop=True)
                last.then_inc(w_ps, 1)

            def x_part(n, u):
                pe.wait_ge(wk_ok, n + 3)
                pe.wait_ge(i_out, n + 1)
                pe.sem_inc(begun, 1)
                for g, q in tiles():
                    last = pe.matmul(p_x[q, g, 0:C + DH], wkd[q, u % 2, g, :, :], mk[q, u, g, 0:C + DH],
                                     start=True, stop=True)
                last.then_inc(x_ps, 1)

            pipeline(pe, NC_, 4, (0, w_part), (1, x_part))


def phase_delta_chain(nc, st, mkv, xt, ot):
    N = 2 * DH + C
    with ExitStack() as ctx:
        sb, ps, sem = opener(nc, ctx, "dc")
        km_ok, xx_ok, wv_ok, s_ok, r_ps, o_out = (sem(n) for n in ("km", "xx", "wv", "s", "r_ps", "o_out"))
        km_k, xx_p, begun = sem("km_k"), sem("xx_p"), sem("begun")
        km = sb("km", [P, 2, G, N])
        xx = sb("xx", [P, 2, G, N])
        wvd = sb("wvd", [P, 2, G, 2, DH])
        s = sb("s", [P, 2, G, 2 * DH])
        p_r = [ps(f"p_r{i}", [P, G, 256]) for i in range(2)]

        def pair(t):
            return t[:, :, 0:2 * DH].rearrange("p g (s i) -> p g s i", s=2)

        def part(t, n, lo):
            return t[:, ds(n, 1), :, lo:lo + C].rearrange("p o g i -> p (o g) i")

        def xt_part(n, k):
            return xt[:, ds(n, 1), :, k, :].rearrange("p o g i -> p (o g) i")

        block = ctx.enter_context(nc.Block())

        @block.gpsimd
        def _(pool):
            with pool.Fori(0, NC_ // 2) as cc:
                for u in range(2):
                    n = 2 * cc + u
                    pool.wait_ge(r_ps, n + 1)
                    expand(st, pool, pair(km[:, u]), part(mkv, n, C), km_k)
                    expand(st, pool, wvd[:, u], part(mkv, n, C + DH), wv_ok)

        def ahead(eng, prepare, finish):
            prepare(0, 0)
            with eng.Fori(0, NC_ // 2 - 1) as cc:
                for u in range(2):
                    prepare(2 * cc + u + 1, 1 - u)
                    finish(2 * cc + u, u)
            prepare(NC_ - 1, 1)
            finish(NC_ - 2, 0)
            finish(NC_ - 1, 1)

        @block.vector
        def _(dve):
            def prepare(n, u):
                dve.wait_ge(r_ps, n + 1)
                expand(st, dve, pair(xx[:, u]), xt_part(n, 1), xx_p)

            def turn(n, u):
                dve.wait_ge(r_ps, n + 3)
                dve.transpose(s[:, 1 - u], p_r[u][:, :, 0:2 * DH]).then_inc(s_ok, 1)

            dve.memset(s[:, 0], 0.0).then_inc(s_ok, 1)
            ahead(dve, prepare, turn)

        @block.scalar
        def _(act):
            def prepare(n, u):
                act.wait_ge(r_ps, n + 1)
                act.activation(km[:, u, :, 2 * DH:N], part(mkv, n, 0), ACT.Copy).then_inc(km_ok, 1)
                act.activation(xx[:, u, :, 2 * DH:N], xt_part(n, 0), ACT.Copy).then_inc(xx_ok, 1)

            def take(n, u):
                act.wait_ge(s_ok, n + 2)
                act.activation(ot[:, :, :, ds(n * C, C)].rearrange("p g b i -> p b g i"),
                               p_r[u][:, :, 2 * DH:N].rearrange("p (b g) i -> p b g i", g=HG),
                               ACT.Copy).then_inc(o_out, 1)

            ahead(act, prepare, take)

        @block.tensor
        def _(pe):
            pe.sem_inc(r_ps, 2)
            pe.sem_inc(o_out, 2)

            with pe.Fori(0, NC_ // 2) as cc:
                for u in range(2):
                    n = 2 * cc + u
                    for done in (km_k, wv_ok, km_ok):
                        pe.wait_ge(done, n + 1)
                    pe.wait_ge(o_out, n + 1)
                    pe.sem_inc(begun, 1)
                    for g, q in tiles():
                        pe.matmul(p_r[u][q, g, 0:N], wvd[q, u, g, :, :], km[q, u, g, :], start=g % 2 == 0, stop=False)
                    pe.wait_ge(xx_p, n + 1)
                    pe.wait_ge(xx_ok, n + 1)
                    pe.wait_ge(s_ok, n + 1)
                    pe.sem_inc(begun, 1)
                    for g, q in tiles():
                        last = pe.matmul(p_r[u][q, g, 0:N], s[q, u, g, :], xx[q, u, g, :], start=False, stop=g % 2 == 1)
                    last.then_inc(r_ps, 1)


def phase_delta_out(nc, st, ot, wo_in, onw_in, y):
    with ExitStack() as ctx:
        sb, ps, sem = opener(nc, ctx, "do")
        w_ld, sq_ok, ms_ps, eps_ok, root, rec, on_ok, y_ps, y_ok, stat, agg = (
            sem(n) for n in ("w_ld", "sq", "ms_ps", "eps", "root", "rec", "on", "y_ps", "y", "stat", "agg"))
        wo = sb("wo", [P, HG, D])
        onw = sb("onw", [P, 1])
        eps = sb("eps", [P, 1])
        sq = sb("sq", [P, 2, HG, L])
        r = sb("r", [P, 2, HG, L])
        on = sb("on", [P, 2, HG, L])
        stats = sb("stats", [P, NT, 6])
        p_ms = [ps(f"p_ms{g}", [P, L]) for g in range(HG)]
        p_y = [ps(f"p_y{t}", [P, 512]) for t in range(TB)]
        block = ctx.enter_context(nc.Block())

        def outputs(b, g):
            return ot[:, g, ds(b, 1), :].rearrange("p o l -> p (o l)")

        def result(n):
            return y[:, ds(n, 1), :].rearrange("p o d -> p (o d)")

        @block.sync
        def _(sp):
            sp.dma_start(wo[:, :, :], wo_in).then_inc(w_ld, 16)
            sp.dma_start(onw[:, :], onw_in).then_inc(w_ld, 16)
            sp.wait_ge(w_ld, 32)

        @block.scalar
        def _(act):
            act.sem_inc(root, HG)
            act.wait_ge(eps_ok, 1)

            def square(b, u):
                for g in range(HG):
                    act.wait_ge(ms_ps, HG * b + g + 1)
                    act.activation(sq[:, u, g, :], outputs(b, g), ACT.Square).then_inc(sq_ok, 1)

            def take_root(b, u):
                for g in range(HG):
                    act.wait_ge(ms_ps, HG * b + g + 2 * HG + 1)
                    act.wait_ge(on_ok, HG * b + g + 1)
                    act.activation(r[:, u, g, :], p_ms[g][:, :], ACT.Sqrt, bias=eps[:, :]).then_inc(root, 1)

            def take_y(b, u):
                for t in range(TB):
                    act.wait_ge(y_ps, TB * b + 2 * TB + t + 1)
                    act.activation(result(TB * b + t), p_y[t][:, 0:D], ACT.Copy).then_inc(y_ok, 1)

            pipeline(act, B, 2, (0, square), (0, take_root), (1, take_y))

        @block.vector
        def _(dve):
            dve.sem_inc(on_ok, 2 * HG)
            dve.memset(eps[:, :], EPS).then_inc(eps_ok, 1)
            dve.wait_ge(w_ld, 32)

            def normalise(b, u):
                for g in range(HG):
                    dve.wait_ge(root, HG * b + g + HG + 1)
                    dve.reciprocal(r[:, u, g, :], r[:, u, g, :]).then_inc(rec, 1)
                for g in range(HG):
                    dve.wait_ge(rec, HG * b + g + 1)
                    dve.wait_ge(y_ps, TB * b + TB)
                    dve.scalar_tensor_tensor(on[:, u, g, :], outputs(b, g), onw[:, 0:1], r[:, u, g, :],
                                             ALU.mult, ALU.mult).then_inc(on_ok, 1)

            def take_stats(b, u):
                for t in range(TB):
                    dve.wait_ge(y_ok, TB * b + TB + t + 1)
                    dve.bn_stats(stats[:, ds(TB * b + t, 1), :].rearrange("p o s -> p (o s)"),
                                 result(TB * b + t)).then_inc(stat, 1)

            pipeline(dve, B, 2, (0, normalise), (1, take_stats))
            dve.wait_ge(stat, NT)
            for n in range(NT):
                dve.bn_aggr(st.mv[:, n, :], stats[:, n, :]).then_inc(agg, 1)

        @block.tensor
        def _(pe):
            pe.sem_inc(ms_ps, 2 * HG)
            pe.sem_inc(y_ps, 2 * TB)
            pe.sem_inc(y_ok, TB)
            pe.wait_ge(w_ld, 32)

            def mean_squares(b, u):
                for g in range(HG):
                    pe.wait_ge(sq_ok, HG * b + g + 1)
                    pe.wait_ge(root, HG * b + g + 1)
                    pe.matmul(p_ms[g][:, :], st.c("mean_blk"), sq[:, u, g, :], start=True, stop=True).then_inc(ms_ps, 1)

            def project(b, u):
                pe.wait_ge(on_ok, HG * b + 3 * HG)
                for t in range(TB):
                    pe.wait_ge(y_ok, TB * b + t + 1)
                    for g in range(HG):
                        last = pe.matmul(p_y[t][:, 0:D], on[:, u, g, t * P:(t + 1) * P], wo[:, g, :],
                                         start=g == 0, stop=g == HG - 1)
                    last.then_inc(y_ps, 1)

            pipeline(pe, B, 2, (0, mean_squares), (1, project))


class Routing:

    def __init__(self, nc, ctx):
        def sb(name, shape, dt=F32):
            return ctx.enter_context(nc.sbuf_tensor(f"rt_{name}", shape, dt))

        self.top = sb("top", [P, NT, 8])
        self.hot = sb("hot", [P, NT, TOPK, NE], BF16)
        self.sel = sb("sel", [P, NT, NE], BF16)
        self.cum = sb("cum", [P, NT + 1, NE], BF16)
        self.erow = sb("erow", [1, XT], I32)
        self.new = sb("new", [1, XT], I32)
        self.slot = sb("slot", [1, XT], I32)


def phase_route(nc, st, rt, wr_in, xna, xt_all):
    with ExitStack() as ctx:
        sb, ps, sem = opener(nc, ctx, "ro")
        w_ld, eps, root, rstd = sem("w_ld"), sem("eps"), sem("root"), sem("rstd")
        xn_ok, xs_ok, xt_ps, xt_ok, l_ps, mx_ok, e_ok, rec, sc_ok, begun, top_ok, kept, idx_ok, idf_ok, hot_ok, sel_ok, cum_ok = (
            sem(n) for n in ("xn", "xs", "xt_ps", "xt", "l_ps", "mx", "e", "rec", "sc", "begun", "top", "kept", "idx", "idf", "hot",
                             "sel", "cum"))
        number_ok, xall_ok = sem("number"), sem("xall")
        wr = sb("wr", [P, KD, NE])
        xn = sb("xn", [P, 2, D])
        xt = sb("xt", [P, 2, KD, P])
        nm = sb("nm", [P, 2, 1])
        e = sb("e", [P, 2, NE])
        se = sb("se", [P, 2, 1])
        sc = sb("sc", [P, 2, NE])
        top = sb("top", [P, 2, 8])
        idx = sb("idx", [P, 2, 8], U32)
        idf = sb("idf", [P, 2, 8])
        p_t = [ps(f"p_t{i}", [P, 4, P]) for i in range(2)]
        p_l = [ps(f"p_l{i}", [P, 512]) for i in range(2)]
        block = ctx.enter_context(nc.Block())

        def tile(t, ap):
            return ap[:, ds(t, 1)]

        @block.sync
        def _(sp):
            sp.dma_start(wr[:, :, :], wr_in).then_inc(w_ld, 16)
            sp.wait_ge(w_ld, 16)

        @block.vector
        def _(dve):
            dve.sem_inc(mx_ok, 2)
            dve.sem_inc(sc_ok, 2)
            dve.sem_inc(xt_ps, 2)
            finish_stats(nc, st, None, dve, eps, root, rstd)
            dve.memset(rt.cum[:, 0, :], 0.0).then_inc(cum_ok, 1)

            def normalise(n, u):
                dve.wait_ge(xt_ps, n + 1)
                dve.wait_ge(xs_ok, n + 1)
                dve.tensor_scalar(xn[:, u, :], tile(n, st.x), st.mv[:, ds(n, 1), 0], st.rstd[:, ds(n, 1)],
                                  ALU.subtract, ALU.mult).then_inc(xn_ok, 1)

            def row_max(n, u):
                dve.wait_ge(l_ps, n + 1)
                dve.wait_ge(e_ok, n + 1)
                dve.tensor_reduce(nm[:, u, :], p_l[u][:, 0:NE], AX.X, ALU.max, negate=True).then_inc(mx_ok, 1)

            def invert(n, u):
                dve.wait_ge(e_ok, n + 3)
                dve.reciprocal(se[:, u, :], se[:, u, :]).then_inc(rec, 1)

            def scale(n, u):
                dve.wait_ge(rec, n + 1)
                dve.tensor_scalar(sc[:, u, :], e[:, u, :], se[:, u, :], None, ALU.mult).then_inc(sc_ok, 1)

            def largest(n, u):
                dve.wait_ge(sc_ok, n + 3)
                dve.sem_inc(begun, 1)
                dve.max(top[:, u, :], sc[:, u, :]).then_inc(top_ok, 1)

            def index(n, u):
                dve.wait_ge(top_ok, n + 1)
                dve.tensor_scalar(tile(n, rt.top).rearrange("p o k -> p (o k)"), top[:, u, :], 1.0, None,
                                  ALU.mult).then_inc(kept, 1)
                dve.max_index(idx[:, u, :], top[:, u, :], sc[:, u, :]).then_inc(idx_ok, 1)

            def to_float(n, u):
                dve.wait_ge(idx_ok, n + 1)
                dve.tensor_copy(idf[:, u, :], idx[:, u, :]).then_inc(idf_ok, 1)

            def one_hot(n, u):
                dve.wait_ge(idf_ok, n + 1)
                dve.tensor_tensor(tile(n, rt.hot).rearrange("p o k e -> p (o k) e"),
                                  idf[:, u, 0:TOPK].unsqueeze(2).to_broadcast([P, TOPK, NE]),
                                  st.c("iota_e").unsqueeze(1).to_broadcast([P, TOPK, NE]),
                                  ALU.is_equal).then_inc(hot_ok, 1)

            def any_choice(n, u):
                dve.wait_ge(hot_ok, n + 1)
                with nc.allow_low_precision("zeros and ones"):
                    dve.tensor_reduce(tile(n, rt.sel).rearrange("p o e -> p (o e)"),
                                      tile(n, rt.hot).rearrange("p o k e -> p e (o k)"), AX.X, ALU.add).then_inc(sel_ok, 1)

            def add_up(n, u):
                dve.wait_ge(sel_ok, n + 1)
                dve.wait_ge(cum_ok, n + 1)
                dve.tensor_tensor(tile(n + 1, rt.cum), tile(n, rt.cum), tile(n, rt.sel),
                                  ALU.add).then_inc(cum_ok, 1)

            pipeline(dve, NT, 2, (3, invert), (4, index), (0, normalise), (3, scale), (4, to_float), (2, row_max),
                     (3, largest), (4, one_hot), (5, any_choice), (6, add_up))

        @block.gpsimd
        def _(pool):
            pool.sem_inc(xs_ok, 2)
            pool.tensor_copy(xna[:, :, D], st.c("number")).then_inc(number_ok, 1)

            def copy(n, u):
                pool.wait_ge(xn_ok, n + 1)
                pool.tensor_copy(xna[:, ds(n, 1), 0:D].rearrange("p o d -> p (o d)"), xn[:, u, :]).then_inc(xs_ok, 1)

            pipeline(pool, NT, 2, (0, copy))

        @block.tensor
        def _(pe):
            pe.wait_ge(w_ld, 16)

            def transposes(n, u):
                pe.wait_ge(xn_ok, n + 1)
                pe.wait_ge(xall_ok, n + 1)
                for c in range(KD):
                    last = pe.transpose(p_t[u][:, c, :], xn[:, u, c * P:(c + 1) * P], st.c("ident"))
                last.then_inc(xt_ps, 1)

            def logits(n, u):
                pe.wait_ge(xt_ok, n + 1)
                pe.wait_ge(mx_ok, n + 1)
                pe.wait_ge(e_ok, n + 1)
                for c in range(KD):
                    last = pe.matmul(p_l[u][:, 0:NE], xt[:, u, c, :], wr[:, c, :], start=c == 0, stop=c == KD - 1)
                last.then_inc(l_ps, 1)

            pipeline(pe, NT, 2, (0, transposes), (1, logits))

        @block.scalar
        def _(act):
            finish_stats(nc, st, act, None, eps, root, rstd)
            act.sem_inc(xall_ok, 2)
            act.sem_inc(e_ok, 2)

            def take_x(n, u):
                act.wait_ge(xt_ps, n + 3)
                act.wait_ge(mx_ok, n + 1)
                act.activation(xt[:, u], p_t[u][:, 0:KD, :], ACT.Copy).then_inc(xt_ok, 1)

            def keep_x(n, u):
                act.activation(xt_all[:, :, ds(n * P, P)], p_t[u][:, 0:KD, :], ACT.Copy).then_inc(xall_ok, 1)

            def exponentials(n, u):
                act.wait_ge(mx_ok, n + 3)
                act.wait_ge(sc_ok, n + 1)
                act.activation(e[:, u, :], p_l[u][:, 0:NE], ACT.Exp, bias=nm[:, u, :],
                               accum_out=se[:, u, :]).then_inc(e_ok, 1)

            pipeline(act, NT, 2, (0, take_x), (1, exponentials), (0, keep_x))


def phase_dispatch(nc, st, rt, xna, xt, w_in, y, xs_dram, sum_dram, zero_sem, n_zero):
    SB = 4
    widths = [slice(c * P, min((c + 1) * P, FE)) for c in range(KF)]
    with ExitStack() as ctx:
        sb, ps, sem = opener(nc, ctx, "dp2")
        cnt_ps, gt_ok, til_ok, scan_ok, base_ok, cmp_ok, ecol_ok, erow_ps, erf_ok, er_ok, new_ok = (
            sem(n) for n in ("cnt", "gt", "til", "scan", "base", "cmp", "ecol", "erow_ps", "erf", "er", "new"))
        begun, r_ps, posf_ok, prod_ok, pos_ok, posu_ok, stg_ok, sent = (
            sem(n) for n in ("begun", "r_ps", "posf", "prod", "pos", "posu", "stg", "sent"))
        pe_begun, w_ld, gv_ps, sg_ok, h_ok, y_ps, y_out, put = (
            sem(n) for n in ("pe_begun", "w_ld", "gv_ps", "sg", "h", "y_ps", "y_out", "put"))
        scat = [sem(f"scat{i}") for i in range(SB)]
        gt = sb("gt", [P, NE, 16])
        til = sb("til", [P, NE])
        scan = sb("scan", [P, NE])
        base = sb("base", [P, NE])
        cmp_ = sb("cmp", [P, 2, NE])
        ecol = sb("ecol", [P, 2])
        erf = sb("erf", [1, XT])
        new = sb("new", [1, XT])
        run_ = sb("run", [1, XT])
        runi = sb("runi", [1, XT], I32)
        one = sb("one", [1, XT])
        posf = sb("posf", [P, NT, NE])
        prod = sb("prod", [P, SB, TOPK, NE])
        pos = sb("pos", [P, SB, 8])
        posu = [sb(f"posu{i}", [P, 8], U32) for i in range(SB)]
        stg = [sb(f"stg{i}", [P, XW]) for i in range(SB)]
        ws = sb("w_shared", [P, WX])
        sg = sb("sg", [P, L])
        h = sb("h", [P, KF, L])
        p_c, p_e, p_g, p_v = (ps(n, [P, 512]) for n in ("p_c", "p_e", "p_g", "p_v"))
        p_r = [ps(f"p_r{i}", [P, NT // 2, NE]) for i in range(2)]
        p_y = [ps(f"p_y{i}", [P, 512]) for i in range(2)]
        block = ctx.enter_context(nc.Block())

        @block.sync
        def _(sp):
            sp.dma_start(ws[:, :], w_in[NE]).then_inc(w_ld, 16)
            for b in range(B):
                sp.wait_ge(y_out, TB * (b + 1) + 2)
                sp.dma_start(sum_dram[0][b * L:(b + 1) * L, :].rearrange("(t p) d -> p t d", p=P),
                             y[:, b * TB:(b + 1) * TB, :]).then_inc(put, 16)
            sp.wait_ge(put, 16 * B)

        @block.tensor
        def _(pe):
            pe.sem_inc(sent, SB)
            pe.sem_inc(h_ok, 1)
            pe.sem_inc(y_out, 2)
            pe.matmul(p_c[:, 0:NE], st.cb[:, 3, :], rt.cum[:, NT, :], start=True, stop=True).then_inc(cnt_ps, 1)
            for i in range(2):
                half = slice(i * NT // 2, (i + 1) * NT // 2)
                pe.matmul(p_r[i][:, :, :], st.cb[:, 3, :], rt.cum[:, half, :], start=True, stop=False)
                pe.matmul(p_r[i][:, :, :], st.cb[:, 2, :], rt.sel[:, half, :], start=False, stop=True).then_inc(r_ps, 1)
            pe.wait_ge(w_ld, 16)

            def gate_value(n, c):
                pe.wait_ge(h_ok, 2 * n + c + 1)
                pe.sem_inc(pe_begun, 1)
                for v, bank in enumerate((p_g, p_v)):
                    for k in range(KD):
                        lo = (2 * k + v) * FE
                        last = pe.matmul(bank[0:widths[c].stop - widths[c].start, 0:L],
                                         ws[:, lo + widths[c].start:lo + widths[c].stop], xt[:, k, ds(n * L, L)],
                                         start=k == 0, stop=k == KD - 1)
                last.then_inc(gv_ps, 1)

            def output(n, u):
                pe.wait_ge(h_ok, 2 * n + 3)
                for t in range(TB):
                    pe.wait_ge(y_out, TB * n + t + 1)
                    for c in range(KF):
                        m = widths[c].stop - widths[c].start
                        lo = KD * 2 * FE + c * D
                        last = pe.matmul(p_y[t % 2][:, 0:D], h[0:m, c, t * P:(t + 1) * P], ws[0:m, lo:lo + D],
                                         start=c == 0, stop=c == KF - 1)
                    last.then_inc(y_ps, 1)

            pipeline(pe, B, 1, (0, lambda n, u: gate_value(n, 0)), (1, output), (0, lambda n, u: gate_value(n, 1)))
            pe.wait_ge(ecol_ok, 2)
            for i in range(2):
                last = pe.matmul(p_e[0:1, i * P:(i + 1) * P], ecol[:, i:i + 1], st.c("ident"), start=True, stop=True)
            last.then_inc(erow_ps, 1)

        @block.vector
        def _(dve):
            dve.sem_inc(y_ps, 1)
            dve.wait_ge(cnt_ps, 1)
            dve.tensor_tensor(gt[:, :, :], p_c[:, 0:NE].unsqueeze(2).to_broadcast([P, NE, 16]),
                              st.c("k128").unsqueeze(1).to_broadcast([P, NE, 16]), ALU.is_gt).then_inc(gt_ok, 1)
            dve.wait_ge(gt_ok, 1)
            dve.tensor_reduce(til[:, :], gt[:, :, :], AX.X, ALU.add).then_inc(til_ok, 1)
            dve.wait_ge(til_ok, 1)
            dve.tensor_tensor_scan(scan[:, :], st.c("ones")[:, 0:NE], til[:, :], 0.0, ALU.mult,
                                   ALU.add).then_inc(scan_ok, 1)
            dve.wait_ge(scan_ok, 1)
            dve.tensor_tensor(base[:, :], scan[:, :], til[:, :], ALU.subtract).then_inc(base_ok, 1)
            dve.wait_ge(base_ok, 1)
            dve.tensor_scalar(base[:, :], base[:, :], float(P), None, ALU.mult).then_inc(base_ok, 1)
            dve.wait_ge(base_ok, 2)
            for i in range(2):
                dve.wait_ge(r_ps, i + 1)
                dve.tensor_tensor(posf[:, i * NT // 2:(i + 1) * NT // 2, :], p_r[i][:, :, :],
                                  base[:, :].unsqueeze(1).to_broadcast([P, NT // 2, NE]), ALU.add).then_inc(posf_ok, 1)
            dve.wait_ge(posf_ok, 2)

            def slots(n, u):
                dve.tensor_tensor(prod[:, u], rt.hot[:, ds(n, 1)].rearrange("p o k e -> p (o k) e"),
                                  posf[:, ds(n, 1), :].to_broadcast([P, TOPK, NE]), ALU.mult).then_inc(prod_ok, 1)
                dve.wait_ge(prod_ok, n + 1)
                dve.tensor_reduce(pos[:, u, 0:TOPK], prod[:, u], AX.X, ALU.add).then_inc(pos_ok, 1)
                dve.wait_ge(pos_ok, n + 1)
                dve.wait_ge(sent, n + 1)
                dve.tensor_copy(posu[u][:, 0:TOPK], pos[:, u, 0:TOPK]).then_inc(posu_ok, 1)
                dve.tensor_copy(stg[u][:, D + 1:D + 1 + TOPK], pos[:, u, 0:TOPK]).then_inc(posu_ok, 1)

            def product(n, c):
                m = widths[c].stop - widths[c].start
                dve.wait_ge(sg_ok, 2 * n + c + 1)
                dve.wait_ge(y_ps, TB * n + 1)
                dve.tensor_tensor(h[0:m, c, :], sg[0:m, :], p_v[0:m, 0:L], ALU.mult).then_inc(h_ok, 1)

            with dve.Fori(0, B) as b:
                for c in range(KF):
                    for u in range(SB // 2):
                        slots(SB * b + c * SB // 2 + u, c * SB // 2 + u)
                    product(b, c)
            for i in range(2):
                dve.tensor_scalar(cmp_[:, i, :], scan[:, :], st.c("iota_p")[:, i:i + 1], None,
                                  ALU.is_le).then_inc(cmp_ok, 1)
                dve.wait_ge(cmp_ok, i + 1)
                dve.tensor_reduce(ecol[:, i:i + 1], cmp_[:, i, :], AX.X, ALU.add).then_inc(ecol_ok, 1)
            dve.wait_ge(erow_ps, 1)
            dve.tensor_scalar(erf[:, :], p_e[0:1, 0:XT], float(NE - 1), None, ALU.min).then_inc(erf_ok, 1)
            dve.wait_ge(erf_ok, 1)
            dve.tensor_copy(rt.erow[:, :], erf[:, :]).then_inc(er_ok, 1)
            dve.memset(new[:, 0:1], 1.0).then_inc(new_ok, 1)
            dve.tensor_tensor(new[:, 1:XT], erf[:, 1:XT], erf[:, 0:XT - 1], ALU.not_equal).then_inc(new_ok, 1)
            dve.memset(one[:, :], 1.0).then_inc(new_ok, 1)
            dve.wait_ge(new_ok, 3)
            dve.tensor_copy(rt.new[:, :], new[:, :]).then_inc(er_ok, 1)
            dve.tensor_tensor_scan(run_[:, :], one[:, :], new[:, :], 0.0, ALU.mult, ALU.add).then_inc(new_ok, 1)
            dve.wait_ge(new_ok, 4)
            dve.tensor_copy(runi[:, :], run_[:, :]).then_inc(new_ok, 1)
            dve.wait_ge(new_ok, 5)
            dve.tensor_scalar(rt.slot[:, :], runi[:, :], NW - 1, None, ALU.bitwise_and).then_inc(er_ok, 1)

        @block.scalar
        def _(act):
            def stage(n, u):
                act.wait_ge(sent, n + 1)
                act.activation(stg[u][:, 0:D + 1], xna[:, ds(n, 1), :].rearrange("p o d -> p (o d)"),
                               ACT.Copy).then_inc(stg_ok, 1)
                act.activation(stg[u][:, D + 1 + TOPK:XW], rt.top[:, ds(n, 1), 0:TOPK].rearrange("p o k -> p (o k)"),
                               ACT.Copy).then_inc(stg_ok, 1)

            def gate(n, c):
                m = widths[c].stop - widths[c].start
                act.wait_ge(gv_ps, 2 * n + c + 1)
                act.activation(sg[0:m, :], p_g[0:m, 0:L], ACT.Silu).then_inc(sg_ok, 1)

            def half(c):
                def both(n, _):
                    for u in range(SB // 2):
                        stage(SB * n + c * SB // 2 + u, c * SB // 2 + u)
                    gate(n, c)
                return both

            def take_y(n, _):
                for t in range(TB):
                    act.wait_ge(y_ps, TB * n + t + 2)
                    act.activation(y[:, ds(TB * n + t, 1), :].rearrange("p o d -> p (o d)"), p_y[t % 2][:, 0:D],
                                   ACT.Copy).then_inc(y_out, 1)

            pipeline(act, B, 1, (0, half(0)), (1, take_y), (0, half(1)))

        @block.gpsimd
        def _(pool):
            pool.wait_ge(zero_sem, 16 * n_zero)

            def send(n, u):
                pool.wait_ge(posu_ok, 2 * n + 2)
                pool.wait_ge(stg_ok, 2 * n + 2)
                pool.sem_inc(begun, 1)
                for k in range(TOPK):
                    pool.indirect_dma_start(xs_dram, bass.IndirectOffsetOnAxis(posu[u][:, k:k + 1], 0),
                                            stg[u][:, :], None).then_inc(scat[u], 16)

            def release(n, u):
                pool.wait_ge(scat[u], 16 * TOPK // SB * (n - u) + 16 * TOPK)
                pool.sem_inc(sent, 1)

            pipeline(pool, NT, SB, (0, send), (2, release))


def phase_experts(nc, st, rt, xs_dram, sum_dram, zero_sem, n_zero, w_in):
    NB = 4
    YB = 8
    with ExitStack() as ctx:
        sb, ps, sem = opener(nc, ctx, "ex")
        ld_w = [sem(f"ld_w{i}") for i in range(NW)]
        ld_x = [sem(f"ld_x{i}") for i in range(NB)]
        added = [sem(f"added{i}") for i in range(2)]
        y_free, begun, mine_ok, part_ok, score_ok, none_ok, idx_ok = (
            sem(n) for n in ("y_free", "begun", "mine", "part", "score", "none", "idx"))
        xt_ps, xt_ok, gv_ps, sg_ok, h_ok, ht_ps, ht_ok, y_ps, y_ok, pad_ok = (
            sem(n) for n in ("xt_ps", "xt", "gv_ps", "sg", "h", "ht_ps", "ht", "y_ps", "y", "pad"))
        xs = sb("xs", [P, NB, XW])
        mine = sb("mine", [P, YB, TOPK])
        part = sb("part", [P, YB, TOPK])
        score = sb("score", [P, YB, 1])
        none = sb("none", [P, YB, 1])
        idx = [sb(f"idx{i}", [P, 1], U32) for i in range(YB)]
        w_ = sb("w", [P, NW, WX])
        xt = sb("xt", [P, 2, KD, P])
        sg = sb("sg", [P, 2, FE])
        h = sb("h", [P, 2, KF * P])
        ht = sb("ht", [P, 2, KF, P])
        y = [sb(f"y{i}", [P, D]) for i in range(YB)]
        p_x, p_gv, p_h, p_y = ([ps(f"p_{m}{i}", [P, 512]) for i in range(2)] for m in ("x", "gv", "h", "y"))
        block = ctx.enter_context(nc.Block())

        def slot(eng, n):
            return eng.value_load(rt.slot[0:1, ds(n, 1)], min_val=0, max_val=NW - 1)

        @block.gpsimd
        def _(pool):
            pool.sem_inc(xt_ps, NB)
            pool.memset(h[:, :, FE:KF * P], 0.0).then_inc(pad_ok, 1)

            def add(n, k):
                if not (isinstance(n, int) and n < 2):
                    pool.wait_ge(added[k % 2], 8 * (n - k % 2))
                    pool.sem_inc(y_free, 1)
                pool.wait_ge(y_ok, n + 3)
                pool.sem_inc(begun, 1)
                pool.indirect_dma_start(sum_dram[k % 2], bass.IndirectOffsetOnAxis(idx[k][:, 0:1], 0), y[k][:, :], None,
                                        compute_op=ALU.add).then_inc(added[k % 2], 16)

            pool.wait_ge(zero_sem, 16 * n_zero)
            pipeline(pool, XT, YB, (1, add))
            for done in added:
                pool.wait_ge(done, 8 * XT)

        @block.sync
        def _(sp):
            sp.sem_inc(y_ps, NW)

            def load(n, k):
                e = sp.value_load(rt.erow[0:1, ds(n, 1)], min_val=0, max_val=NE)
                new = sp.value_load(rt.new[0:1, ds(n, 1)], min_val=0, max_val=1)
                w = slot(sp, n)
                sp.wait_ge(y_ps, n + 1)
                sp.dma_start(w_[:, ds(w, 1), :].rearrange("p o f -> p (o f)"),
                             w_in[ds(e, 1)].rearrange("o p f -> p (o f)"), cond=new).then_inc(ld_w[k], 16)

            pipeline(sp, XT, NW, (0, load))

        @block.tensor
        def _(pe):
            def h_part(n, k):
                pe.wait_ge(h_ok, n + 1)
                for c in range(KF):
                    last = pe.transpose(p_h[k % 2][:, c * P:(c + 1) * P], h[:, k % 2, c * P:(c + 1) * P], st.c("ident"))
                last.then_inc(ht_ps, 1)

            def x_part(n, k):
                pe.wait_ge(ld_x[k % NB], 4 * (n - k % NB) + 16)
                for c in range(KD):
                    last = pe.transpose(p_x[k % 2][:, c * P:(c + 1) * P], xs[:, k % NB, c * P:(c + 1) * P],
                                        st.c("ident"))
                last.then_inc(xt_ps, 1)

            def gv_part(n, k):
                w = slot(pe, n)
                pe.wait_ge(ld_w[k], 2 * (n - k) + 16)
                pe.wait_ge(xt_ok, n + 1)
                for c in range(KD):
                    last = pe.matmul(p_gv[k % 2][:, 0:2 * FE], xt[:, k % 2, c, :],
                                     w_[:, ds(w, 1), c * 2 * FE:(c + 1) * 2 * FE].rearrange("p o f -> p (o f)"),
                                     start=c == 0, stop=c == KD - 1)
                last.then_inc(gv_ps, 1)

            def y_part(n, k):
                w = slot(pe, n)
                pe.wait_ge(ht_ok, n + 1)
                pe.wait_ge(y_ok, n + 1)
                for c in range(KF):
                    own = slice(KD * 2 * FE + c * D, KD * 2 * FE + (c + 1) * D)
                    last = pe.matmul(p_y[k % 2][:, 0:D], ht[:, k % 2, c, :],
                                     w_[:, ds(w, 1), own].rearrange("p o f -> p (o f)"),
                                     start=c == 0, stop=c == KF - 1)
                last.then_inc(y_ps, 1)

            pipeline(pe, XT, NW, (3, h_part), (0, x_part), (1, gv_part), (4, y_part))

        @block.scalar
        def _(act):
            def load(n, k):
                act.wait_ge(xt_ps, n + 1)
                act.wait_ge(idx_ok, n + 1)
                act.dma_start(xs[:, k, :], xs_dram[ds(n * P, P), :]).then_inc(ld_x[k], 16)

            def take_x(n, k):
                act.wait_ge(xt_ps, n + NB + 1)
                act.activation(xt[:, k % 2], p_x[k % 2][:, 0:D].rearrange("p (c t) -> p c t", c=KD),
                               ACT.Copy).then_inc(xt_ok, 1)

            def gate(n, k):
                act.wait_ge(gv_ps, n + 1)
                act.activation(sg[:, k % 2, :], p_gv[k % 2][:, 0:FE], ACT.Silu).then_inc(sg_ok, 1)

            def take_h(n, k):
                act.wait_ge(ht_ps, n + 3)
                act.wait_ge(y_ps, n + NW - 1)
                act.activation(ht[:, k % 2], p_h[k % 2][:, 0:KF * P].rearrange("p (c t) -> p c t", c=KF),
                               ACT.Copy).then_inc(ht_ok, 1)

            pipeline(act, XT, NB, (5, take_h), (2, take_x), (0, load), (3, gate))

        @block.vector
        def _(dve):
            dve.sem_inc(ht_ps, 2)
            dve.sem_inc(y_ok, 2)
            dve.sem_inc(y_free, YB)
            dve.sem_inc(idx_ok, NB)
            dve.wait_ge(pad_ok, 1)

            def gate(n, k):
                dve.wait_ge(sg_ok, n + 1)
                dve.wait_ge(ht_ps, n + 1)
                dve.tensor_tensor(h[:, k % 2, 0:FE], sg[:, k % 2, :], p_gv[k % 2][:, FE:2 * FE], ALU.mult).then_inc(h_ok, 1)

            def take_y(n, k):
                dve.wait_ge(y_ps, n + NW + 1)
                dve.wait_ge(y_free, n + 1)
                dve.tensor_scalar(y[k][:, :], p_y[k % 2][:, 0:D], score[:, k, :], None, ALU.mult).then_inc(y_ok, 1)

            def match(n, k):
                dve.wait_ge(ld_x[k % NB], 4 * (n - k % NB) + 16)
                dve.tensor_tensor(mine[:, k, :], xs[:, k % NB, D + 1:D + 1 + TOPK],
                                  st.c("slots")[:, ds(n, 1)].to_broadcast([P, TOPK]), ALU.is_equal).then_inc(mine_ok, 1)
                dve.tensor_scalar(none[:, k, :], xs[:, k % NB, D:D + 1], 0.0, st.c("beyond"),
                                  ALU.is_equal, ALU.mult).then_inc(none_ok, 1)

            def weigh(n, k):
                dve.wait_ge(mine_ok, n + 1)
                dve.tensor_tensor(part[:, k, :], mine[:, k, :], xs[:, k % NB, D + 1 + TOPK:XW], ALU.mult).then_inc(part_ok, 1)

            def find(n, k):
                dve.wait_ge(part_ok, n + 1)
                dve.wait_ge(none_ok, n + 1)
                dve.tensor_reduce(score[:, k, :], part[:, k, :], AX.X, ALU.add).then_inc(score_ok, 1)
                dve.wait_ge(y_free, n + 1)
                dve.scalar_tensor_tensor(idx[k][:, :], xs[:, k % NB, D:D + 1], -1.0, none[:, k, :],
                                         ALU.add, ALU.add).then_inc(idx_ok, 1)

            pipeline(dve, XT, YB, (0, match), (1, gate), (0, weigh), (4, take_y), (0, find))


def phase_combine(nc, st, sum_dram, yout):
    with ExitStack() as ctx:
        sb, ps, sem = opener(nc, ctx, "cb")
        y_ok, stat, agg = (sem(n) for n in ("y", "stat", "agg"))
        ld = [[sem(f"ld{i}_{b}") for b in range(B)] for i in range(2)]
        more = sb("more", [P, NT, D])
        stats = sb("stats", [P, NT, 6])
        block = ctx.enter_context(nc.Block())

        @block.sync
        def _(sp):
            for b in range(B):
                for i, dst in enumerate((yout, more)):
                    sp.dma_start(dst[:, b * TB:(b + 1) * TB, :],
                                 sum_dram[i][b * L:(b + 1) * L, :].rearrange("(t p) d -> p t d", p=P)
                                 ).then_inc(ld[i][b], 16)
            for i in range(2):
                for b in range(B):
                    sp.wait_ge(ld[i][b], 16)

        @block.vector
        def _(dve):
            for b in range(B):
                for i in range(2):
                    dve.wait_ge(ld[i][b], 16)
                own = slice(b * TB, (b + 1) * TB)
                dve.tensor_tensor(yout[:, own, :], yout[:, own, :], more[:, own, :], ALU.add).then_inc(y_ok, 1)
                dve.wait_ge(y_ok, b + 1)
                for n in range(b * TB, (b + 1) * TB):
                    dve.bn_stats(stats[:, n, :], yout[:, n, :]).then_inc(stat, 1)
            dve.wait_ge(stat, NT)
            for n in range(NT):
                dve.bn_aggr(st.mv[:, n, :], stats[:, n, :]).then_inc(agg, 1)


class AttentionData:

    def __init__(self, nc, ctx):
        def sb(name, shape):
            return ctx.enter_context(nc.sbuf_tensor(f"ad_{name}", shape, F32))

        self.qt = sb("qt", [P, HG, T])
        self.kt = sb("kt", [P, HG, T])
        self.v = sb("v", [P, NT, H, DH])


def phase_attention_project(nc, st, ad, w_in):
    with ExitStack() as ctx:
        sb, ps, sem = opener(nc, ctx, "ap")
        w_ld, eps, root, rstd = (sem(n) for n in ("w_ld", "eps", "root", "rstd"))
        xn_ok, xt_ps, xt_ok, qk_ps, rot_in, rot_ok, qkt_ps, v_out, qkt_out = (
            sem(n) for n in ("xn", "xt_ps", "xt", "qk_ps", "rot_in", "rot", "qkt_ps", "v_out", "qkt_out"))
        w = sb("w", [P, KD, 3 * D])
        xn = sb("xn", [P, 2, D])
        xt = sb("xt", [P, 2, KD, P])
        rc = sb("rc", [P, 2, 2 * D])
        rs = sb("rs", [P, 2, 2 * D])
        qk = sb("qk", [P, 2, 2 * D])
        p_x, p_qk, p_v, p_t = ([ps(f"p_{m}{i}", [P, 512]) for i in range(2)] for m in ("x", "qk", "v", "t"))
        block = ctx.enter_context(nc.Block())

        @block.sync
        def _(sp):
            sp.dma_start(w[:, :, :], w_in).then_inc(w_ld, 16)
            sp.wait_ge(w_ld, 16)

        @block.vector
        def _(dve):
            finish_stats(nc, st, None, dve, eps, root, rstd)

            def normalise(n, k):
                dve.wait_ge(xt_ps, n + 1)
                dve.tensor_scalar(xn[:, k % 2, :], st.x[:, ds(n, 1), :], st.mv[:, ds(n, 1), 0],
                                  st.rstd[:, ds(n, 1)], ALU.subtract, ALU.mult).then_inc(xn_ok, 1)

            def rotate(n, k):
                dve.wait_ge(qk_ps, n + 3)
                dve.wait_ge(rot_ok, 2 * n + 2)
                src = p_qk[k % 2][:, :].rearrange("p (h j s) -> p h j s", h=2 * H, s=2)
                for dst, name in ((rc, "cos"), (rs, "sin")):
                    table = st.c(name)[:, k * DH // 2:(k + 1) * DH // 2]
                    for s in range(2):
                        dve.tensor_tensor(dst[:, k % 2, :].rearrange("p (h j s) -> p h j s", h=2 * H, s=2)[..., s],
                                          src[..., s], table.unsqueeze(1).to_broadcast([P, 2 * H, DH // 2]),
                                          ALU.mult).then_inc(rot_in, 1)

            pipeline(dve, NT, TB, (0, normalise), (2, rotate))

        @block.gpsimd
        def _(pool):
            pool.sem_inc(rot_ok, 4)

            def combine(n, k):
                pool.wait_ge(rot_in, 4 * n + 12)
                pool.wait_ge(qkt_ps, n + 1)
                c, s, o = (a[:, k % 2, :].rearrange("p (m e) -> p m e", e=2) for a in (rc, rs, qk))
                pool.tensor_tensor(o[:, :, 0], c[:, :, 0], s[:, :, 1], ALU.subtract).then_inc(rot_ok, 1)
                pool.tensor_tensor(o[:, :, 1], s[:, :, 0], c[:, :, 1], ALU.add).then_inc(rot_ok, 1)

            pipeline(pool, NT, TB, (0, combine))

        @block.scalar
        def _(act):
            finish_stats(nc, st, act, None, eps, root, rstd)
            act.sem_inc(xt_ok, 2)
            act.sem_inc(v_out, 2)
            act.sem_inc(qkt_out, 4)

            def take_x(n, k):
                act.wait_ge(xt_ps, n + 3)
                act.wait_ge(qk_ps, n + 1)
                act.activation(xt[:, k % 2], p_x[k % 2][:, 0:D].rearrange("p (c t) -> p c t", c=KD),
                               ACT.Copy).then_inc(xt_ok, 1)

            def take_v(n, k):
                act.wait_ge(qk_ps, n + 3)
                act.activation(ad.v[:, ds(n, 1)].rearrange("p o h d -> p (o h d)"), p_v[k % 2][:, 0:D],
                               ACT.Copy).then_inc(v_out, 1)

            def take_qk(n, k):
                act.wait_ge(qkt_ps, n + 3)
                src = p_t[k % 2][:, :].rearrange("p (m t) -> p m t", m=4)
                cols = ds(n * P, P)
                act.activation(ad.qt[:, :, cols], src[:, 0:2], ACT.Copy).then_inc(qkt_out, 1)
                act.activation(ad.kt[:, :, cols], src[:, 2:4], ACT.Copy).then_inc(qkt_out, 1)

            pipeline(act, NT, TB, (0, take_x), (1, take_v), (3, take_qk))

        @block.tensor
        def _(pe):
            pe.sem_inc(xt_ps, 2)
            pe.sem_inc(qk_ps, 2)
            pe.sem_inc(qkt_ps, 2)
            pe.sem_inc(rot_in, 8)
            pe.wait_ge(w_ld, 16)

            def x_part(n, k):
                pe.wait_ge(xn_ok, n + 1)
                pe.wait_ge(xt_ok, n + 1)
                for c in range(KD):
                    last = pe.transpose(p_x[k % 2][:, c * P:(c + 1) * P], xn[:, k % 2, c * P:(c + 1) * P], st.c("ident"))
                last.then_inc(xt_ps, 1)

            def qkv_part(n, k):
                pe.wait_ge(xt_ok, n + 3)
                pe.wait_ge(rot_in, 4 * n + 4)
                pe.wait_ge(v_out, n + 1)
                for c in range(KD):
                    pe.matmul(p_qk[k % 2][:, :], xt[:, k % 2, c, :], w[:, c, 0:2 * D], start=c == 0, stop=c == KD - 1)
                for c in range(KD):
                    last = pe.matmul(p_v[k % 2][:, 0:D], xt[:, k % 2, c, :], w[:, c, 2 * D:3 * D],
                                     start=c == 0, stop=c == KD - 1)
                last.then_inc(qk_ps, 1)

            def qkt_part(n, k):
                pe.wait_ge(rot_ok, 2 * n + 6)
                pe.wait_ge(qkt_out, 2 * n + 2)
                for m in range(4):
                    last = pe.transpose(p_t[k % 2][:, m * P:(m + 1) * P], qk[:, k % 2, m * P:(m + 1) * P], st.c("ident"))
                last.then_inc(qkt_ps, 1)

            pipeline(pe, NT, TB, (0, x_part), (1, qkv_part), (3, qkt_part))


def phase_attention(nc, st, ad, wo_in, y):
    SQ = 2
    UN = SQ * TB * H
    QT = SQ * TB
    SB, PB = 3, 4
    LT, LC, LV = 2, 3, 4
    with ExitStack() as ctx:
        sb, ps, sem = opener(nc, ctx, "at")
        w_ld, pad_ok, in_ok = sem("w_ld"), sem("pad"), sem("in")
        s_ps, max_ok, exp_ok, pt_ps, o_ps = (sem(n) for n in ("s_ps", "max", "exp", "pt_ps", "o_ps"))
        pt_ok = [sem("pt_dve"), sem("pt_act")]
        rec_ok, o_out, turned, norm_ok, back, on_ok, y_ps, y_ok, stat, agg = (
            sem(n) for n in ("rec", "o_out", "turned", "norm", "back", "on", "y_ps", "y", "stat", "agg"))
        wo = sb("wo", [P, HG, D])
        kt = sb("kt", [P, SQ, HG, L])
        qz = sb("qz", [P, SQ, HG, HP, L])
        vp = sb("vp", [P, SQ, TB, H, 2 * DH])
        nm = sb("nm", [P, SB, 1])
        se = sb("se", [P, 2, H])
        rec = sb("rec", [P, H])
        pr = sb("pr", [P, PB, L])
        pt = sb("pt", [P, 2, L])
        o = sb("o", [P, HG, P])
        oq = sb("oq", [P, D])
        on = sb("on", [P, HG, P])
        stats = sb("stats", [P, NT, 6])
        p_s = [ps(f"p_s{i}", [P, L]) for i in range(SB)]
        p_t = [ps(f"p_t{i}", [P, L]) for i in range(2)]
        p_o = [ps(f"p_o{i}", [P, 4, P]) for i in range(2)]
        p_y = ps("p_y", [P, L])
        block = ctx.enter_context(nc.Block())

        def of(i):
            return i // (TB * H), i // H % TB, i % H

        def at(i, lag):
            j, r = divmod(i - LV - lag, H)
            return j - 1 if r == 0 and 1 <= j <= QT else None

        STEPS = UN + LV + 7

        @block.sync
        def _(sp):
            sp.dma_start(wo[:, :, :], wo_in).then_inc(w_ld, 16)
            sp.wait_ge(w_ld, 16)

        @block.gpsimd
        def _(pool):
            pool.memset(vp[:, :, :, :, :], 0.0).then_inc(pad_ok, 1)
            pool.wait_ge(pad_ok, 1)
            for s in range(B):
                u = s % SQ
                if s >= SQ:
                    pool.wait_ge(o_ps, TB * H * (s - SQ + 1) + 2)
                for t in range(TB):
                    n, own, cols = s * TB + t, slice(t * P, (t + 1) * P), slice((s * TB + t) * P, (s * TB + t + 1) * P)
                    pool.tensor_copy(kt[:, u, :, own], ad.kt[:, :, cols]).then_inc(in_ok, 1)
                    for g in range(HG):
                        pool.tensor_tensor(qz[:, u, g, :, own], ad.qt[:, g, cols].unsqueeze(1).to_broadcast([P, HP, P]),
                                           st.c("heads").unsqueeze(2).to_broadcast([P, HP, P]),
                                           ALU.mult).then_inc(in_ok, 1)
                    for k in range(2):
                        pool.tensor_copy(vp[:, u, t, k:H:2, k * DH:(k + 1) * DH], ad.v[:, n, k:H:2, :]).then_inc(in_ok, 1)

        @block.vector
        def _(dve):
            dve.sem_inc(pt_ok[0], 1)
            dve.sem_inc(rec_ok, 2)
            with dve.Fori(0, B // SQ) as b:
                for i in range(STEPS):
                    if LC <= i < UN + LC and (i - LC) % 2 == 0:
                        k = i - LC
                        n = UN * b + k
                        nk = of(k)[1] + 1
                        dve.wait_ge(pt_ps, n + PB + 1)
                        dve.wait_ge(o_ps, n + 1)
                        dve.tensor_copy(pt[:, 0, 0:nk * P], p_t[0][:, 0:nk * P]).then_inc(pt_ok[0], 1)
                    if i < UN:
                        n = UN * b + i
                        dve.wait_ge(s_ps, n + 1)
                        nk = of(i)[1] + 1
                        dve.tensor_reduce(nm[:, i % SB, :], p_s[i % SB][:, 0:nk * P], AX.X, ALU.max,
                                          negate=True).then_inc(max_ok, 1)
                    j = at(i, 1)
                    if j is not None:
                        n = QT * b + j
                        dve.wait_ge(exp_ok, UN * b + H * (j + 1) + SB)
                        dve.reciprocal(rec[:, :], se[:, j % 2, :]).then_inc(rec_ok, 1)
                        dve.wait_ge(rec_ok, n + 3)
                        dve.wait_ge(turned, n + 1)
                        dve.tensor_tensor(oq[:, :].rearrange("p (h d) -> p h d", d=DH),
                                          p_y[:, 0:D].rearrange("p (h d) -> p h d", d=DH),
                                          rec[:, :].unsqueeze(2).to_broadcast([P, H, DH]), ALU.mult).then_inc(norm_ok, 1)
                    j = at(i, 6)
                    if j is not None:
                        n = QT * b + j
                        dve.wait_ge(y_ok, n + 2)
                        dve.bn_stats(stats[:, ds(n, 1), :].rearrange("p o s -> p (o s)"),
                                     y[:, ds(n, 1), :].rearrange("p o d -> p (o d)")).then_inc(stat, 1)
            dve.wait_ge(stat, NT)
            for n in range(NT):
                dve.bn_aggr(st.mv[:, n, :], stats[:, n, :]).then_inc(agg, 1)

        @block.scalar
        def _(act):
            act.sem_inc(exp_ok, SB)
            act.sem_inc(pt_ok[1], 1)
            act.sem_inc(o_out, 2)
            act.sem_inc(y_ok, 1)
            with act.Fori(0, B // SQ) as b:
                for i in range(STEPS):
                    if LC <= i < UN + LC and (i - LC) % 2 == 1:
                        k = i - LC
                        n = UN * b + k
                        nk = of(k)[1] + 1
                        act.wait_ge(pt_ps, n + PB + 1)
                        act.wait_ge(o_ps, n + 1)
                        act.activation(pt[:, 1, 0:nk * P], p_t[1][:, 0:nk * P], ACT.Copy).then_inc(pt_ok[1], 1)
                    if i < UN:
                        n = UN * b + i
                        nk = of(i)[1] + 1
                        j = i // H
                        if i % H == 0:
                            act.wait_ge(rec_ok, QT * b + j + 1)
                        act.wait_ge(max_ok, n + 1)
                        act.wait_ge(pt_ps, n + 1)
                        act.activation(pr[:, i % PB, 0:nk * P], p_s[i % SB][:, 0:nk * P], ACT.Exp,
                                       bias=nm[:, i % SB, :], accum_out=se[:, j % 2, i % H:i % H + 1]).then_inc(exp_ok, 1)
                    j = at(i, 0)
                    if j is not None:
                        n = QT * b + j
                        act.wait_ge(o_ps, UN * b + H * (j + 1) + 2)
                        act.activation(o[:, :, :], p_o[j % 2][:, 0:HG, :], ACT.Copy).then_inc(o_out, 1)
                    j = at(i, 3)
                    if j is not None:
                        n = QT * b + j
                        act.wait_ge(back, n + 1)
                        act.activation(on[:, :, :], p_y[:, D:2 * D].rearrange("p (g t) -> p g t", g=HG),
                                       ACT.Copy).then_inc(on_ok, 1)
                    j = at(i, 5)
                    if j is not None:
                        n = QT * b + j
                        act.wait_ge(y_ps, n + 1)
                        act.activation(y[:, ds(n, 1), :].rearrange("p o d -> p (o d)"), p_y[:, 0:D],
                                       ACT.Copy).then_inc(y_ok, 1)

        @block.tensor
        def _(pe):
            pe.sem_inc(pt_ps, PB)
            pe.sem_inc(o_ps, 2)
            pe.wait_ge(w_ld, 16)

            def scores(b, i):
                n, (s, t, h) = UN * b + i, of(i)
                nk, hg = t + 1, h // HP
                if h == 0:
                    pe.wait_ge(in_ok, 5 * (QT * b + i // H) + 5)
                pe.matmul(p_s[i % SB][:, 0:nk * P], qz[:, s, hg, h % HP, t * P:(t + 1) * P], kt[:, s, hg, 0:nk * P],
                          start=True, stop=False)
                pe.matmul(p_s[i % SB][:, t * P:nk * P], st.cb[:, 0, :], st.cb[:, 1, :],
                          start=False, stop=True).then_inc(s_ps, 1)

            def transposes(b, i):
                n, nk = UN * b + i, of(i)[1] + 1
                pe.wait_ge(exp_ok, n + SB + 1)
                for c in range(nk):
                    last = pe.transpose(p_t[i % 2][:, c * P:(c + 1) * P], pr[:, i % PB, c * P:(c + 1) * P],
                                        st.c("ident"))
                last.then_inc(pt_ps, 1)

            def values(b, i):
                s, t, h = of(i)
                j, nk, hg, r = i // H, t + 1, h // HP, (h % HP) // 2 * 2 * DH
                if h == 0:
                    pe.wait_ge(o_out, QT * b + j + 1)
                pe.wait_ge(pt_ok[i % 2], UN // 2 * b + i // 2 + 2)
                for c in range(nk):
                    last = pe.matmul(p_o[j % 2][r:r + 2 * DH, hg, :], vp[:, s, c, h, :], pt[:, i % 2, c * P:(c + 1) * P],
                                     start=c == 0 and h % 2 == 0, stop=c == nk - 1 and h % 2 == 1)
                last.then_inc(o_ps, 1)

            with pe.Fori(0, B // SQ) as b:
                for i in range(STEPS):
                    if i < UN:
                        scores(b, i)
                    if LV <= i < UN + LV:
                        values(b, i - LV)
                    if LT <= i < UN + LT:
                        transposes(b, i - LT)
                    j = at(i, 1)
                    if j is not None:
                        pe.wait_ge(o_out, QT * b + j + 3)
                        pe.wait_ge(y_ok, QT * b + j + 1)
                        for g in range(HG):
                            last = pe.transpose(p_y[:, g * P:(g + 1) * P], o[:, g, :], st.c("ident"))
                        last.then_inc(turned, 1)
                    j = at(i, 3)
                    if j is not None:
                        pe.wait_ge(norm_ok, QT * b + j + 1)
                        for g in range(HG):
                            last = pe.transpose(p_y[:, D + g * P:D + (g + 1) * P], oq[:, g * P:(g + 1) * P],
                                                st.c("ident"))
                        last.then_inc(back, 1)
                    j = at(i, 5)
                    if j is not None:
                        pe.wait_ge(on_ok, QT * b + j + 1)
                        for g in range(HG):
                            last = pe.matmul(p_y[:, 0:D], on[:, g, :], wo[:, g, :], start=g == 0, stop=g == HG - 1)
                        last.then_inc(y_ps, 1)


def phase_ffn(nc, st, wgu_in, wd_in, y):
    FQ = FF // 4
    with ExitStack() as ctx:
        sb, ps, sem = opener(nc, ctx, "ff")
        w_ld, wd_ld, eps, root, rstd, stat, agg = (sem(n) for n in ("w_ld", "wd_ld", "eps", "root", "rstd", "stat", "agg"))
        xn_ok, xt_ps, xt_ok, g_ps, u_ps, sg_ok, h_ok, abs_ok, c_ok, ef_ok, s_ok, k_ok, ht_ps, ht_ok, y_ps, y_ok = (
            sem(n) for n in ("xn", "xt_ps", "xt", "g_ps", "u_ps", "sg", "h", "abs", "c", "ef", "s", "k",
                             "ht_ps", "ht", "y_ps", "y"))
        wgu = sb("wgu", [P, KD, 2, FF])
        wd = sb("wd", [P, FF // P, D])
        xn = sb("xn", [P, 2, D])
        xt = sb("xt", [P, 2, KD, P])
        sg = sb("sg", [P, 2, 512])
        h = sb("h", [P, 2, FF])
        a = sb("a", [P, 2, FF])
        cm = sb("cm", [P, 2, 3, 2, FQ], BF16)
        ef = sb("ef", [P, 2, 2, 2, FQ], BF16)
        sm = sb("sm", [P, 2, 4, FQ], BF16)
        hk = sb("hk", [P, 2, FF])
        ht = sb("ht", [P, 2, FF // P, P])
        stats = sb("stats", [P, NT, 6])
        p_t = ps("p_t", [P, 512])
        p_g = [ps(f"p_g{i}", [P, 512]) for i in range(2)]
        p_u = [ps(f"p_u{i}", [P, 512]) for i in range(2)]
        p_h = [ps(f"p_h{i}", [P, 512]) for i in range(2)]
        p_y = ps("p_y", [P, 512])
        block = ctx.enter_context(nc.Block())

        def quads(ap):
            return ap.rearrange("p (m s) -> p s m", s=4)

        @block.sync
        def _(sp):
            sp.dma_start(wgu[:, :, :, :], wgu_in).then_inc(w_ld, 16)
            sp.dma_start(wd[:, :, :], wd_in).then_inc(wd_ld, 16)
            sp.wait_ge(w_ld, 16)
            sp.wait_ge(wd_ld, 16)

        @block.vector
        def _(dve):
            dve.sem_inc(xt_ps, 2)
            dve.sem_inc(abs_ok, 2)
            dve.sem_inc(ef_ok, 4)
            dve.sem_inc(s_ok, 5)
            dve.sem_inc(ht_ps, 3)
            finish_stats(nc, st, None, dve, eps, root, rstd)

            def normalise(n, u):
                dve.wait_ge(xt_ps, n + 1)
                dve.tensor_scalar(xn[:, u, :], st.x[:, ds(n, 1), :], st.mv[:, ds(n, 1), 0], st.rstd[:, ds(n, 1)],
                                  ALU.subtract, ALU.mult).then_inc(xn_ok, 1)

            def gate(n, u):
                for j in range(2):
                    dve.wait_ge(sg_ok, 2 * n + j + 1)
                    dve.wait_ge(u_ps, 2 * n + j + 4)
                    dve.tensor_tensor(h[:, u, j * 512:(j + 1) * 512], sg[:, j, :], p_u[j][:, :],
                                      ALU.mult).then_inc(h_ok, 1)

            def compare(n, u):
                dve.wait_ge(abs_ok, 2 * n + 4)
                dve.wait_ge(s_ok, 4 * n + 1)
                v = quads(a[:, u, :])
                dve.tensor_tensor(cm[:, u, 0], v[:, 0:4:2], v[:, 1:4:2], ALU.is_ge).then_inc(c_ok, 1)
                dve.tensor_tensor(cm[:, u, 1], v[:, 0:2], v[:, 2:4], ALU.is_ge).then_inc(c_ok, 1)
                for s in range(2):
                    dve.tensor_tensor(cm[:, u, 2, s], v[:, s], v[:, 3 - s], ALU.is_ge).then_inc(c_ok, 1)

            def select(n, u):
                hv, kv = quads(h[:, u, :]), quads(hk[:, u, :])
                dve.wait_ge(ht_ps, 2 * n + 1)
                for s, (least, op) in enumerate(((2.0, ALU.is_ge), (1.0, ALU.is_ge), (0.0, ALU.is_ge),
                                                 (1.0, ALU.is_le))):
                    dve.wait_ge(s_ok, 4 * n + s + 6)
                    dve.scalar_tensor_tensor(kv[:, s], sm[:, u, s], least, hv[:, s], op, ALU.mult).then_inc(k_ok, 1)

            def take_stats(n, u):
                dve.wait_ge(y_ok, n + 2)
                dve.bn_stats(stats[:, ds(n, 1), :].rearrange("p o s -> p (o s)"),
                             y[:, ds(n, 1), :].rearrange("p o d -> p (o d)")).then_inc(stat, 1)

            pipeline(dve, NT, 2, (0, normalise), (3, compare), (2, gate), (3, select), (5, take_stats))
            dve.wait_ge(stat, NT)
            for n in range(NT):
                dve.bn_aggr(st.mv[:, n, :], stats[:, n, :]).then_inc(agg, 1)

        @block.gpsimd
        def _(pool):
            pool.sem_inc(k_ok, 5)

            def sums(n, u):
                c, e = cm[:, u], ef[:, u]
                pool.wait_ge(c_ok, 4 * n + 9)
                pool.tensor_tensor(e[:, 0], c[:, 1], c[:, 2], ALU.add).then_inc(ef_ok, 1)
                for s in range(2):
                    pool.tensor_tensor(e[:, 1, s], c[:, 1, s], c[:, 2, 1 - s], ALU.add).then_inc(ef_ok, 1)
                pool.wait_ge(ef_ok, 3 * n + 7)
                pool.wait_ge(k_ok, 4 * n + 1)
                pool.tensor_tensor(sm[:, u, 0], c[:, 0, 0], e[:, 0, 0], ALU.add).then_inc(s_ok, 1)
                pool.tensor_tensor(sm[:, u, 1], e[:, 0, 1], c[:, 0, 0], ALU.subtract).then_inc(s_ok, 1)
                pool.tensor_tensor(sm[:, u, 2], c[:, 0, 1], e[:, 1, 0], ALU.subtract).then_inc(s_ok, 1)
                pool.tensor_tensor(sm[:, u, 3], c[:, 0, 1], e[:, 1, 1], ALU.add).then_inc(s_ok, 1)

            pipeline(pool, NT, 2, (3, sums))

        @block.scalar
        def _(act):
            act.sem_inc(y_ok, 1)
            finish_stats(nc, st, act, None, eps, root, rstd)
            act.sem_inc(xt_ok, 1)
            act.sem_inc(h_ok, 2)
            act.sem_inc(c_ok, 5)
            act.sem_inc(u_ps, 3)
            act.sem_inc(ht_ok, 2)
            act.sem_inc(y_ps, 2)

            def take_x(n, u):
                act.wait_ge(xt_ps, n + 3)
                act.wait_ge(u_ps, 2 * n + 1)
                act.activation(xt[:, u], p_t[:, 0:D].rearrange("p (c t) -> p c t", c=KD), ACT.Copy).then_inc(xt_ok, 1)

            def take_h(n, u):
                for j in range(2):
                    act.wait_ge(ht_ps, 2 * n + j + 4)
                    act.wait_ge(y_ps, n + 1)
                    act.activation(ht[:, u, 4 * j:4 * j + 4, :], p_h[j][:, :].rearrange("p (c t) -> p c t", t=P),
                                   ACT.Copy).then_inc(ht_ok, 1)

            def gate(n, u):
                for j in range(2):
                    act.wait_ge(g_ps, 2 * n + j + 1)
                    act.wait_ge(h_ok, 2 * n + j + 1)
                    act.activation(sg[:, j, :], p_g[j][:, :], ACT.Silu).then_inc(sg_ok, 1)

            def magnitudes(n, u):
                for j in range(2):
                    act.wait_ge(h_ok, 2 * n + j + 3)
                    act.wait_ge(c_ok, 4 * n + 1)
                    act.activation(a[:, u, j * 512:(j + 1) * 512], h[:, u, j * 512:(j + 1) * 512],
                                   ACT.Abs).then_inc(abs_ok, 1)

            def take_y(n, u):
                act.wait_ge(y_ps, n + 3)
                act.activation(y[:, ds(n, 1), :].rearrange("p o d -> p (o d)"), p_y[:, 0:D], ACT.Copy).then_inc(y_ok, 1)

            pipeline(act, NT, 2, (1, take_x), (4, take_h), (2, gate), (2, magnitudes), (4, take_y))

        @block.tensor
        def _(pe):
            pe.wait_ge(w_ld, 16)
            pe.wait_ge(wd_ld, 16)

            def x_part(n, u):
                pe.wait_ge(xn_ok, n + 1)
                pe.wait_ge(xt_ok, n + 1)
                for c in range(KD):
                    last = pe.transpose(p_t[:, c * P:(c + 1) * P], xn[:, u, c * P:(c + 1) * P], st.c("ident"))
                last.then_inc(xt_ps, 1)

            def gu_part(n, u):
                pe.wait_ge(xt_ok, n + 2)
                for j in range(2):
                    pe.wait_ge(h_ok, 2 * n + j + 1)
                    for m, (bank, done) in enumerate(((p_g[j], g_ps), (p_u[j], u_ps))):
                        for c in range(KD):
                            last = pe.matmul(bank[:, :], xt[:, u, c, :], wgu[:, c, m, j * 512:(j + 1) * 512],
                                             start=c == 0, stop=c == KD - 1)
                        last.then_inc(done, 1)

            def h_part(n, u):
                pe.wait_ge(k_ok, 4 * n + 9)
                for j in range(2):
                    pe.wait_ge(ht_ok, 2 * n + j + 1)
                    for c in range(4):
                        last = pe.transpose(p_h[j][:, c * P:(c + 1) * P],
                                            hk[:, u, (4 * j + c) * P:(4 * j + c + 1) * P], st.c("ident"))
                    last.then_inc(ht_ps, 1)

            def y_part(n, u):
                pe.wait_ge(ht_ok, 2 * n + 4)
                pe.wait_ge(y_ok, n + 1)
                for c in range(FF // P):
                    last = pe.matmul(p_y[:, 0:D], ht[:, u, c, :], wd[:, c, :], start=c == 0, stop=c == FF // P - 1)
                last.then_inc(y_ps, 1)

            pipeline(pe, NT, 2, (1, x_part), (4, h_part), (2, gu_part), (4, y_part))


def phase_last(nc, st, y, out):
    with ExitStack() as ctx:
        sb, ps, sem = opener(nc, ctx, "la")
        eps, root, rstd, shifted, yn, x_pool, x_dve, o_d = (
            sem(n) for n in ("eps", "root", "rstd", "shifted", "yn", "x_pool", "x_dve", "out"))
        shift = sb("shift", [P, NT])
        block = ctx.enter_context(nc.Block())

        @block.scalar
        def _(act):
            finish_stats(nc, st, act, None, eps, root, rstd)
            normalise(st, act, y, shift, shifted, yn)

        @block.gpsimd
        def _(pool):
            for t in range(0, NT, 2):
                pool.wait_ge(yn, t + 1)
                pool.tensor_tensor(st.x[:, t, :], st.x[:, t, :], y[:, t, :], ALU.add).then_inc(x_pool, 1)

        @block.vector
        def _(dve):
            finish_stats(nc, st, None, dve, eps, root, rstd)
            find_shift(st, dve, shift, shifted)
            for t in range(1, NT, 2):
                dve.wait_ge(yn, t + 1)
                dve.tensor_tensor(st.x[:, t, :], st.x[:, t, :], y[:, t, :], ALU.add).then_inc(x_dve, 1)

        @block.sync
        def _(sp):
            for b in range(B):
                sp.wait_ge(x_pool, TB // 2 * (b + 1))
                sp.wait_ge(x_dve, TB // 2 * (b + 1))
                sp.dma_start(out[b].rearrange("(t p) d -> p t d", p=P),
                             st.x[:, b * TB:(b + 1) * TB, :]).then_inc(o_d, 16)
            sp.wait_ge(o_d, 16 * B)


def build(nc, x, cst, w_dp, wo_d, onw, w_r, w_x, w_at, wo_a, w_gu, w_down, out):
    kvb_dram = nc.dram_tensor("kvb_dram", (T, H, KVW), F32, kind="Internal").ap()
    xs_dram = nc.dram_tensor("xs_dram", (XT * P, XW), F32, kind="Internal").ap()
    sum_dram = [nc.dram_tensor(f"sum{i}_dram", (T + P, D), F32, kind="Internal").ap() for i in range(2)]
    with ExitStack() as ctx:
        def sb(c, name, shape, dt=F32):
            return c.enter_context(nc.sbuf_tensor(name, shape, dt))

        st = State(nc, ctx)
        phase_load(nc, st, x, cst)
        with ExitStack() as until_dispatch:
            zeros = sb(until_dispatch, "zeros", [P, ZW])
            zero_sem = until_dispatch.enter_context(nc.semaphore("slots_zeroed"))
            n_zero = XT * XW // ZW + -(-(T // P + 1) * D // ZW) + 1
            att = sb(until_dispatch, "att", [P, C, NC_ * G])
            with ExitStack() as delta:
                mkv = sb(delta, "mkv", [P, NC_, G, C + KVW])
                kqt = sb(delta, "kqt", [P, NC_, G, 2, C])
                with ExitStack() as raw:
                    qr = sb(raw, "q_raw", [P, NT, D])
                    kvb = sb(raw, "kvb", [P, NT, H, KVW])
                    norms = sb(raw, "norms", [P, NT, 2 * H])
                    wall = sb(raw, "w_qkvb", [P, KD, 3 * D + H])
                    phase_delta_project(nc, st, w_dp, qr, kvb, norms, wall, zeros)
                    phase_delta_layout(nc, st, qr, kvb, norms, kqt, kvb_dram)
                phase_delta_scores(nc, st, kqt, kvb_dram, mkv, att)
                phase_delta_invert(nc, st, mkv, att, zeros, xs_dram, sum_dram, zero_sem)
                xt = sb(delta, "xt", [P, NC_, G, 2, C])
                phase_delta_wy(nc, st, kqt, mkv, att, xt)
                ot = att[:, :, :].rearrange("p a b -> p (a b)").rearrange("p (g b l) -> p g b l", g=HG, b=B)
                phase_delta_chain(nc, st, mkv, xt, ot)
            y = sb(until_dispatch, "y_first", [P, NT, D])
            phase_delta_out(nc, st, ot, wo_d, onw, y)
            phase_update(nc, st, y, "up1")
            rt = Routing(nc, until_dispatch)
            with ExitStack() as dispatch:
                xna = sb(dispatch, "xna", [P, NT, D + 1])
                xt = sb(dispatch, "xt_all", [P, KD, T])
                phase_route(nc, st, rt, w_r, xna, xt)
                phase_dispatch(nc, st, rt, xna, xt, w_x, y, xs_dram, sum_dram, zero_sem, n_zero)
            phase_experts(nc, st, rt, xs_dram, sum_dram, zero_sem, n_zero, w_x)
            phase_combine(nc, st, sum_dram, y)
            phase_update(nc, st, y, "up2")
        y = sb(ctx, "y", [P, NT, D])
        with ExitStack() as attention:
            ad = AttentionData(nc, attention)
            phase_attention_project(nc, st, ad, w_at)
            phase_attention(nc, st, ad, wo_a, y)
        phase_update(nc, st, y, "up3")
        phase_ffn(nc, st, w_gu, w_down, y)
        phase_last(nc, st, y, out)


def rows(w, k):
    return np.ascontiguousarray(np.moveaxis(w.reshape(w.shape[:-2] + (k, w.shape[-2] // k, w.shape[-1])), -3, -2))


def flat(w):
    return w.reshape(w.shape[:2] + (-1,))


def kernel(**inputs):
    import concourse.bacc as _bacc
    from concourse.bass_utils import run_bass_kernel_spmd as _run

    a = {k: np.asarray(v) for k, v in inputs.items()}
    l0, lf, l1, lg = "L0_attn_", "L0_ffn_", "L1_attn_", "L1_ffn_"

    def with_shared(name):
        return np.concatenate([a[lf + name], a[lf + "s" + name][None]])

    arrays = {
        "x": a[l0 + "hidden_states"],
        "cst": constants(),
        "w_dp": rows(np.concatenate([a[l0 + n] for n in ("Wq", "Wk", "Wv", "Wb")], 1), KD),
        "wo_d": rows(a[l0 + "Wo"], HG),
        "onw": np.ascontiguousarray(np.tile(a[l0 + "o_norm_weight"], HP)[:, None]),
        "w_r": rows(a[lf + "w_router"].T, KD),
        "w_x": np.concatenate([flat(rows(np.concatenate([with_shared("wg"), with_shared("wv")], 2), KD)),
                               flat(rows(np.pad(with_shared("wo"), ((0, 0), (0, KF * P - FE), (0, 0))), KF))], 2),
        "w_at": rows(np.concatenate([a[l1 + n].T for n in ("Wq", "Wk", "Wv")], 1), KD),
        "wo_a": rows(a[l1 + "Wo"].T, HG),
        "w_gu": np.ascontiguousarray(np.stack([rows(a[lg + "w_gate"], KD), rows(a[lg + "w_up"], KD)], 2)),
        "w_down": rows(a[lg + "w_down"], FF // P),
    }
    nc = _bacc.Bacc("TRN2", target_bir_lowering=False, num_devices=1)
    args = [nc.dram_tensor(f"in_{k}", v.shape, mybir.dt.from_np(v.dtype), kind="ExternalInput").ap()
            for k, v in arrays.items()]
    out = nc.dram_tensor("out", (B, L, D), F32, kind="ExternalOutput").ap()
    build(nc, *args, out)
    r = _run(nc, [{f"in_{k}": v for k, v in arrays.items()}], core_ids=[0])
    return r.results[0]["out"]
```
